# Optimizing a Trainium2 kernel written in Bass

```python
import numpy as np
import jax
import jax.numpy as jnp

def _softmax(x, axis=-1):
    return jax.nn.softmax(x, axis=axis)

def _gelu(x):
    return jax.nn.gelu(x, approximate=True)

def _silu(x):
    return jax.nn.silu(x)

def _sigmoid(x):
    return jax.nn.sigmoid(x)

def _layernorm(x, axis=-1, eps=1e-05):
    m = jnp.mean(x, axis=axis, keepdims=True)
    v = jnp.var(x, axis=axis, keepdims=True)
    return (x - m) / jnp.sqrt(v + eps)

def _scatter_add(tgt, idx, src, axis=0):
    return tgt.at[idx].add(src)

def _segment_sum(src, seg, n):
    return jax.ops.segment_sum(src, seg, n)
kernel_name = 'mk_decoder_preln_d1_seqx_r8_de60f3'

def setup_inputs(seed: int=0):
    np.random.seed(seed)
    _w = jnp.asarray

    def _rec_inputs():
        import jax
        import jax.numpy as jnp
        _rk = jax.random.key(seed)
        x = 7.22e-05 + 1 * jax.random.normal(jax.random.fold_in(_rk, 1), (8, 128, 256), jnp.float32)
        _lenS = 128 - jax.random.randint(jax.random.fold_in(_rk, 7), (8,), 0, max(1, 128 // 4) + 1, jnp.int32)
        _lenS2 = 128 - jax.random.randint(jax.random.fold_in(_rk, 8), (8,), 0, max(1, 128 // 4) + 1, jnp.int32)
        _ctx_512P = jax.random.normal(jax.random.fold_in(_rk, 11), (8, 16, 64), jnp.float32)
        _ctx_512c = jax.random.dirichlet(jax.random.fold_in(_rk, 511), 0.3 * jnp.ones((16,), jnp.float32), (8, 128))
        _ctx_512t = jnp.einsum('bsk,bkd->bsd', _ctx_512c, _ctx_512P)
        _ctx_512t = _ctx_512t * jax.lax.rsqrt(jnp.mean(jnp.square(_ctx_512t)) + 1e-12) * 0.953939
        ctx_512 = -0.000514642 + 1.00011 * (_ctx_512t + 0.3 * jax.random.normal(jax.random.fold_in(_rk, 611), (8, 128, 64), jnp.float32))
        return (x, ctx_512)
    x, ctx_512 = _rec_inputs()

    def _L0_attn_setup():
        import jax, jax.numpy as jnp
        import numpy as np
        B, S, D = (2, 512, 256)
        H, DK, DV = (16, 128, 128)
        SEG = 64
        UPDATE = 'delta'
        CAUSAL = True
        key = jax.random.key(seed)
        ks = jax.random.split(key, 6)
        s = 0.02
        return {'x': jax.random.normal(ks[0], (B, S, D), jnp.float32), 'Wq': jax.random.normal(ks[1], (D, H * DK), jnp.float32) * s, 'Wk': jax.random.normal(ks[2], (D, H * DK), jnp.float32) * s, 'Wv': jax.random.normal(ks[3], (D, H * DV), jnp.float32) * s, 'Wo': jax.random.normal(ks[4], (H * DV, D), jnp.float32) * s, 'betas': jax.random.normal(ks[5], (1, H, 1, DV), jnp.float32)}
    _L0_attn_all = _L0_attn_setup()
    _L0_attn_in = {k: v for k, v in _L0_attn_all.items() if k in ('Wq', 'Wk', 'Wv', 'Wo', 'betas')}
    del _L0_attn_all

    def _L0_xattn_setup():
        import jax, jax.numpy as jnp
        import numpy as np
        B, S, H, NH, L = (2, 256, 256, 16, 64)
        HD = H // NH
        key = jax.random.key(seed)
        k1, k2, k3, k4, k5 = jax.random.split(key, 5)
        scale = 0.02
        return {'q': jax.random.normal(k1, (B, S, H), dtype=jnp.float32), 'latent_kv': jax.random.normal(k2, (B, S, L), dtype=jnp.float32), 'Wq': jax.random.normal(k3, (H, H), dtype=jnp.float32) * scale, 'Wkv_expand': jax.random.normal(k4, (2 * H, L), dtype=jnp.float32) * scale, 'Wout': jax.random.normal(k5, (H, H), dtype=jnp.float32) * scale}
    _L0_xattn_all = _L0_xattn_setup()
    _L0_xattn_in = {k: v for k, v in _L0_xattn_all.items() if k in ('Wq', 'Wkv_expand', 'Wout')}
    del _L0_xattn_all

    def _L0_ffn_setup():
        import jax, jax.numpy as jnp
        import numpy as np
        NUM_EXPERTS = 8
        TOP_K = 2
        EMB = 256
        MLP = 512
        B, S = (4, 128)
        key = jax.random.key(seed)
        ks = jax.random.split(key, 5)
        scale_x = 1.0
        return {'x': jax.random.normal(ks[0], (B, S, EMB), dtype=jnp.float32), 'gate_kernel': jax.random.normal(ks[1], (EMB, NUM_EXPERTS), dtype=jnp.float32) / np.sqrt(EMB), 'w0_kernel': jax.random.normal(ks[2], (NUM_EXPERTS, EMB, MLP), dtype=jnp.float32) / np.sqrt(EMB), 'w1_kernel': jax.random.normal(ks[3], (NUM_EXPERTS, EMB, MLP), dtype=jnp.float32) / np.sqrt(EMB), 'wo_kernel': jax.random.normal(ks[4], (NUM_EXPERTS, MLP, EMB), dtype=jnp.float32) / np.sqrt(MLP)}
    _L0_ffn_all = _L0_ffn_setup()
    _L0_ffn_in = {k: v for k, v in _L0_ffn_all.items() if k in ('gate_kernel', 'w0_kernel', 'w1_kernel', 'wo_kernel')}
    del _L0_ffn_all
    return {'x': x, 'ctx_512': ctx_512, 'L0_attn_Wq': _L0_attn_in['Wq'], 'L0_attn_Wk': _L0_attn_in['Wk'], 'L0_attn_Wv': _L0_attn_in['Wv'], 'L0_attn_Wo': _L0_attn_in['Wo'], 'L0_attn_betas': _L0_attn_in['betas'], 'L0_xattn_Wq': _L0_xattn_in['Wq'], 'L0_xattn_Wkv_expand': _L0_xattn_in['Wkv_expand'], 'L0_xattn_Wout': _L0_xattn_in['Wout'], 'L0_ffn_gate_kernel': _L0_ffn_in['gate_kernel'], 'L0_ffn_w0_kernel': _L0_ffn_in['w0_kernel'], 'L0_ffn_w1_kernel': _L0_ffn_in['w1_kernel'], 'L0_ffn_wo_kernel': _L0_ffn_in['wo_kernel']}

def reference(x, ctx_512, L0_attn_Wq, L0_attn_Wk, L0_attn_Wv, L0_attn_Wo, L0_attn_betas, L0_xattn_Wq, L0_xattn_Wkv_expand, L0_xattn_Wout, L0_ffn_gate_kernel, L0_ffn_w0_kernel, L0_ffn_w1_kernel, L0_ffn_wo_kernel):
    import jax
    import jax.numpy as jnp

    def _L0_attn_ref(x, Wq, Wk, Wv, Wo, betas):
        import jax, jax.numpy as jnp
        import numpy as np
        B, S, D = (2, 512, 256)
        H, DK, DV = (16, 128, 128)
        SEG = 64
        UPDATE = 'delta'
        CAUSAL = True
        Bsz, seq, _ = x.shape
        nseg = seq // SEG
        q = (x @ Wq).reshape(Bsz, seq, H, DK).transpose(0, 2, 1, 3)
        k = (x @ Wk).reshape(Bsz, seq, H, DK).transpose(0, 2, 1, 3)
        v = (x @ Wv).reshape(Bsz, seq, H, DV).transpose(0, 2, 1, 3)
        qs = q.reshape(Bsz, H, nseg, SEG, DK).transpose(2, 0, 1, 3, 4)
        ks_ = k.reshape(Bsz, H, nseg, SEG, DK).transpose(2, 0, 1, 3, 4)
        vs = v.reshape(Bsz, H, nseg, SEG, DV).transpose(2, 0, 1, 3, 4)
        causal_mask = jnp.tril(jnp.ones((SEG, SEG), bool))
        scale = DK ** 0.5
        beta = jax.nn.sigmoid(betas)

        def step(carry, seg):
            mem, z = carry
            qq, kk, vv = seg
            sigma_q = jax.nn.elu(qq) + 1.0
            scores = jnp.einsum('bhsk,bhtk->bhst', qq, kk) / scale
            if CAUSAL:
                scores = jnp.where(causal_mask, scores, -jnp.inf)
            att_dot = jax.nn.softmax(scores, axis=-1) @ vv
            att_mem = sigma_q @ mem / (sigma_q @ z)
            sigma_k = jax.nn.elu(kk) + 1.0
            if UPDATE == 'linear':
                mem_new = mem + jnp.einsum('bhsk,bhsv->bhkv', sigma_k, vv)
            else:
                delta = vv - sigma_k @ mem / (sigma_k @ z)
                mem_new = mem + jnp.einsum('bhsk,bhsv->bhkv', sigma_k, delta)
            z_new = z + sigma_k.sum(axis=-2, keepdims=True).transpose(0, 1, 3, 2)
            att = beta * att_mem + (1.0 - beta) * att_dot
            out = att.reshape(Bsz, SEG, H * DV) @ Wo
            return ((mem_new, z_new), out)
        mem0 = jnp.zeros((Bsz, H, DK, DV), x.dtype)
        z0 = jnp.ones((Bsz, H, DK, 1), x.dtype) / DK
        _, outs = jax.lax.scan(step, (mem0, z0), (qs, ks_, vs))
        return outs.transpose(1, 0, 2, 3).reshape(Bsz, seq, D)

    def _L0_xattn_ref(q, latent_kv, Wq, Wkv_expand, Wout):
        import jax, jax.numpy as jnp
        import numpy as np
        B, S, H, NH, L = (2, 256, 256, 16, 64)
        HD = H // NH
        b, sq, _ = q.shape
        sk = latent_kv.shape[1]
        qp = q @ Wq.T
        kv = latent_kv @ Wkv_expand.T
        k, v = jnp.split(kv, 2, axis=-1)
        qh = qp.reshape(b, sq, NH, HD).transpose(0, 2, 1, 3)
        kh = k.reshape(b, sk, NH, HD).transpose(0, 2, 1, 3)
        vh = v.reshape(b, sk, NH, HD).transpose(0, 2, 1, 3)
        inv_sqrt_d = 1.0 / jnp.sqrt(jnp.float32(HD))
        scores = jnp.einsum('bhqd,bhkd->bhqk', qh, kh) * inv_sqrt_d
        causal = jnp.tril(jnp.ones((sq, sk), dtype=bool))
        scores = jnp.where(causal, scores, jnp.finfo(scores.dtype).min)
        attn = jax.nn.softmax(scores, axis=-1)
        out = jnp.einsum('bhqk,bhkd->bhqd', attn, vh)
        out = out.transpose(0, 2, 1, 3).reshape(b, sq, H)
        return out @ Wout.T

    def _L0_ffn_ref(x, gate_kernel, w0_kernel, w1_kernel, wo_kernel):
        import jax, jax.numpy as jnp
        import numpy as np
        NUM_EXPERTS = 8
        TOP_K = 2
        EMB = 256
        MLP = 512
        B, S = (4, 128)
        gate_logits = jnp.einsum('bsd,de->bse', x, gate_kernel)
        top_k_weights, top_k_indices = jax.lax.top_k(gate_logits, TOP_K)
        top_k_weights = jax.nn.softmax(top_k_weights.astype(jnp.float32), axis=-1).astype(x.dtype)
        one_hot = jax.nn.one_hot(top_k_indices, NUM_EXPERTS, dtype=x.dtype)
        combine = jnp.einsum('bsk,bske->bse', top_k_weights, one_hot)
        h0 = jnp.einsum('bsd,edm->bsem', x, w0_kernel)
        h1 = jnp.einsum('bsd,edm->bsem', x, w1_kernel)
        inter = jax.nn.silu(h0) * h1
        out = jnp.einsum('bse,bsem,emd->bsd', combine, inter, wo_kernel)
        return out
    x = x + _L0_attn_ref(_layernorm(x, axis=-1), L0_attn_Wq, L0_attn_Wk, L0_attn_Wv, L0_attn_Wo, L0_attn_betas)
    x = x + _L0_xattn_ref(_layernorm(x, axis=-1), ctx_512, L0_xattn_Wq, L0_xattn_Wkv_expand, L0_xattn_Wout)
    x = x + _L0_ffn_ref(_layernorm(x, axis=-1), L0_ffn_gate_kernel, L0_ffn_w0_kernel, L0_ffn_w1_kernel, L0_ffn_wo_kernel)
    return x

_drawn_inputs = setup_inputs


def setup_inputs(seed=0):
    import zlib

    import numpy as np

    out = dict(_drawn_inputs(seed))
    spreads = {}
    factors = {'L0_attn_Wq': 3.777, 'L0_attn_Wk': 3.226, 'L0_xattn_Wq': 23.211}
    for name, (base, spread) in spreads.items():
        noise = np.random.default_rng([zlib.crc32(name.encode()), seed]).standard_normal(out[name].shape)
        drawn = base * np.exp(spread * noise) if base else spread * noise
        out[name] = jnp.asarray(drawn.astype(out[name].dtype))
    for name, factor in factors.items():
        out[name] = (out[name] * factor).astype(out[name].dtype)
    return out
```

```python
from contextlib import ExitStack

import concourse.bass as bass
from concourse import mybir

F32 = mybir.dt.float32
F32R = mybir.dt.float32r
BF16 = mybir.dt.bfloat16
I32 = mybir.dt.int32
U32 = mybir.dt.uint32
ALU = mybir.AluOpType
ACT = mybir.ActivationFunctionType
AX = mybir.AxisListType

P = 128
BANK = 512
B, S, D = 8, 128, 256
KD = D // P
H, DK, SEG = 16, 128, 64
HB = 4
HALVES = B // HB
TOK = HB * S
GH = 4
NG = H // GH
NH, NGRP = HALVES * H, HALVES * NG
LN_EPS = 1e-5
MASKED = -3.0e38
ATT_SCALE = 1.0 / float(DK) ** 0.5


class Core:

    def __init__(self, nc, ctx):
        self.nc, self.ctx = nc, ctx
        self.psum = ctx.enter_context(nc.psum_tensor("psum", [P, 8 * BANK], F32))
        self.bank = [self.psum[:, i * BANK:(i + 1) * BANK] for i in range(8)]
        self.x_sb = self.sb("x_sb", [P, B, D], F32)
        self.ident = self.sb("ident", [P, P], F32)
        self.ident_b = self.sb("ident_b", [P, P], BF16)
        self.eps = self.sb("eps", [P, 1], F32)

    def sb(self, name, shape, dt, ctx=None):
        return (ctx or self.ctx).enter_context(self.nc.sbuf_tensor(name, shape, dt))

    def sem(self, name):
        return self.ctx.enter_context(self.nc.semaphore(name))


def wait_past(eng, sem, value):
    if not isinstance(value, int) or value > 0:
        eng.wait_ge(sem, value)


class Head:

    def __init__(self, half, first, loop=None):
        turns = loop if loop is not None else 0
        self.half, self.j, self.looped = half, first % GH, loop is not None
        self.h = turns * GH + first
        self.n = turns * GH + (first + half * H)
        self.pair = turns * (GH // 2) + (first + half * H) // 2
        self.group = turns + (first + half * H) // GH

    def at(self, half, h):
        return not self.looped and self.half == half and self.h == h


def head_steps(eng, step):
    for half in range(HALVES):
        step(Head(half, 0))
        with eng.Fori(0, NG - 1) as turn:
            for first in range(1, 1 + GH):
                step(Head(half, first, turn))
        for h in range(H - 3, H):
            step(Head(half, h))


def attention_phase(c, x, betas, wqk, wv, wo, beta_dram):
    nc = c.nc
    phase = ExitStack()

    def sb(name, shape, dt):
        return c.sb(name, shape, dt, phase)

    xn = sb("a_xn", [P, B, D], F32)
    stats = sb("a_stats", [P, B, 6], F32)
    meanvar = sb("a_meanvar", [P, B, 2], F32)
    std = sb("a_std", [P, B], F32)
    rstd = sb("a_rstd", [P, B], F32)
    xt_hi = sb("a_xt_hi", [P, KD, B * S], F32R)
    xt_lo = sb("a_xt_lo", [P, KD, B * S], F32R)
    qk_raw = sb("a_qk_raw", [P, 2, 2 * KD * DK], F32)
    qk_hi = sb("a_qk_hi", [P, 2, 2 * KD * DK], F32R)
    qk_lo = sb("a_qk_lo", [P, 2, 2 * KD * DK], F32R)
    wo_sb = sb("a_wo", [P, H, D], F32)
    wv_raw = sb("a_wv_raw", [P, KD, GH * DK], F32)
    wv_hi = sb("a_wv_hi", [P, KD, GH * DK], F32R)
    wv_lo = sb("a_wv_lo", [P, KD, GH * DK], F32R)
    gate_in = sb("a_gate_in", [H, DK], F32)
    gate_exp = sb("a_gate_exp", [H, 2, DK], F32)
    gate = sb("a_gate", [H, 2, DK], F32)
    gate_x = sb("a_gate_x", [P, H * DK], F32)
    gate_y = sb("a_gate_y", [P, H * DK], F32)
    v_x = sb("a_v_x", [P, HB, GH * DK], F32)
    v_y = sb("a_v_y", [P, HB, GH * DK], F32)
    qk = sb("a_qk", [P, 2 * TOK + SEG], F32)
    relu_neg = sb("a_relu_neg", [P, 2, HB, SEG], F32)
    exp_neg = sb("a_exp_neg", [P, 2, HB, SEG], F32)
    sigma = sb("a_sigma", [P, 2, HB, SEG + 1], F32)
    row_max = sb("a_row_max", [P, HB], F32)
    shifted = sb("a_shifted", [P, HB, SEG], F32)
    probs = sb("a_probs", [P, HB, SEG], F32)
    sums = sb("a_sums", [P, 2, HB], F32)
    inv = sb("a_inv", [P, 2, HB], F32)
    weights = sb("a_weights", [P, HB, 2, SEG], F32)
    weights_t = sb("a_weights_t", [P, HB, S], F32)
    att = sb("a_att", [P, H, HB * 2, H, SEG // H], F32)
    mask = sb("a_mask", [P, HB, SEG], BF16)

    q_sb = qk[:, 0:TOK].rearrange("p (b t) -> p b t", b=HB)
    k_sb = qk[:, TOK + SEG:2 * TOK + SEG].rearrange("p (b t) -> p b t", b=HB)
    linear_in = qk[:, SEG:2 * TOK + SEG].rearrange("p (a b g t) -> p a b g t", a=2, b=HB, g=2)[:, :, :, 0, :]
    q_ps, k_ps = c.bank[0], c.bank[1]
    soft_ps = c.bank[2][:, 0:HB * SEG].rearrange("p (b t) -> p b t", b=HB)
    lin_ps = c.bank[3][:, 0:HB * (SEG + 1)].rearrange("p (b t) -> p b t", b=HB)
    t_ps = c.bank[4][:, :].rearrange("p (b s) -> p b s", b=HB)
    att_ps = c.bank[5][:, :].rearrange("p (b s) -> p b s", b=HB)
    o_ps = [c.bank[6], c.bank[7]]

    sem = c.sem
    x_loaded = [sem(f"x_loaded{i}") for i in range(HALVES)]
    gate_loaded, gate_exped, gate_made, gate_stored = (sem(f"gate_{s}") for s in ("loaded", "exped", "made", "stored"))
    gate_spread = sem("gate_spread")
    ident_zeroed, consts_ready, fills_ready = sem("ident_zeroed"), sem("consts_ready"), sem("fills_ready")
    ln_chain, var_ready, std_ready, xn_ready = sem("ln_chain"), sem("var_ready"), sem("std_ready"), sem("xn_ready")
    xt_done, xt_hi_ready, xt_lo_ready = sem("xt_done"), sem("xt_hi_ready"), sem("xt_lo_ready")
    qk_loaded = [sem(f"qk_loaded{i}") for i in range(2)]
    wo_loaded = sem("wo_loaded")
    wv_loaded = sem("wv_loaded")
    qk_hi_ready, qk_lo_ready = sem("qk_hi_ready"), sem("qk_lo_ready")
    wv_hi_ready, wv_lo_ready = sem("wv_hi_ready"), sem("wv_lo_ready")
    proj_done, qk_ready = sem("proj_done"), sem("qk_ready")
    relu_ready, expneg_ready, sigma_ready = sem("relu_ready"), sem("expneg_ready"), sem("sigma_ready")
    soft_done, lin_done = sem("soft_done"), sem("lin_done")
    max_ready, shifted_ready, probs_ready = sem("max_ready"), sem("shifted_ready"), sem("probs_ready")
    sums_ready, inv_ready, weights_ready = sem("sums_ready"), sem("inv_ready"), sem("weights_ready")
    t_done, wt_ready = sem("t_done"), sem("wt_ready")
    att_done, att_ready = sem("att_done"), sem("att_ready")
    v_done, v_ready = sem("v_done"), sem("v_ready")
    out_done, x_added = sem("out_done"), sem("x_added")

    with nc.Block() as block:
        @block.sync
        def _(sp):
            xv = x.rearrange("b s d -> s b d")

            def load_qk(h, slot):
                sp.dma_start(qk_raw[:, slot, :], wqk[bass.ds(h, 1)].rearrange("a p n -> (a p) n")).then_inc(qk_loaded[slot], 16)

            def load_wv(g):
                sp.dma_start(wv_raw[:, :, :], wv[bass.ds(g, 1)].rearrange("a p (k n) -> (a p) k n", k=KD)).then_inc(wv_loaded, 16)

            sp.dma_start(c.x_sb[:, 0:HB, :], xv[:, 0:HB, :]).then_inc(x_loaded[0], 16)
            sp.dma_start(c.x_sb[:, HB:B, :], xv[:, HB:B, :]).then_inc(x_loaded[1], 16)
            load_qk(0, 0)
            load_wv(0)
            load_qk(1, 1)
            sp.dma_start(wo_sb[:, :, :], wo.rearrange("h v n -> v h n")).then_inc(wo_loaded, 16)

            def step(s):
                if s.half < HALVES - 1 or s.looped or s.h < H - 2:
                    ahead = s.h + 2 if s.looped else (s.h + 2) % H
                    sp.wait_ge(qk_lo_ready, s.n + 1)
                    load_qk(ahead, s.j % 2)
                if s.j == 1 and not s.at(HALVES - 1, H - 3):
                    sp.wait_ge(wv_lo_ready, s.group + 1)
                    load_wv(s.group - s.half * NG + 1 if s.looped else (s.group + 1) % NG)

            head_steps(sp, step)

        @block.gpsimd
        def _(pool):
            pool.dma_start(gate_in[:, :], betas.rearrange("a h b v -> (a h b) v")).then_inc(gate_loaded, 16)
            pool.memset(c.ident[:, :], 0.0).then_inc(ident_zeroed, 1)
            pool.memset(c.ident_b[:, :], 0.0).then_inc(ident_zeroed, 1)
            pool.memset(mask[:, :, :], 0.0).then_inc(ident_zeroed, 1)
            pool.memset(c.eps[:, :], LN_EPS).then_inc(consts_ready, 1)
            pool.wait_ge(ident_zeroed, 3)
            for m in (c.ident, c.ident_b):
                pool.affine_select(out=m[:, :], in_=m[:, :], compare_op=ALU.not_equal, fill=1.0, base=0,
                                   pattern=[[-1, P]], channel_multiplier=1).then_inc(consts_ready, 1)
            for seg in range(2):
                pool.wait_ge(consts_ready, 3 + seg)
                rows = mask[seg * SEG:(seg + 1) * SEG, :, :]
                pool.affine_select(out=rows, in_=rows, compare_op=ALU.is_ge, fill=MASKED, base=0,
                                   pattern=[[0, HB], [-1, SEG]], channel_multiplier=1).then_inc(consts_ready, 1)
            pool.wait_ge(consts_ready, 5)
            pool.wait_ge(gate_made, 2)
            pool.dma_start(beta_dram.rearrange("a h v -> h a v"), gate[:, :, :]).then_inc(gate_stored, 16)
            pool.wait_ge(gate_stored, 16)
            beta_rows = beta_dram.rearrange("a h v -> a (h v)")
            pool.dma_start(gate_x[0:SEG, :], beta_rows[0:1, :].to_broadcast([SEG, H * DK])).then_inc(gate_spread, 16)
            pool.dma_start(gate_x[SEG:P, :], beta_rows[1:2, :].to_broadcast([SEG, H * DK])).then_inc(gate_spread, 16)
            pool.dma_start(gate_y[:, :], beta_rows[1:2, :].to_broadcast([P, H * DK])).then_inc(gate_spread, 16)

            def split_qk(n, slot):
                pool.wait_ge(qk_hi_ready, n + 1)
                pool.tensor_tensor(qk_lo[:, slot, :], qk_raw[:, slot, :], qk_hi[:, slot, :], ALU.subtract).then_inc(qk_lo_ready, 1)

            def split_wv(group):
                pool.wait_ge(wv_hi_ready, group + 1)
                pool.tensor_tensor(wv_lo[:, :, :], wv_raw[:, :, :], wv_hi[:, :, :], ALU.subtract).then_inc(wv_lo_ready, 1)

            split_qk(0, 0)
            split_wv(0)
            split_qk(1, 1)

            def step(s):
                if s.half < HALVES - 1 or s.looped or s.h < H - 2:
                    split_qk(s.n + 2, s.j % 2)
                if s.j == 2 and not s.at(HALVES - 1, H - 2):
                    split_wv(s.group + 1)

            head_steps(pool, step)

        @block.scalar
        def _(act):
            act.wait_ge(gate_loaded, 16)
            act.activation(gate_exp[:, 0, :], gate_in[:, :], ACT.Exp, scale=-1.0).then_inc(gate_exped, 1)
            act.activation(gate_exp[:, 1, :], gate_in[:, :], ACT.Exp).then_inc(gate_exped, 1)
            act.wait_ge(var_ready, 1)
            act.wait_ge(consts_ready, 1)
            act.activation(std[:, :], meanvar[:, :, 1], ACT.Sqrt, bias=c.eps[:, :]).then_inc(std_ready, 1)

            def split_qk(n, pair, slot):
                act.wait_ge(qk_loaded[slot], pair * 16 + 16)
                act.activation(qk_hi[:, slot, :], qk_raw[:, slot, :], ACT.Copy).then_inc(qk_hi_ready, 1)

            def split_wv(group):
                act.wait_ge(wv_loaded, group * 16 + 16)
                act.activation(wv_hi[:, :, :], wv_raw[:, :, :], ACT.Copy).then_inc(wv_hi_ready, 1)

            def evacuate_qk(n):
                act.wait_ge(proj_done, n * 2 + 1)
                act.activation(qk[:, 0:TOK], q_ps[:, :], ACT.Copy).then_inc(qk_ready, 1)
                act.wait_ge(proj_done, n * 2 + 2)
                act.activation(qk[:, TOK + SEG:2 * TOK + SEG], k_ps[:, :], ACT.Copy).then_inc(qk_ready, 1)
                act.wait_ge(qk_ready, n * 2 + 2)
                act.activation(relu_neg[:, :, :, :], linear_in, ACT.Relu, scale=-1.0).then_inc(relu_ready, 1)
                act.wait_ge(relu_ready, n + 1)
                act.activation(exp_neg[:, :, :, :], relu_neg[:, :, :, :], ACT.Exp, scale=-1.0).then_inc(expneg_ready, 1)

            def transposed_x(half):
                for k in range(KD):
                    act.wait_ge(xt_done, half * KD + k + 1)
                    act.activation(xt_hi[:, k, half * TOK:(half + 1) * TOK], c.bank[4 + k][:, :], ACT.Copy).then_inc(xt_hi_ready, 1)

            split_qk(0, 0, 0)
            split_wv(0)
            transposed_x(0)
            split_qk(1, 0, 1)
            evacuate_qk(0)
            transposed_x(1)

            def step(s):
                act.wait_ge(shifted_ready, s.n + 1)
                act.activation(probs[:, :, :], shifted[:, :, :], ACT.Exp, scale=ATT_SCALE).then_inc(probs_ready, 1)
                if s.half < HALVES - 1 or s.looped or s.h < H - 2:
                    split_qk(s.n + 2, s.pair + 1, s.j % 2)
                if not s.at(HALVES - 1, H - 1):
                    evacuate_qk(s.n + 1)
                act.wait_ge(att_done, s.n + 1)
                if s.at(1, 0):
                    act.wait_ge(out_done, HB)
                act.activation(att[:, :, :, bass.ds(s.h, 1), :].rearrange("p c g h q -> p (h g) q c"),
                               att_ps.rearrange("p b (g q c) -> p (b g) q c", g=2, c=H), ACT.Copy).then_inc(att_ready, 1)
                if s.j == 2 and not s.at(HALVES - 1, H - 2):
                    act.wait_ge(v_done, s.group * HB + HB)
                    split_wv(s.group + 1)

            head_steps(act, step)

        @block.vector
        def _(dve):
            dve.memset(sigma[:, :, :, :], 1.0 / DK).then_inc(fills_ready, 1)
            dve.memset(sums[:, :, :], 1.0).then_inc(fills_ready, 1)
            dve.memset(weights[:, :, :, :], 0.0).then_inc(fills_ready, 1)
            dve.wait_ge(gate_exped, 2)
            dve.tensor_scalar(gate_exp[:, :, :], gate_exp[:, :, :], 1.0, None, ALU.add).then_inc(gate_made, 1)
            dve.wait_ge(gate_made, 1)
            dve.reciprocal(gate[:, :, :], gate_exp[:, :, :]).then_inc(gate_made, 1)
            for b in range(B):
                if b % HB == 0:
                    dve.wait_ge(x_loaded[b // HB], 16)
                dve.bn_stats(stats[:, b, :], c.x_sb[:, b, :]).then_inc(ln_chain, 1)
            for b in range(B):
                dve.wait_ge(ln_chain, b + 1)
                last = dve.bn_aggr(meanvar[:, b, :], stats[:, b, :])
            last.then_inc(var_ready, 1)
            dve.wait_ge(std_ready, 1)
            dve.reciprocal(rstd[:, :], std[:, :]).then_inc(ln_chain, 1)
            dve.wait_ge(ln_chain, B + 1)

            def normalise(half):
                for b in range(half * HB, (half + 1) * HB):
                    dve.tensor_scalar(xn[:, b, :], c.x_sb[:, b, :], meanvar[:, b, 0:1], rstd[:, b:b + 1],
                                      ALU.subtract, ALU.mult).then_inc(xn_ready, 1)

            def transposed_x(half):
                for k in range(KD):
                    dve.wait_ge(xt_hi_ready, half * KD + k + 1)
                    hi = xt_hi[:, k, half * TOK:(half + 1) * TOK]
                    dve.tensor_tensor(xt_lo[:, k, half * TOK:(half + 1) * TOK], c.bank[4 + k][:, :], hi,
                                      ALU.subtract).then_inc(xt_lo_ready, 1)

            def sigma_of(n):
                dve.wait_ge(expneg_ready, n + 1)
                dve.scalar_tensor_tensor(out=sigma[:, :, :, 0:SEG], in0=linear_in, scalar=1.0, in1=exp_neg[:, :, :, :],
                                         op0=ALU.add, op1=ALU.max).then_inc(sigma_ready, 1)

            def scaled_values(group, cols):
                for b in range(HB):
                    v_ps = c.bank[b % 2]
                    dve.wait_ge(v_done, group * HB + b + 1)
                    dve.tensor_tensor(v_x[:, b, :], v_ps[:, :], gate_x[:, cols], ALU.mult)
                    dve.tensor_tensor(v_y[:, b, :], v_ps[:, :], gate_y[:, cols], ALU.mult).then_inc(v_ready, 1)

            normalise(0)
            normalise(1)
            transposed_x(0)
            sigma_of(0)
            dve.wait_ge(gate_spread, 48)
            scaled_values(0, bass.ds(0, GH * DK))
            transposed_x(1)

            def step(s):
                dve.wait_ge(soft_done, s.n + 1)
                dve.tensor_reduce(row_max[:, :], soft_ps, AX.X, ALU.max).then_inc(max_ready, 1)
                dve.wait_ge(max_ready, s.n + 1)
                dve.tensor_tensor(shifted[:, :, :], soft_ps, row_max[:, :].unsqueeze(2).to_broadcast([P, HB, SEG]),
                                  ALU.subtract).then_inc(shifted_ready, 1)
                dve.wait_ge(lin_done, s.n + 1)
                dve.tensor_reduce(sums[SEG:P, 1, :], lin_ps[SEG:P, :, :], AX.X, ALU.add)
                dve.wait_ge(probs_ready, s.n + 1)
                dve.tensor_reduce(sums[:, 0, :], probs[:, :, :], AX.X, ALU.add).then_inc(sums_ready, 1)
                dve.wait_ge(sums_ready, s.n + 1)
                dve.reciprocal(inv[:, :, :], sums[:, :, :]).then_inc(inv_ready, 1)
                dve.wait_ge(inv_ready, s.n + 1)
                if not s.at(0, 0):
                    dve.wait_ge(t_done, s.n)
                for seg in range(2):
                    rows = slice(seg * SEG, (seg + 1) * SEG)
                    dve.tensor_tensor(weights[rows, :, seg, :], probs[rows, :, :],
                                      inv[rows, 0, :].unsqueeze(2).to_broadcast([SEG, HB, SEG]), ALU.mult)
                dve.tensor_tensor(weights[SEG:P, :, 0, :], lin_ps[SEG:P, :, 0:SEG],
                                  inv[SEG:P, 1, :].unsqueeze(2).to_broadcast([SEG, HB, SEG]), ALU.mult).then_inc(weights_ready, 1)
                if s.at(1, 0):
                    add_output(0)
                dve.wait_ge(t_done, s.n + 1)
                dve.tensor_copy(weights_t[:, :, :], t_ps).then_inc(wt_ready, 1)
                if not s.at(HALVES - 1, H - 1):
                    sigma_of(s.n + 1)
                if s.j == GH - 1 and not s.at(HALVES - 1, H - 1):
                    first = s.group - s.half * NG + 1 if s.looped else (s.group + 1) % NG
                    scaled_values(s.group + 1, bass.ds(first * (GH * DK), GH * DK))

            def add_output(half):
                for b in range(HB):
                    dve.wait_ge(out_done, half * HB + b + 1)
                    rows = c.x_sb[:, half * HB + b, :]
                    dve.tensor_tensor(rows, rows, o_ps[b % 2][:, 0:D], ALU.add).then_inc(x_added, 1)

            head_steps(dve, step)
            add_output(HALVES - 1)

        @block.tensor
        def _(pe):
            def transpose_x(half):
                for k in range(KD):
                    pe.wait_ge(xn_ready, (half + 1) * HB)
                    for b in range(HB):
                        last = pe.transpose(c.bank[4 + k][:, b * S:(b + 1) * S],
                                            xn[:, half * HB + b, k * P:(k + 1) * P], c.ident[:, :])
                    last.then_inc(xt_done, 1)

            def split_product(out, left, right, pick_l, pick_r, start=True):
                n = 0
                for k in range(KD):
                    for a, b in ((0, 0), (0, 1), (1, 0)):
                        last = pe.matmul(out, pick_l(left[a], k), pick_r(right[b], k),
                                         start=start and n == 0, stop=n == 3 * KD - 1, skip_group_check=not start)
                        n += 1
                return last

            def project(n, half, slot, free):
                pe.wait_ge(qk_lo_ready, n + 1)
                toks = slice(half * TOK, (half + 1) * TOK)
                for i, out in enumerate((q_ps, k_ps)):
                    if free:
                        pe.wait_ge(qk_ready, n * 2 + i - 1)
                    split_product(out[:, :], (qk_hi, qk_lo), (xt_hi, xt_lo),
                                  lambda w, k: w[:, slot, (i * KD + k) * DK:(i * KD + k + 1) * DK],
                                  lambda t, k: t[:, k, toks]).then_inc(proj_done, 1)

            def project_values(n, half, group):
                pe.wait_ge(wv_lo_ready, group + 1)
                pe.wait_ge(qk_ready, n * 2 + 2)
                for b in range(HB):
                    if b >= 2:
                        pe.wait_ge(v_ready, group * HB + b - 1)
                    at = (half * HB + b) * S
                    split_product(c.bank[b % 2][:, :], (xt_hi, xt_lo), (wv_hi, wv_lo),
                                  lambda t, k: t[:, k, at:at + S], lambda w, k: w[:, k, :]).then_inc(v_done, 1)

            def soft_scores(n):
                pe.wait_ge(qk_ready, n * 2 + 2)
                pe.matmul(c.bank[2][:, 0:HB * SEG], c.ident_b[:, :], mask[:, :, :], start=True, stop=False,
                          skip_group_check=True)
                for b in range(HB):
                    for seg in range(2):
                        at = slice(seg * SEG, (seg + 1) * SEG)
                        last = pe.matmul(soft_ps[at, b, :], q_sb[:, b, at], k_sb[:, b, at], start=False, stop=True,
                                         skip_group_check=True)
                last.then_inc(soft_done, 1)

            def linear_scores(n):
                pe.wait_ge(sigma_ready, n + 1)
                for b in range(HB):
                    last = pe.matmul(lin_ps[SEG:P, b, :], sigma[:, 0, b, 0:SEG], sigma[:, 1, b, :], start=True, stop=True)
                last.then_inc(lin_done, 1)

            def output(half):
                pe.wait_ge(wo_loaded, 16)
                pe.wait_ge(att_ready, (half + 1) * H)
                for b in range(HB):
                    if half * HB + b >= 2:
                        pe.wait_ge(x_added, half * HB + b - 1)
                    for i in range(H):
                        last = pe.matmul(o_ps[b % 2][:, 0:D], att[:, i, 2 * b:2 * b + 2, :, :].rearrange("p g h q -> p (g h q)"),
                                         wo_sb[:, i, :], start=i == 0, stop=i == H - 1)
                    last.then_inc(out_done, 1)

            pe.wait_ge(consts_ready, 5)
            pe.wait_ge(fills_ready, 3)
            transpose_x(0)
            pe.wait_ge(xt_lo_ready, KD)
            project(0, 0, 0, False)
            project_values(0, 0, 0)
            soft_scores(0)
            linear_scores(0)
            transpose_x(1)

            def step(s):
                if s.j == 0:
                    pe.wait_ge(v_ready, s.group * HB + HB)
                if not s.at(HALVES - 1, H - 1):
                    next_half = s.half + 1 if s.at(s.half, H - 1) else s.half
                    if s.at(0, H - 1):
                        pe.wait_ge(xt_lo_ready, HALVES * KD)
                    project(s.n + 1, next_half, (s.j + 1) % 2, True)
                pe.wait_ge(weights_ready, s.n + 1)
                for b in range(HB):
                    last = pe.transpose(t_ps[:, b, :], weights[:, b, :, :].rearrange("p g t -> p (g t)"), c.ident[:, :])
                last.then_inc(t_done, 1)
                if not s.at(HALVES - 1, H - 1):
                    soft_scores(s.n + 1)
                pe.wait_ge(wt_ready, s.n + 1)
                if not s.at(0, 0):
                    pe.wait_ge(att_ready, s.n)
                cols = slice(s.j * DK, (s.j + 1) * DK)
                for b in range(HB):
                    pe.matmul(att_ps[:, b, 0:SEG], v_y[:, b, cols], weights_t[:, b, 0:SEG], start=True, stop=True)
                    last = pe.matmul(att_ps[:, b, SEG:S], v_x[:, b, cols], weights_t[:, b, SEG:S], start=True, stop=True)
                last.then_inc(att_done, 1)
                if not s.at(HALVES - 1, H - 1):
                    linear_scores(s.n + 1)
                    if s.j == GH - 1:
                        project_values(s.n + 1, next_half, s.group + 1)
                if s.at(s.half, H - 1):
                    output(s.half)

            head_steps(pe, step)
    phase.close()

NX, HD, L = 16, 16, 64
CROSS_SCALE = 1.0 / float(HD) ** 0.5
CH = NX // 2
ROWG = 32


def cross_phase(c, ctx_t, wq_t, wkv_t, wout_t):
    nc = c.nc
    phase = ExitStack()

    def sb(name, shape, dt):
        return c.sb(name, shape, dt, phase)

    wq = sb("x_wq", [P, KD, D], F32)
    wkv = sb("x_wkv", [L, 2 * D], F32)
    wout = sb("x_wout", [P, KD, D], F32)
    ctx_in = sb("x_ctx", [L, B, S], F32)
    xn = sb("x_xn", [P, B, D], F32)
    stats = sb("x_stats", [P, B, 6], F32)
    meanvar = sb("x_meanvar", [P, B, 2], F32)
    std = sb("x_std", [P, B], F32)
    rstd = sb("x_rstd", [P, B], F32)
    xn_t = sb("x_xn_t", [P, KD, B * S], F32)
    q_t = sb("x_q_t", [P, KD, B * S], F32)
    k_t = sb("x_k_t", [P, KD, B * S], F32)
    v_aug = sb("x_v_aug", [P, B, NX, HD + 1], F32)
    parity = sb("x_parity", [P, 2], F32)
    q_sel = sb("x_q_sel", [P, 2, KD, S], F32)
    zero_rows = sb("x_zero_rows", [P, D], F32)
    k_sel = sb("x_k_sel", [P, KD, S], F32)
    mask = sb("x_mask", [P, 4, S], BF16)
    row_max = sb("x_row_max", [P, 2, CH], F32)
    shifted = sb("x_shifted", [P, CH, S], F32)
    probs = sb("x_probs", [P, 2, CH, S], F32)
    probs_t = sb("x_probs_t", [P, 2, CH, S], F32)
    inv = sb("x_inv", [P, NX], F32)
    heads = sb("x_heads", [P, NX, HD], F32)
    heads_t = sb("x_heads_t", [P, KD, S], F32)

    s_ps = [c.psum[:, 2 * i * BANK:2 * (i + 1) * BANK].rearrange("p (h t) -> p h t", h=CH) for i in range(2)]
    t_ps = c.psum[:, 4 * BANK:6 * BANK].rearrange("p (h t) -> p h t", h=CH)
    o_ps = c.bank[6][:, 0:NX * (HD + 1)].rearrange("p (h d) -> p h d", h=NX)
    ht_ps = c.bank[7][:, 0:KD * S]
    y_ps = c.bank[7][:, KD * S:KD * S + D]

    sem = c.sem
    w_loaded, consts = sem("xw_loaded"), sem("x_consts")
    ln_chain, var_ready, std_ready, xn_ready = sem("x_ln_chain"), sem("x_var_ready"), sem("x_std_ready"), sem("x_xn_ready")
    kv_done, kv_ready = sem("x_kv_done"), sem("x_kv_ready")
    xt_done, xt_ready = sem("x_xt_done"), sem("x_xt_ready")
    q_done, q_ready, sel_ready = sem("x_q_done"), sem("x_q_ready"), sem("x_sel_ready")
    s_done, max_ready, shifted_ready = sem("x_s_done"), sem("x_max_ready"), sem("x_shifted_ready")
    probs_ready, t_done, t_ready = sem("x_probs_ready"), sem("x_t_done"), sem("x_t_ready")
    pv_done, inv_ready, heads_ready = sem("x_pv_done"), sem("x_inv_ready"), sem("x_heads_ready")
    ht_done, ht_ready, y_done, y_added = sem("x_ht_done"), sem("x_ht_ready"), sem("x_y_done"), sem("x_y_added")

    def chunk_heads(ch):
        return [(r * 4 + k * 2 + odd, 2 * ch + r, k, odd) for r in range(2) for k in range(KD) for odd in range(2)]

    def batches(eng, step):
        step(0, 0)
        step(1, 1)
        with eng.Fori(2, B - 1) as b:
            step(b, None)
        step(B - 1, B - 1)

    with nc.Block() as block:
        @block.sync
        def _(sp):
            sp.dma_start(ctx_in[:, :, :], ctx_t.rearrange("b l s -> l b s")).then_inc(w_loaded, 16)
            sp.dma_start(wkv[:, :], wkv_t).then_inc(w_loaded, 16)
            sp.dma_start(wq[:, :, :], wq_t.rearrange("(k p) n -> p k n", p=P)).then_inc(w_loaded, 16)
            sp.dma_start(wout[:, :, :], wout_t.rearrange("(k p) n -> p k n", p=P)).then_inc(w_loaded, 16)
            c.load_experts(sp, zero_rows)

        @block.gpsimd
        def _(pool):
            pool.memset(zero_rows[:, :], 0.0).then_inc(c.zeros_made, 1)
            pool.wait_ge(c.zeros_made, 1)
            pool.memset(mask[:, :, :], 0.0).then_inc(consts, 1)
            pool.memset(v_aug[:, :, :, HD:HD + 1], 1.0).then_inc(consts, 1)
            pool.memset(parity[:, :], 0.0).then_inc(consts, 1)
            pool.wait_ge(consts, 3)
            pool.affine_select(out=mask[:, :, :], in_=mask[:, :, :], compare_op=ALU.is_ge, fill=MASKED, base=0,
                               pattern=[[0, 4], [-1, S]], channel_multiplier=1).then_inc(consts, 1)
            n = 4
            for odd in range(2):
                col = parity[:, odd:odd + 1]
                for start in range(HD * odd, P, 2 * HD):
                    for base, fill in ((start, 1.0), (start + HD, 0.0)):
                        if base < P:
                            pool.wait_ge(consts, n)
                            pool.affine_select(out=col, in_=col, compare_op=ALU.is_gt, fill=fill, base=base,
                                               pattern=[[0, 1]], channel_multiplier=-1).then_inc(consts, 1)
                            n += 1
            c.n_x_consts = n
            pool.wait_ge(consts, n)

        @block.scalar
        def _(act):
            for i in range(4):
                act.wait_ge(kv_done, i + 1)
                act.activation(k_t[:, i // 2, (i % 2) * BANK:(i % 2 + 1) * BANK], c.bank[i][:, :], ACT.Copy).then_inc(kv_ready, 1)
            for i in range(4):
                act.wait_ge(kv_done, 5 + i)
                act.activation(v_aug[:, 2 * i:2 * i + 2, :, 0:HD], c.bank[4 + i][:, :].rearrange("p (b h d) -> p b h d", b=2, h=NX),
                               ACT.Copy).then_inc(kv_ready, 1)
            act.wait_ge(var_ready, 1)
            act.activation(std[:, :], meanvar[:, :, 1], ACT.Sqrt, bias=c.eps[:, :]).then_inc(std_ready, 1)
            for i in range(4):
                act.wait_ge(q_done, i + 1)
                act.activation(q_t[:, i // 2, (i % 2) * BANK:(i % 2 + 1) * BANK], c.bank[4 + i][:, :], ACT.Copy).then_inc(q_ready, 1)

            def step(b, static):
                for ch in range(2):
                    u = 2 * b + ch
                    act.wait_ge(shifted_ready, u + 1)
                    if not static == 0:
                        act.wait_ge(t_done, u - 1)
                    act.activation(probs[:, ch, :, :], shifted[:, :, :], ACT.Exp, scale=CROSS_SCALE).then_inc(probs_ready, 1)
                    act.wait_ge(t_done, u + 1)
                    if not static == 0:
                        act.wait_ge(pv_done, u - 1)
                    act.activation(probs_t[:, ch, :, :], t_ps, ACT.Copy).then_inc(t_ready, 1)
                    if ch == 0 and static != 0:
                        head_columns(b - 1)

            def head_columns(b):
                act.wait_ge(ht_done, b + 1)
                act.activation(heads_t[:, :, :], ht_ps.rearrange("p (k s) -> p k s", k=KD), ACT.Copy).then_inc(ht_ready, 1)

            batches(act, step)
            head_columns(B - 1)

        @block.vector
        def _(dve):
            for b in range(B):
                dve.bn_stats(stats[:, b, :], c.x_sb[:, b, :]).then_inc(ln_chain, 1)
            for b in range(B):
                dve.wait_ge(ln_chain, b + 1)
                last = dve.bn_aggr(meanvar[:, b, :], stats[:, b, :])
            last.then_inc(var_ready, 1)
            dve.wait_ge(std_ready, 1)
            dve.reciprocal(rstd[:, :], std[:, :]).then_inc(ln_chain, 1)
            dve.wait_ge(ln_chain, B + 1)
            for b in range(B):
                dve.tensor_scalar(xn[:, b, :], c.x_sb[:, b, :], meanvar[:, b, 0:1], rstd[:, b:b + 1],
                                  ALU.subtract, ALU.mult).then_inc(xn_ready, 1)
            for i in range(4):
                dve.wait_ge(xt_done, i + 1)
                dve.tensor_copy(xn_t[:, i % 2, (i // 2) * BANK:(i // 2 + 1) * BANK], c.bank[i][:, :]).then_inc(xt_ready, 1)

            def select(b, ch):
                rows = slice(2 * ch * ROWG, 2 * (ch + 1) * ROWG)
                at = bass.ds(b * S, S)
                for odd in range(2):
                    dve.tensor_scalar(q_sel[rows, odd, :, :], q_t[rows, :, at], parity[rows, odd:odd + 1], None, ALU.mult)
                dve.tensor_copy(k_sel[rows, :, :], k_t[rows, :, at]).then_inc(sel_ready, 1)

            dve.wait_ge(q_ready, 4)
            dve.wait_ge(kv_ready, 4)
            dve.wait_ge(consts, c.n_x_consts)
            select(0, 0)
            select(0, 1)

            def step(b, static):
                for ch in range(2):
                    u = 2 * b + ch
                    dve.wait_ge(s_done, u + 1)
                    dve.tensor_reduce(row_max[:, ch, :], s_ps[ch], AX.X, ALU.max).then_inc(max_ready, 1)
                    dve.wait_ge(max_ready, u + 1)
                    if not (static == 0 and ch == 0):
                        dve.wait_ge(probs_ready, u)
                    dve.tensor_tensor(shifted[:, :, :], s_ps[ch], row_max[:, ch, :].unsqueeze(2).to_broadcast([P, CH, S]),
                                      ALU.subtract).then_inc(shifted_ready, 1)
                    if static != B - 1:
                        select(b + 1, ch)
                    if ch == 0 and static != 0:
                        normalise(b - 1)
                    if ch == 1 and static != 0:
                        add_output(b - 1)

            def normalise(b):
                dve.wait_ge(pv_done, 2 * b + 2)
                dve.reciprocal(inv[:, :], o_ps[:, :, HD]).then_inc(inv_ready, 1)
                dve.wait_ge(inv_ready, b + 1)
                dve.tensor_tensor(heads[:, :, :], o_ps[:, :, 0:HD], inv[:, :].unsqueeze(2).to_broadcast([P, NX, HD]),
                                  ALU.mult).then_inc(heads_ready, 1)

            def add_output(b):
                dve.wait_ge(y_done, b + 1)
                rows = c.x_sb[:, bass.ds(b, 1), :].rearrange("p b d -> p (b d)")
                dve.tensor_tensor(rows, rows, y_ps, ALU.add).then_inc(y_added, 1)

            batches(dve, step)
            normalise(B - 1)
            add_output(B - 1)

        @block.tensor
        def _(pe):
            pe.wait_ge(w_loaded, 64)
            for i in range(4):
                pe.matmul(c.bank[i][:, :], wkv[:, (i // 2) * P:(i // 2 + 1) * P],
                          ctx_in[:, (i % 2) * HB:(i % 2 + 1) * HB, :], start=True, stop=True).then_inc(kv_done, 1)
            for i in range(4):
                for b in range(2):
                    last = pe.matmul(c.bank[4 + i][:, b * D:(b + 1) * D], ctx_in[:, 2 * i + b, :], wkv[:, D:2 * D],
                                     start=True, stop=True)
                last.then_inc(kv_done, 1)
            pe.wait_ge(kv_ready, 4)
            for i in range(4):
                half, k = i // 2, i % 2
                pe.wait_ge(xn_ready, (half + 1) * HB)
                for b in range(HB):
                    last = pe.transpose(c.bank[i][:, b * S:(b + 1) * S], xn[:, half * HB + b, k * P:(k + 1) * P], c.ident[:, :])
                last.then_inc(xt_done, 1)
            pe.wait_ge(kv_ready, 8)
            pe.wait_ge(xt_ready, 4)
            for i in range(4):
                for k in range(KD):
                    last = pe.matmul(c.bank[4 + i][:, :], wq[:, k, (i // 2) * P:(i // 2 + 1) * P],
                                     xn_t[:, k, (i % 2) * BANK:(i % 2 + 1) * BANK], start=k == 0, stop=k == KD - 1)
                last.then_inc(q_done, 1)
            pe.wait_ge(q_ready, 4)
            pe.wait_ge(consts, c.n_x_consts)

            def scores(b, ch, first):
                if not first:
                    pe.wait_ge(shifted_ready, 2 * b + ch - 1)
                pe.wait_ge(sel_ready, 2 * b + ch + 1)
                for r in range(2):
                    pe.matmul(c.bank[2 * ch + r][:, :], c.ident_b[:, :], mask[:, :, :], start=True, stop=False,
                              skip_group_check=True)
                for place, group, k, odd in chunk_heads(ch):
                    rows = slice(group * ROWG, (group + 1) * ROWG)
                    last = pe.matmul(s_ps[ch][:, place, :], q_sel[rows, odd, k, :], k_sel[rows, k, :],
                                     start=False, stop=True, skip_group_check=True)
                last.then_inc(s_done, 1)

            def weigh(b, ch):
                pe.wait_ge(t_ready, 2 * b + ch + 1)
                if ch == 0:
                    wait_past(pe, heads_ready, b)
                for place, group, k, odd in chunk_heads(ch):
                    head = k * CH + group * 2 + odd
                    last = pe.matmul(o_ps[:, head, :], probs_t[:, ch, place, :],
                                     v_aug[:, bass.ds(b, 1), head, :].rearrange("p b d -> p (b d)"), start=True, stop=True)
                last.then_inc(pv_done, 1)

            def transpose_weights(b, ch, first):
                pe.wait_ge(probs_ready, 2 * b + ch + 1)
                if not first:
                    pe.wait_ge(t_ready, 2 * b + ch)
                for place in range(CH):
                    last = pe.transpose(t_ps[:, place, :], probs[:, ch, place, :], c.ident[:, :])
                last.then_inc(t_done, 1)

            def transpose_heads(b):
                pe.wait_ge(heads_ready, b + 1)
                wait_past(pe, y_added, b)
                for k in range(KD):
                    last = pe.transpose(ht_ps[:, k * S:(k + 1) * S], heads[:, k * CH:(k + 1) * CH, :].rearrange("p h d -> p (h d)"),
                                        c.ident[:, :])
                last.then_inc(ht_done, 1)

            def project(b):
                pe.wait_ge(ht_ready, b + 1)
                for k in range(KD):
                    last = pe.matmul(y_ps, heads_t[:, k, :], wout[:, k, :], start=k == 0, stop=k == KD - 1)
                last.then_inc(y_done, 1)

            scores(0, 0, True)

            def step(b, static):
                scores(b, 1, static == 0)
                if static != 0:
                    weigh(b - 1, 1)
                transpose_weights(b, 0, static == 0)
                if static != 0:
                    transpose_heads(b - 1)
                if static != B - 1:
                    scores(b + 1, 0, False)
                if static != 0:
                    project(b - 1)
                weigh(b, 0)
                transpose_weights(b, 1, False)

            batches(pe, step)
            weigh(B - 1, 1)
            transpose_heads(B - 1)
            project(B - 1)
    phase.close()

NE, M = 8, 512
KM = M // P
TOPK = 2
TILES = (TOPK * B * S + NE * (P - 1)) // P + 1
EW = 2 * KD * M + KM * D


def expert_phase(c, gate_w, rows_dram, out_dram, out):
    nc = c.nc
    phase = ExitStack()

    def sb(name, shape, dt):
        return c.sb(name, shape, dt, phase)

    xn = sb("e_xn", [P, B, D], F32)
    stats = sb("e_stats", [P, B, 6], F32)
    meanvar = sb("e_meanvar", [P, B, 2], F32)
    std = sb("e_std", [P, B], F32)
    rstd = sb("e_rstd", [P, B], F32)
    xn_t = sb("e_xn_t", [P, KD, B * S], F32)
    gate = sb("e_gate", [P, KD, NE], F32)
    iota_i = sb("e_iota_i", [P, 32], I32)
    iota = sb("e_iota", [P, 32], F32)
    ones = sb("e_ones", [P, P], BF16)
    before = sb("e_before", [P, P], BF16)
    ones_f = sb("e_ones_f", [P, NE], F32)
    logits = sb("e_logits", [P, B, NE], F32)
    top = sb("e_top", [P, B, NE], F32)
    top_idx = sb("e_top_idx", [P, B, NE], U32)
    chosen_id = sb("e_chosen_id", [P, B, TOPK], F32)
    chosen = sb("e_chosen", [P, TOPK, B, NE], F32)
    either = sb("e_either", [P, B, NE], BF16)
    diff = sb("e_diff", [P, B], F32)
    ratio = sb("e_ratio", [P, B], F32)
    share = sb("e_share", [P, TOPK, B], F32)
    offsets = sb("e_offsets", [P, B + 1, NE], F32)
    n_over = sb("e_n_over", [P, NE, NE], F32)
    n_tiles = sb("e_n_tiles", [P, NE], F32)
    end_tile = sb("e_end_tile", [P, NE], F32)
    base = sb("e_base", [P, NE], F32)
    place = sb("e_place", [P, B, NE], F32)
    place_k = sb("e_place_k", [P, TOPK, B, NE], F32)
    row_f = sb("e_row_f", [P, TOPK, B], F32)
    row = sb("e_row", [P, TOPK, B], U32)
    ended = sb("e_ended", [1, TILES, NE], F32)
    owner_f = sb("e_owner_f", [1, TILES], F32)
    owner = sb("e_owner", [1, TILES], I32)
    x_rows = sb("e_x_rows", [P, 2, D], F32)
    x_cols = sb("e_x_cols", [P, 2, KD, P], F32)
    silu = sb("e_silu", [P, 2, M], F32)
    inner = sb("e_inner", [P, 2, M], F32)
    inner_t = sb("e_inner_t", [P, 2, KM, P], F32)
    y_rows = sb("e_y_rows", [P, 2, D], F32)
    picked = sb("e_picked", [P, TOPK, B, D], F32)

    x_ps = c.bank[0][:, 0:KD * P].rearrange("p (k t) -> p k t", k=KD)
    t_ps = c.bank[1].rearrange("p (m t) -> p m t", m=KM)
    y_ps = [c.bank[2][:, 0:D], c.bank[3][:, 0:D]]
    h_ps = [(c.bank[4], c.bank[5]), (c.bank[6], c.bank[7])]
    logit_ps = c.bank[0][:, 0:B * NE].rearrange("p (b e) -> p b e", b=B)
    rank_ps = c.bank[1][:, 0:B * NE].rearrange("p (b e) -> p b e", b=B)
    total_ps = c.bank[2][:, 0:B * NE].rearrange("p (b e) -> p b e", b=B)

    sem = c.sem
    gate_loaded, consts, iota_made = sem("e_gate_loaded"), sem("e_consts"), sem("e_iota_made")
    ln_chain, var_ready, std_ready, xn_ready = sem("e_ln_chain"), sem("e_var_ready"), sem("e_std_ready"), sem("e_xn_ready")
    xt_done, xt_ready = sem("e_xt_done"), sem("e_xt_ready")
    logits_done, route, diff_ready, ratio_ready = sem("e_logits_done"), sem("e_route"), sem("e_diff_ready"), sem("e_ratio_ready")
    either_ready, counts_done = sem("e_either_ready"), sem("e_counts_done")
    rows_known, owner_known, scattered = sem("e_rows_known"), sem("e_owner_known"), sem("e_scattered")
    x_loaded = [sem(f"e_x_loaded{i}") for i in range(2)]
    y_stored = [sem(f"e_y_stored{i}") for i in range(2)]
    x_done, x_ready = sem("e_x_done"), sem("e_x_ready")
    h_done, silu_ready, inner_ready = sem("e_h_done"), sem("e_silu_ready"), sem("e_inner_ready")
    t_done, t_ready, y_done, y_ready = sem("e_t_done"), sem("e_t_ready"), sem("e_y_done"), sem("e_y_ready")
    gathered = [sem(f"e_gathered{i}") for i in range(B)]
    mixed, out_stored = sem("e_mixed"), sem("e_out_stored")

    def tiles(eng, step):
        for slot in range(2):
            step(slot, slot, 0, False)
        with eng.Fori(1, TILES // 2 - 1) as pair:
            for slot in range(2):
                step(pair * 2 + slot, slot, pair, False)
        for slot in range(2):
            step(TILES - 2 + slot, slot, TILES // 2 - 1, True)

    with nc.Block() as block:
        @block.sync
        def _(sp):
            sp.dma_start(gate[:, :, :], gate_w.rearrange("(k p) e -> p k e", p=P)).then_inc(gate_loaded, 16)
            sp.wait_ge(scattered, 16 * TOPK * B)

            def load(tile, slot):
                sp.dma_start(x_rows[:, slot, :], rows_dram[bass.ds(tile * P, P), :]).then_inc(x_loaded[slot], 16)

            load(0, 0)
            load(1, 1)

            def step(tile, slot, pair, last):
                if not last:
                    sp.wait_ge(x_done, tile + 1)
                    load(tile + 2, slot)
                sp.wait_ge(y_ready, tile + 1)
                sp.dma_start(out_dram[bass.ds(tile * P, P), :], y_rows[:, slot, :]).then_inc(y_stored[slot], 16)

            tiles(sp, step)
            for b in range(B):
                sp.wait_ge(mixed, TOPK * (b + 1))
                sp.dma_start(out[b], c.x_sb[:, b, :]).then_inc(out_stored, 16)
            sp.wait_ge(out_stored, 16 * B)

        @block.gpsimd
        def _(pool):
            pool.memset(ones[:, :], 1.0).then_inc(consts, 1)
            pool.memset(before[:, :], 1.0).then_inc(consts, 1)
            pool.wait_ge(consts, 2)
            pool.affine_select(out=before[:, :], in_=before[:, :], compare_op=ALU.is_gt, fill=0.0, base=0,
                               pattern=[[1, P]], channel_multiplier=-1).then_inc(consts, 1)
            pool.wait_ge(consts, 3)
            pool.iota(iota_i[:, :], pattern=[[1, 32]], base=0, channel_multiplier=0).then_inc(iota_made, 1)
            pool.wait_ge(iota_made, 1)
            pool.wait_ge(rows_known, 1)
            pool.wait_ge(c.rows_cleared, 16)
            for b in range(B):
                for k in range(TOPK):
                    pool.indirect_dma_start(out=rows_dram, out_offset=bass.IndirectOffsetOnAxis(ap=row[:, k, b:b + 1], axis=0),
                                            in_=xn[:, b, :], in_offset=None).then_inc(scattered, 16)
            for slot in range(2):
                pool.wait_ge(y_stored[slot], 16 * (TILES // 2))
            for b in range(B):
                for k in range(TOPK):
                    pool.indirect_dma_start(out=picked[:, k, b, :], out_offset=None, in_=out_dram,
                                            in_offset=bass.IndirectOffsetOnAxis(ap=row[:, k, b:b + 1], axis=0)).then_inc(gathered[b], 16)

        @block.scalar
        def _(act):
            act.wait_ge(var_ready, 1)
            act.activation(std[:, :], meanvar[:, :, 1], ACT.Sqrt, bias=c.eps[:, :]).then_inc(std_ready, 1)
            act.wait_ge(diff_ready, 1)
            act.activation(ratio[:, :], diff[:, :], ACT.Exp).then_inc(ratio_ready, 1)

            def columns(tile, slot):
                act.wait_ge(x_done, tile + 1)
                act.activation(x_cols[:, slot, :, :], x_ps, ACT.Copy).then_inc(x_ready, 1)

            columns(0, 0)

            def step(tile, slot, pair, last):
                act.wait_ge(h_done, tile * 2 + 1)
                act.activation(silu[:, slot, :], h_ps[slot][0], ACT.Silu).then_inc(silu_ready, 1)
                if not (last and slot):
                    columns(tile + 1, 1 - slot)
                act.wait_ge(t_done, tile + 1)
                act.activation(inner_t[:, slot, :, :], t_ps, ACT.Copy).then_inc(t_ready, 1)

            tiles(act, step)

        @block.vector
        def _(dve):
            for b in range(B):
                dve.bn_stats(stats[:, b, :], c.x_sb[:, b, :]).then_inc(ln_chain, 1)
            for b in range(B):
                dve.wait_ge(ln_chain, b + 1)
                last = dve.bn_aggr(meanvar[:, b, :], stats[:, b, :])
            last.then_inc(var_ready, 1)
            dve.wait_ge(std_ready, 1)
            dve.reciprocal(rstd[:, :], std[:, :]).then_inc(ln_chain, 1)
            dve.wait_ge(ln_chain, B + 1)
            for b in range(B):
                dve.tensor_scalar(xn[:, b, :], c.x_sb[:, b, :], meanvar[:, b, 0:1], rstd[:, b:b + 1],
                                  ALU.subtract, ALU.mult).then_inc(xn_ready, 1)
            for i in range(4):
                dve.wait_ge(xt_done, i + 1)
                dve.tensor_copy(xn_t[:, i % 2, (i // 2) * BANK:(i // 2 + 1) * BANK], c.bank[4 + i][:, :]).then_inc(xt_ready, 1)

            n_route = [0]

            def chained(instruction):
                n_route[0] += 1
                instruction.then_inc(route, 1)
                dve.wait_ge(route, n_route[0])

            dve.wait_ge(iota_made, 1)
            chained(dve.tensor_copy(iota[:, :], iota_i[:, :]))
            chained(dve.memset(ones_f[:, :], 1.0))
            dve.wait_ge(logits_done, 1)
            chained(dve.tensor_copy(logits[:, :, :], logit_ps))
            for b in range(B):
                dve.max(top[:, b, :], logits[:, b, :])
            chained(dve.memset(offsets[:, 0, :], 0.0))
            for b in range(B):
                last = dve.max_index(top_idx[:, b, :], top[:, b, :], logits[:, b, :])
            chained(last)
            dve.tensor_tensor(diff[:, :], top[:, :, 1], top[:, :, 0], ALU.subtract).then_inc(diff_ready, 1)
            chained(dve.tensor_copy(chosen_id[:, :, :], top_idx[:, :, 0:TOPK]))
            ids = iota[:, 0:NE].unsqueeze(1).to_broadcast([P, B, NE])
            for k in range(TOPK):
                chained(dve.tensor_tensor(chosen[:, k, :, :], ids, chosen_id[:, :, k].unsqueeze(2).to_broadcast([P, B, NE]), ALU.is_equal))
            dve.tensor_tensor(either[:, :, :], chosen[:, 0, :, :], chosen[:, 1, :, :], ALU.add).then_inc(either_ready, 1)
            dve.wait_ge(ratio_ready, 1)
            chained(dve.tensor_scalar(share[:, 1, :], ratio[:, :], 1.0, None, ALU.add))
            chained(dve.reciprocal(share[:, 0, :], share[:, 1, :]))
            chained(dve.tensor_tensor(share[:, 1, :], share[:, 0, :], ratio[:, :], ALU.mult))
            dve.wait_ge(counts_done, 1)
            for b in range(B):
                chained(dve.tensor_tensor(offsets[:, b + 1, :], total_ps[:, b, :], offsets[:, b, :], ALU.add))
            chained(dve.tensor_scalar(n_over[:, 0, :], iota[:, 0:NE], float(P), None, ALU.mult))
            chained(dve.tensor_copy(base[:, :], n_over[:, 0, :]))
            chained(dve.tensor_tensor(n_over[:, :, :], offsets[:, B, :].unsqueeze(2).to_broadcast([P, NE, NE]),
                                      base[:, :].unsqueeze(1).to_broadcast([P, NE, NE]), ALU.is_gt))
            chained(dve.tensor_reduce(n_tiles[:, :], n_over[:, :, :], AX.X, ALU.add))
            chained(dve.tensor_tensor_scan(end_tile[:, :], ones_f[:, :], n_tiles[:, :], 0.0, ALU.mult, ALU.add))
            chained(dve.tensor_tensor(base[:, :], end_tile[:, :], n_tiles[:, :], ALU.subtract))
            chained(dve.tensor_scalar(base[:, :], base[:, :], float(P), None, ALU.mult))
            chained(dve.tensor_tensor(place[:, :, :], rank_ps, offsets[:, 0:B, :], ALU.add))
            chained(dve.tensor_tensor(place[:, :, :], place[:, :, :], base[:, :].unsqueeze(1).to_broadcast([P, B, NE]), ALU.add))
            for k in range(TOPK):
                last = dve.tensor_tensor(place_k[:, k, :, :], chosen[:, k, :, :], place[:, :, :], ALU.mult)
            chained(last)
            chained(dve.tensor_reduce(row_f[:, :, :], place_k[:, :, :, :], AX.X, ALU.add))
            dve.tensor_copy(row[:, :, :], row_f[:, :, :]).then_inc(rows_known, 1)
            chained(dve.tensor_tensor(ended[:, :, :], end_tile[0:1, :].unsqueeze(1).to_broadcast([1, TILES, NE]),
                                      iota[0:1, 0:TILES].unsqueeze(2).to_broadcast([1, TILES, NE]), ALU.is_le))
            chained(dve.tensor_reduce(owner_f[:, :], ended[:, :, :], AX.X, ALU.add))
            chained(dve.tensor_scalar(owner_f[:, :], owner_f[:, :], float(NE - 1), float(EW), ALU.min, ALU.mult))
            dve.tensor_copy(owner[:, :], owner_f[:, :]).then_inc(owner_known, 1)

            def step(tile, slot, pair, last):
                dve.wait_ge(h_done, tile * 2 + 2)
                dve.wait_ge(silu_ready, tile + 1)
                dve.tensor_tensor(inner[:, slot, :], h_ps[slot][1], silu[:, slot, :], ALU.mult).then_inc(inner_ready, 1)
                dve.wait_ge(y_done, tile + 1)
                wait_past(dve, y_stored[slot], pair * 16)
                dve.tensor_copy(y_rows[:, slot, :], y_ps[slot]).then_inc(y_ready, 1)

            tiles(dve, step)
            for b in range(B):
                dve.wait_ge(gathered[b], 16 * TOPK)
                for k in range(TOPK):
                    if k:
                        dve.wait_ge(mixed, TOPK * b + k)
                    dve.scalar_tensor_tensor(out=c.x_sb[:, b, :], in0=picked[:, k, b, :], scalar=share[:, k, b:b + 1],
                                             in1=c.x_sb[:, b, :], op0=ALU.mult, op1=ALU.add).then_inc(mixed, 1)

        @block.tensor
        def _(pe):
            for i in range(4):
                half, k = i // 2, i % 2
                pe.wait_ge(xn_ready, (half + 1) * HB)
                for b in range(HB):
                    last = pe.transpose(c.bank[4 + i][:, b * S:(b + 1) * S], xn[:, half * HB + b, k * P:(k + 1) * P], c.ident[:, :])
                last.then_inc(xt_done, 1)
            pe.wait_ge(gate_loaded, 16)
            pe.wait_ge(xt_ready, 4)
            for b in range(B):
                for k in range(KD):
                    last = pe.matmul(logit_ps[:, b, :], xn_t[:, k, b * S:(b + 1) * S], gate[:, k, :], start=k == 0, stop=k == KD - 1)
            last.then_inc(logits_done, 1)
            pe.wait_ge(consts, 3)
            pe.wait_ge(either_ready, 1)
            pe.matmul(rank_ps, before[:, :], either[:, :, :], start=True, stop=True)
            pe.matmul(total_ps, ones[:, :], either[:, :, :], start=True, stop=True).then_inc(counts_done, 1)

            def columns(tile, slot, pair, first):
                pe.wait_ge(x_loaded[slot], pair * 16 + 16)
                if not first:
                    pe.wait_ge(x_ready, tile)
                for k in range(KD):
                    last = pe.transpose(x_ps[:, k, :], x_rows[:, slot, k * P:(k + 1) * P], c.ident[:, :])
                last.then_inc(x_done, 1)

            def expand(tile, slot, first):
                at = pe.value_load(owner[0:1, bass.ds(tile, 1)], min_val=0, max_val=(NE - 1) * EW)
                pe.wait_ge(x_ready, tile + 1)
                for i in range(2):
                    if not first:
                        wait_past(pe, inner_ready, tile - 1)
                    for k in range(KD):
                        last = pe.matmul(h_ps[slot][i], x_cols[:, slot, k, :], c.expert_w[:, bass.ds(at + (i * KD + k) * M, M)],
                                         start=k == 0, stop=k == KD - 1)
                    last.then_inc(h_done, 1)
                return at

            def reduce(tile, slot, pair):
                at = pe.value_load(owner[0:1, bass.ds(tile, 1)], min_val=0, max_val=(NE - 1) * EW)
                pe.wait_ge(inner_ready, tile + 1)
                wait_past(pe, t_ready, tile)
                for m in range(KM):
                    last = pe.transpose(t_ps[:, m, :], inner[:, slot, m * P:(m + 1) * P], c.ident[:, :])
                last.then_inc(t_done, 1)
                pe.wait_ge(t_ready, tile + 1)
                wait_past(pe, y_ready, pair * 2)
                for m in range(KM):
                    last = pe.matmul(y_ps[slot], inner_t[:, slot, m, :], c.expert_w[:, bass.ds(at + 2 * KD * M + m * D, D)],
                                     start=m == 0, stop=m == KM - 1)
                last.then_inc(y_done, 1)

            pe.wait_ge(owner_known, 1)
            pe.wait_ge(c.experts_loaded, 16 * NE)
            columns(0, 0, 0, True)
            expand(0, 0, True)

            def step(tile, slot, pair, last):
                if not (last and slot):
                    columns(tile + 1, 1 - slot, pair + slot, False)
                    expand(tile + 1, 1 - slot, False)
                reduce(tile, slot, pair)

            tiles(pe, step)
    phase.close()


def decoder_layer(nc, x, betas, wqk, wv, wo, ctx_t, xwq_t, xwkv_t, xwout_t, gate_w, expert_w, out):
    gates_dram = nc.dram_tensor("gates_dram", (2, H, DK), F32, kind="Internal").ap()
    rows_dram = nc.dram_tensor("rows_dram", (TILES * P, D), F32, kind="Internal").ap()
    out_dram = nc.dram_tensor("expert_out_dram", (TILES * P, D), F32, kind="Internal").ap()
    with ExitStack() as ctx:
        c = Core(nc, ctx)
        c.experts_loaded, c.rows_cleared, c.zeros_made = c.sem("experts_loaded"), c.sem("rows_cleared"), c.sem("zeros_made")
        attention_phase(c, x, betas, wqk, wv, wo, gates_dram)
        c.expert_w = c.sb("expert_w", [P, NE * EW], F32)

        def load_experts(sp, zero_rows):
            sp.wait_ge(c.zeros_made, 1)
            sp.dma_start(rows_dram.rearrange("(n p) d -> p n d", p=P), zero_rows[:, :].unsqueeze(1).to_broadcast([P, TILES, D])).then_inc(c.rows_cleared, 16)
            for e in range(NE):
                sp.dma_start(c.expert_w[:, e * EW:(e + 1) * EW], expert_w[e]).then_inc(c.experts_loaded, 16)

        c.load_experts = load_experts
        cross_phase(c, ctx_t, xwq_t, xwkv_t, xwout_t)
        expert_phase(c, gate_w, rows_dram, out_dram, out)


def kernel(x, ctx_512, L0_attn_Wq, L0_attn_Wk, L0_attn_Wv, L0_attn_Wo, L0_attn_betas, L0_xattn_Wq, L0_xattn_Wkv_expand,
           L0_xattn_Wout, L0_ffn_gate_kernel, L0_ffn_w0_kernel, L0_ffn_w1_kernel, L0_ffn_wo_kernel):
    import numpy as np
    import concourse.bacc as bacc
    from concourse.bass_utils import run_bass_kernel_spmd

    def laid(a):
        return np.ascontiguousarray(a)

    def rows(w):
        w = np.asarray(w)
        lead = w.shape[:-2]
        w = w.reshape(*lead, w.shape[-2] // P, P, w.shape[-1])
        return np.moveaxis(w, -3, -2).reshape(*lead, P, -1)

    def by_head(w, n):
        w = np.asarray(w)
        return np.moveaxis(w.reshape(w.shape[0], H // n, n * DK), 1, 0)

    arrays = {
        "x": laid(x),
        "betas": laid(L0_attn_betas),
        "wqk": laid(np.concatenate([rows(by_head(L0_attn_Wq, 1)), rows(by_head(L0_attn_Wk, 1))], axis=-1)),
        "wv": laid(rows(by_head(L0_attn_Wv, GH))),
        "wo": laid(np.asarray(L0_attn_Wo).reshape(H, DK, D)),
        "ctx_t": laid(np.asarray(ctx_512).transpose(0, 2, 1)),
        "xwq_t": laid(np.asarray(L0_xattn_Wq).T),
        "xwkv_t": laid(np.asarray(L0_xattn_Wkv_expand).T),
        "xwout_t": laid(np.asarray(L0_xattn_Wout).T),
        "gate_w": laid(L0_ffn_gate_kernel),
        "expert_w": laid(np.concatenate([rows(L0_ffn_w0_kernel), rows(L0_ffn_w1_kernel), rows(L0_ffn_wo_kernel)], axis=-1)),
    }
    nc = bacc.Bacc("TRN2", target_bir_lowering=False, num_devices=1)
    args = [nc.dram_tensor(f"in_{name}", a.shape, mybir.dt.from_np(a.dtype), kind="ExternalInput").ap() for name, a in arrays.items()]
    out = nc.dram_tensor("out_0", (B, S, D), F32, kind="ExternalOutput").ap()
    decoder_layer(nc, *args, out)
    r = run_bass_kernel_spmd(nc, [{f"in_{name}": a for name, a in arrays.items()}], core_ids=[0])
    return r.results[0]["out_0"]
```

```python
from contextlib import ExitStack

import concourse.bass as bass
from concourse import mybir

F32 = mybir.dt.float32
F32R = mybir.dt.float32r
BF16 = mybir.dt.bfloat16
I32 = mybir.dt.int32
U32 = mybir.dt.uint32
ALU = mybir.AluOpType
ACT = mybir.ActivationFunctionType
AX = mybir.AxisListType

P = 128
BANK = 512
B, S, D = 8, 128, 256
KD = D // P
H, DK, SEG = 16, 128, 64
HB = 4
HALVES = B // HB
TOK = HB * S
TURN = 4
GH = 2
NG = H // GH
LN_EPS = 1e-5
MASKED = -3.0e38
ATT_SCALE = 1.0 / float(DK) ** 0.5


class Core:

    def __init__(self, nc, ctx):
        self.nc, self.ctx = nc, ctx
        self.psum = ctx.enter_context(nc.psum_tensor("psum", [P, 8 * BANK], F32))
        self.bank = [self.psum[:, i * BANK:(i + 1) * BANK] for i in range(8)]
        self.x_sb = self.sb("x_sb", [P, B, D], F32)
        self.ident = self.sb("ident", [P, P], F32)
        self.ident_b = self.sb("ident_b", [P, P], BF16)
        self.eps = self.sb("eps", [P, 1], F32)

    def sb(self, name, shape, dt, ctx=None):
        return (ctx or self.ctx).enter_context(self.nc.sbuf_tensor(name, shape, dt))

    def sem(self, name):
        return self.ctx.enter_context(self.nc.semaphore(name))


def wait_past(eng, sem, value):
    if not isinstance(value, int) or value > 0:
        eng.wait_ge(sem, value)


class Head:

    def __init__(self, half, first, loop=None):
        turns = loop if loop is not None else 0
        self.half, self.j, self.looped = half, first % TURN, loop is not None
        self.member, self.slot = self.j % GH, self.j // GH
        self.h = turns * TURN + first
        self.n = turns * TURN + (first + half * H)
        self.pair = turns * (TURN // GH) + (first + half * H) // GH
        self.quad = turns + (first + half * H) // TURN

    def at(self, half, h):
        return not self.looped and self.half == half and self.h == h

    def follows(self, n):
        return self.looped or self.half < HALVES - 1 or self.h + n < H

    def next_pair(self, n):
        at = self.pair - self.half * NG + n
        return at if self.looped else at % NG


def head_steps(eng, step):
    for half in range(HALVES):
        step(Head(half, 0))
        with eng.Fori(0, H // TURN - 1) as turn:
            for first in range(1, 1 + TURN):
                step(Head(half, first, turn))
        for h in range(H - 3, H):
            step(Head(half, h))


def attention_phase(c, x, betas_t, wqk, wv, wo):
    nc = c.nc
    phase = ExitStack()

    def sb(name, shape, dt):
        return c.sb(name, shape, dt, phase)

    xn = sb("a_xn", [P, B, D], F32)
    stats = sb("a_stats", [P, B, 6], F32)
    meanvar = sb("a_meanvar", [P, B, 2], F32)
    std = sb("a_std", [P, B], F32)
    rstd = sb("a_rstd", [P, B], F32)
    xt_hi = sb("a_xt_hi", [P, KD, B * S], F32R)
    xt_lo = sb("a_xt_lo", [P, KD, B * S], F32R)
    qk_raw = sb("a_qk_raw", [P, 2, 2 * KD * DK], F32)
    qk_hi = sb("a_qk_hi", [P, 2, 2 * KD * DK], F32R)
    qk_lo = sb("a_qk_lo", [P, 2, 2 * KD * DK], F32R)
    wo_sb = sb("a_wo", [P, H, D], F32)
    wv_raw = sb("a_wv_raw", [P, 2, KD, GH * DK], F32)
    wv_hi = sb("a_wv_hi", [P, 2, KD, GH * DK], F32R)
    wv_lo = sb("a_wv_lo", [P, 2, KD, GH * DK], F32R)
    gate_in = sb("a_gate_in", [DK, H], F32)
    gate_exp = sb("a_gate_exp", [DK, 2, H], F32)
    gate = sb("a_gate", [DK, 2, H], F32)
    v_sb = sb("a_v", [P, 2, HB, GH * DK], F32)
    qk = sb("a_qk", [P, 2 * TOK + SEG], F32)
    relu_neg = sb("a_relu_neg", [P, 2, HB, SEG], F32)
    exp_neg = sb("a_exp_neg", [P, 2, HB, SEG], F32)
    sigma = sb("a_sigma", [P, 2, HB, SEG + 1], F32)
    row_max = sb("a_row_max", [P, HB], F32)
    shifted = sb("a_shifted", [P, HB, SEG], F32)
    probs = sb("a_probs", [P, HB, SEG], F32)
    sums = sb("a_sums", [P, 2, HB], F32)
    inv = sb("a_inv", [P, 2, HB], F32)
    weights = sb("a_weights", [P, HB, 2, SEG], F32)
    weights_t = sb("a_weights_t", [P, HB, 3, SEG], F32)
    att = sb("a_att", [P, HB, 2, H, SEG], F32)
    mask = sb("a_mask", [P, HB, SEG], BF16)

    q_sb = qk[:, 0:TOK].rearrange("p (b t) -> p b t", b=HB)
    k_sb = qk[:, TOK + SEG:2 * TOK + SEG].rearrange("p (b t) -> p b t", b=HB)
    linear_in = qk[:, SEG:2 * TOK + SEG].rearrange("p (a b g t) -> p a b g t", a=2, b=HB, g=2)[:, :, :, 0, :]
    q_ps, k_ps = c.bank[0], c.bank[1]
    soft_ps = c.bank[2][:, 0:HB * SEG].rearrange("p (b t) -> p b t", b=HB)
    lin_ps = c.bank[3][:, 0:HB * (SEG + 1)].rearrange("p (b t) -> p b t", b=HB)
    t_ps = c.bank[4][:, :].rearrange("p (b s) -> p b s", b=HB)
    att_ps = [c.bank[i][:, 0:2 * 3 * SEG].rearrange("p (b g s) -> p b g s", b=2, g=3) for i in (5, 7)]
    v_ps = c.bank[6].rearrange("p (b n) -> p b n", b=2)
    o_ps = [c.bank[7][:, 0:D], c.bank[6][:, 0:D]]

    sem = c.sem
    x_loaded = [sem(f"x_loaded{i}") for i in range(HALVES)]
    gate_loaded, gate_exped, gate_made = (sem(f"gate_{s}") for s in ("loaded", "exped", "made"))
    ident_zeroed, consts_ready, fills_ready = sem("ident_zeroed"), sem("consts_ready"), sem("fills_ready")
    ln_chain, var_ready, std_ready, xn_ready = sem("ln_chain"), sem("var_ready"), sem("std_ready"), sem("xn_ready")
    xt_done, xt_hi_ready, xt_lo_ready = sem("xt_done"), sem("xt_hi_ready"), sem("xt_lo_ready")
    qk_loaded = [sem(f"qk_loaded{i}") for i in range(2)]
    wo_loaded = sem("wo_loaded")
    wv_loaded = [sem(f"wv_loaded{i}") for i in range(2)]
    qk_hi_ready, qk_lo_ready = sem("qk_hi_ready"), sem("qk_lo_ready")
    wv_hi_ready, wv_lo_ready = sem("wv_hi_ready"), sem("wv_lo_ready")
    proj_done, qk_ready = sem("proj_done"), sem("qk_ready")
    relu_ready, expneg_ready, sigma_ready = sem("relu_ready"), sem("expneg_ready"), sem("sigma_ready")
    soft_done, lin_done = sem("soft_done"), sem("lin_done")
    max_ready, shifted_ready, probs_ready = sem("max_ready"), sem("shifted_ready"), sem("probs_ready")
    sums_ready, inv_ready, weights_ready = sem("sums_ready"), sem("inv_ready"), sem("weights_ready")
    t_done, wt_ready, wt_near_ready = sem("t_done"), sem("wt_ready"), sem("wt_near_ready")
    att_done, att_ready, memory_added = sem("att_done"), sem("att_ready"), sem("memory_added")
    v_done, v_ready = sem("v_done"), sem("v_ready")
    out_done, x_added = sem("out_done"), sem("x_added")

    def att_of(h, i, seg):
        return att[:, 2 * i:2 * i + 2, seg, bass.ds(h, 1), :].rearrange("p b h s -> p (h b) s")

    with nc.Block() as block:
        @block.sync
        def _(sp):
            xv = x.rearrange("b s d -> s b d")

            def load_qk(h, slot):
                sp.dma_start(qk_raw[:, slot, :], wqk[bass.ds(h, 1)].rearrange("a p n -> (a p) n")).then_inc(qk_loaded[slot], 16)

            def load_wv(g, slot):
                sp.dma_start(wv_raw[:, slot, :, :], wv[bass.ds(g, 1)].rearrange("a p (k n) -> (a p) k n", k=KD)).then_inc(wv_loaded[slot], 16)

            sp.dma_start(c.x_sb[:, 0:HB, :], xv[:, 0:HB, :]).then_inc(x_loaded[0], 16)
            sp.dma_start(c.x_sb[:, HB:B, :], xv[:, HB:B, :]).then_inc(x_loaded[1], 16)
            load_qk(0, 0)
            load_wv(0, 0)
            load_qk(1, 1)
            load_wv(1, 1)
            sp.dma_start(wo_sb[:, :, :], wo.rearrange("h v n -> v h n")).then_inc(wo_loaded, 16)

            def step(s):
                if s.follows(2):
                    ahead = s.h + 2 if s.looped else (s.h + 2) % H
                    sp.wait_ge(qk_lo_ready, s.n + 1)
                    load_qk(ahead, s.j % 2)
                if s.member == 0 and s.follows(4):
                    sp.wait_ge(wv_lo_ready, s.pair + 1)
                    load_wv(s.next_pair(2), s.slot)

            head_steps(sp, step)

        @block.gpsimd
        def _(pool):
            pool.dma_start(gate_in[:, :], betas_t).then_inc(gate_loaded, 16)
            pool.memset(c.ident[:, :], 0.0).then_inc(ident_zeroed, 1)
            pool.memset(c.ident_b[:, :], 0.0).then_inc(ident_zeroed, 1)
            pool.memset(mask[:, :, :], 0.0).then_inc(ident_zeroed, 1)
            pool.memset(c.eps[:, :], LN_EPS).then_inc(consts_ready, 1)
            pool.wait_ge(ident_zeroed, 3)
            for m in (c.ident, c.ident_b):
                pool.affine_select(out=m[:, :], in_=m[:, :], compare_op=ALU.not_equal, fill=1.0, base=0,
                                   pattern=[[-1, P]], channel_multiplier=1).then_inc(consts_ready, 1)
            for seg in range(2):
                pool.wait_ge(consts_ready, 3 + seg)
                rows = mask[seg * SEG:(seg + 1) * SEG, :, :]
                pool.affine_select(out=rows, in_=rows, compare_op=ALU.is_ge, fill=MASKED, base=0,
                                   pattern=[[0, HB], [-1, SEG]], channel_multiplier=1).then_inc(consts_ready, 1)
            pool.wait_ge(consts_ready, 5)
            def split_qk(n, slot):
                pool.wait_ge(qk_hi_ready, n + 1)
                pool.tensor_tensor(qk_lo[:, slot, :], qk_raw[:, slot, :], qk_hi[:, slot, :], ALU.subtract).then_inc(qk_lo_ready, 1)

            def split_wv(group, slot):
                pool.wait_ge(wv_hi_ready, group + 1)
                pool.tensor_tensor(wv_lo[:, slot, :, :], wv_raw[:, slot, :, :], wv_hi[:, slot, :, :],
                                   ALU.subtract).then_inc(wv_lo_ready, 1)

            split_qk(0, 0)
            split_wv(0, 0)
            split_qk(1, 1)
            split_wv(1, 1)

            def step(s):
                if s.follows(2):
                    split_qk(s.n + 2, s.member)
                if s.member == 1 and s.follows(3):
                    split_wv(s.pair + 2, s.slot)

            head_steps(pool, step)

        @block.scalar
        def _(act):
            act.wait_ge(gate_loaded, 16)
            act.activation(gate_exp[:, 0, :], gate_in[:, :], ACT.Exp, scale=-1.0).then_inc(gate_exped, 1)
            act.activation(gate_exp[:, 1, :], gate_in[:, :], ACT.Exp).then_inc(gate_exped, 1)
            act.wait_ge(var_ready, 1)
            act.wait_ge(consts_ready, 1)
            act.activation(std[:, :], meanvar[:, :, 1], ACT.Sqrt, bias=c.eps[:, :]).then_inc(std_ready, 1)

            def split_qk(n, pair, slot):
                act.wait_ge(qk_loaded[slot], pair * 16 + 16)
                act.activation(qk_hi[:, slot, :], qk_raw[:, slot, :], ACT.Copy).then_inc(qk_hi_ready, 1)

            def split_wv(turn_pair, slot):
                act.wait_ge(wv_loaded[slot], turn_pair * 16 + 16)
                act.activation(wv_hi[:, slot, :, :], wv_raw[:, slot, :, :], ACT.Copy).then_inc(wv_hi_ready, 1)

            def near_weights(n):
                act.wait_ge(t_done, n + 1)
                act.activation(weights_t[0:SEG, :, 0:3:2, :], t_ps[0:SEG, :, :].rearrange("p b (g s) -> p b g s", g=2),
                               ACT.Copy).then_inc(wt_near_ready, 1)

            def evacuate_qk(n):
                act.wait_ge(proj_done, n * 2 + 1)
                act.activation(qk[:, 0:TOK], q_ps[:, :], ACT.Copy).then_inc(qk_ready, 1)
                act.wait_ge(proj_done, n * 2 + 2)
                act.activation(qk[:, TOK + SEG:2 * TOK + SEG], k_ps[:, :], ACT.Copy).then_inc(qk_ready, 1)
                if not (isinstance(n, int) and n == 0):
                    near_weights(n - 1)
                act.wait_ge(qk_ready, n * 2 + 2)
                act.activation(relu_neg[:, :, :, :], linear_in, ACT.Relu, scale=-1.0).then_inc(relu_ready, 1)
                act.wait_ge(relu_ready, n + 1)
                act.activation(exp_neg[:, :, :, :], relu_neg[:, :, :, :], ACT.Exp, scale=-1.0).then_inc(expneg_ready, 1)

            def evacuate_values(fill, part, slot):
                act.wait_ge(v_done, fill + 1)
                act.activation(v_sb[:, slot, 2 * part:2 * part + 2, :], v_ps, ACT.Copy).then_inc(v_ready, 1)

            def transposed_x(half):
                for k in range(KD):
                    act.wait_ge(xt_done, half * KD + k + 1)
                    act.activation(xt_hi[:, k, half * TOK:(half + 1) * TOK], c.bank[4 + k][:, :], ACT.Copy).then_inc(xt_hi_ready, 1)

            split_qk(0, 0, 0)
            split_wv(0, 0)
            transposed_x(0)
            split_qk(1, 0, 1)
            split_wv(0, 1)
            evacuate_qk(0)
            for part in range(2):
                evacuate_values(part, part, 0)
            transposed_x(1)
            act.wait_ge(gate_made, 2)

            def gate_products(h, n):
                act.wait_ge(att_done, n + 1)
                for i in range(2):
                    out = att[:, 2 * i:2 * i + 2, :, bass.ds(h, 1), :].rearrange("p b g h s -> p (h b) g s")
                    act.activation(out, att_ps[i][:, :, 0:2, :], ACT.Copy, scale=gate[:, 1, bass.ds(h, 1)]).then_inc(att_ready, 1)

            def step(s):
                if s.at(1, 0):
                    gate_products(H - 1, s.n - 1)
                act.wait_ge(shifted_ready, s.n + 1)
                act.activation(probs[:, :, :], shifted[:, :, :], ACT.Exp, scale=ATT_SCALE).then_inc(probs_ready, 1)
                if s.looped or s.h > 0:
                    gate_products(s.h - 1, s.n - 1)
                if s.follows(2):
                    split_qk(s.n + 2, s.pair + 1, s.member)
                if s.member == 1 and s.follows(3):
                    act.wait_ge(v_done, s.n + 1)
                    split_wv(s.quad + 1, s.slot)
                if s.at(1, 0):
                    act.wait_ge(out_done, HB)
                if not s.at(HALVES - 1, H - 1):
                    evacuate_qk(s.n + 1)
                else:
                    near_weights(s.n)
                if s.follows(2):
                    if not s.at(0, 0):
                        act.wait_ge(att_done, s.n)
                    evacuate_values(s.n + 2, s.member, 1 - s.slot)

            head_steps(act, step)
            gate_products(H - 1, HALVES * H - 1)

        @block.vector
        def _(dve):
            dve.memset(sigma[:, :, :, :], 1.0 / DK).then_inc(fills_ready, 1)
            dve.memset(sums[:, :, :], 1.0).then_inc(fills_ready, 1)
            dve.memset(weights_t[:, :, :, :], 0.0).then_inc(fills_ready, 1)
            dve.memset(weights[:, :, :, :], 0.0).then_inc(fills_ready, 1)
            dve.wait_ge(gate_exped, 2)
            dve.tensor_scalar(gate_exp[:, :, :], gate_exp[:, :, :], 1.0, None, ALU.add).then_inc(gate_made, 1)
            dve.wait_ge(gate_made, 1)
            dve.reciprocal(gate[:, :, :], gate_exp[:, :, :]).then_inc(gate_made, 1)
            for b in range(B):
                if b % HB == 0:
                    dve.wait_ge(x_loaded[b // HB], 16)
                dve.bn_stats(stats[:, b, :], c.x_sb[:, b, :]).then_inc(ln_chain, 1)
            for b in range(B):
                dve.wait_ge(ln_chain, b + 1)
                last = dve.bn_aggr(meanvar[:, b, :], stats[:, b, :])
            last.then_inc(var_ready, 1)
            dve.wait_ge(std_ready, 1)
            dve.reciprocal(rstd[:, :], std[:, :]).then_inc(ln_chain, 1)
            dve.wait_ge(ln_chain, B + 1)

            def normalise(half):
                for b in range(half * HB, (half + 1) * HB):
                    dve.tensor_scalar(xn[:, b, :], c.x_sb[:, b, :], meanvar[:, b, 0:1], rstd[:, b:b + 1],
                                      ALU.subtract, ALU.mult).then_inc(xn_ready, 1)

            def transposed_x(half):
                for k in range(KD):
                    dve.wait_ge(xt_hi_ready, half * KD + k + 1)
                    hi = xt_hi[:, k, half * TOK:(half + 1) * TOK]
                    dve.tensor_tensor(xt_lo[:, k, half * TOK:(half + 1) * TOK], c.bank[4 + k][:, :], hi,
                                      ALU.subtract).then_inc(xt_lo_ready, 1)

            def sigma_of(n):
                dve.wait_ge(expneg_ready, n + 1)
                dve.scalar_tensor_tensor(out=sigma[:, :, :, 0:SEG], in0=linear_in, scalar=1.0, in1=exp_neg[:, :, :, :],
                                         op0=ALU.add, op1=ALU.max).then_inc(sigma_ready, 1)

            normalise(0)
            normalise(1)
            transposed_x(0)
            sigma_of(0)
            transposed_x(1)

            def step(s):
                if s.at(1, 0):
                    add_memory(H - 1, s.n - 1)
                dve.wait_ge(soft_done, s.n + 1)
                dve.tensor_reduce(row_max[:, :], soft_ps, AX.X, ALU.max).then_inc(max_ready, 1)
                dve.wait_ge(max_ready, s.n + 1)
                dve.tensor_tensor(shifted[:, :, :], soft_ps, row_max[:, :].unsqueeze(2).to_broadcast([P, HB, SEG]),
                                  ALU.subtract).then_inc(shifted_ready, 1)
                dve.wait_ge(lin_done, s.n + 1)
                dve.tensor_reduce(sums[SEG:P, 1, :], lin_ps[SEG:P, :, :], AX.X, ALU.add)
                dve.wait_ge(probs_ready, s.n + 1)
                dve.tensor_reduce(sums[:, 0, :], probs[:, :, :], AX.X, ALU.add).then_inc(sums_ready, 1)
                dve.wait_ge(sums_ready, s.n + 1)
                dve.reciprocal(inv[:, :, :], sums[:, :, :]).then_inc(inv_ready, 1)
                dve.wait_ge(inv_ready, s.n + 1)
                if not s.at(0, 0):
                    dve.wait_ge(t_done, s.n)
                for seg in range(2):
                    rows = slice(seg * SEG, (seg + 1) * SEG)
                    dve.tensor_tensor(weights[rows, :, seg, :], probs[rows, :, :],
                                      inv[rows, 0, :].unsqueeze(2).to_broadcast([SEG, HB, SEG]), ALU.mult)
                dve.tensor_tensor(weights[SEG:P, :, 0, :], lin_ps[SEG:P, :, 0:SEG],
                                  inv[SEG:P, 1, :].unsqueeze(2).to_broadcast([SEG, HB, SEG]), ALU.mult).then_inc(weights_ready, 1)
                if s.looped or s.h > 0:
                    add_memory(s.h - 1, s.n - 1)
                if s.at(1, 0):
                    add_output(0)
                dve.wait_ge(t_done, s.n + 1)
                dve.tensor_copy(weights_t[SEG:P, :, 0:2, :].rearrange("p b g s -> p b (g s)"), t_ps[SEG:P, :, :]).then_inc(wt_ready, 1)
                if not s.at(HALVES - 1, H - 1):
                    sigma_of(s.n + 1)

            def add_memory(h, n):
                for i in range(2):
                    dve.wait_ge(att_ready, n * 2 + i + 1)
                    out = att_of(h, i, 1)
                    last = dve.scalar_tensor_tensor(out=out, in0=att_ps[i][:, :, 2, :], scalar=gate[:, 0, bass.ds(h, 1)],
                                                    in1=out, op0=ALU.mult, op1=ALU.add)
                last.then_inc(memory_added, 1)

            def add_output(half):
                for b in range(HB):
                    dve.wait_ge(out_done, half * HB + b + 1)
                    rows = c.x_sb[:, half * HB + b, :]
                    dve.tensor_tensor(rows, rows, o_ps[b % 2], ALU.add).then_inc(x_added, 1)

            head_steps(dve, step)
            add_memory(H - 1, HALVES * H - 1)
            add_output(HALVES - 1)

        @block.tensor
        def _(pe):
            def transpose_x(half):
                for k in range(KD):
                    pe.wait_ge(xn_ready, (half + 1) * HB)
                    for b in range(HB):
                        last = pe.transpose(c.bank[4 + k][:, b * S:(b + 1) * S],
                                            xn[:, half * HB + b, k * P:(k + 1) * P], c.ident[:, :])
                    last.then_inc(xt_done, 1)

            def split_product(out, left, right, pick_l, pick_r, start=True):
                n = 0
                for k in range(KD):
                    for a, b in ((0, 0), (0, 1), (1, 0)):
                        last = pe.matmul(out, pick_l(left[a], k), pick_r(right[b], k),
                                         start=start and n == 0, stop=n == 3 * KD - 1, skip_group_check=not start)
                        n += 1
                return last

            def project(n, half, slot, free):
                pe.wait_ge(qk_lo_ready, n + 1)
                toks = slice(half * TOK, (half + 1) * TOK)
                for i, out in enumerate((q_ps, k_ps)):
                    if free:
                        pe.wait_ge(qk_ready, n * 2 + i - 1)
                    split_product(out[:, :], (qk_hi, qk_lo), (xt_hi, xt_lo),
                                  lambda w, k: w[:, slot, (i * KD + k) * DK:(i * KD + k + 1) * DK],
                                  lambda t, k: t[:, k, toks]).then_inc(proj_done, 1)

            def project_values(fill, half, group, part, slot):
                pe.wait_ge(wv_lo_ready, group + 1)
                if not (isinstance(fill, int) and fill == 0):
                    pe.wait_ge(v_ready, fill)
                for i in range(2):
                    at = (half * HB + 2 * part + i) * S
                    last = split_product(v_ps[:, i, :], (xt_hi, xt_lo), (wv_hi, wv_lo),
                                         lambda t, k: t[:, k, at:at + S], lambda w, k: w[:, slot, k, :])
                last.then_inc(v_done, 1)

            def soft_scores(n):
                pe.wait_ge(qk_ready, n * 2 + 2)
                pe.matmul(c.bank[2][:, 0:HB * SEG], c.ident_b[:, :], mask[:, :, :], start=True, stop=False,
                          skip_group_check=True)
                for b in range(HB):
                    for seg in range(2):
                        at = slice(seg * SEG, (seg + 1) * SEG)
                        last = pe.matmul(soft_ps[at, b, :], q_sb[:, b, at], k_sb[:, b, at], start=False, stop=True,
                                         skip_group_check=True)
                last.then_inc(soft_done, 1)

            def linear_scores(n):
                pe.wait_ge(sigma_ready, n + 1)
                for b in range(HB):
                    last = pe.matmul(lin_ps[SEG:P, b, :], sigma[:, 0, b, 0:SEG], sigma[:, 1, b, :], start=True, stop=True)
                last.then_inc(lin_done, 1)

            def output(half):
                pe.wait_ge(wo_loaded, 16)
                pe.wait_ge(memory_added, (half + 1) * H)
                for b in range(HB):
                    if b == 1:
                        pe.wait_ge(v_ready, H + 2 if half < HALVES - 1 else HALVES * H)
                    if half * HB + b >= 2:
                        pe.wait_ge(x_added, half * HB + b - 1)
                    for i in range(H):
                        last = pe.matmul(o_ps[b % 2], att[:, b, :, :, :].rearrange("p g h (q c) -> p (g h q) c", c=H)[:, :, i],
                                         wo_sb[:, i, :], start=i == 0, stop=i == H - 1)
                    last.then_inc(out_done, 1)

            pe.wait_ge(consts_ready, 5)
            pe.wait_ge(fills_ready, 4)
            transpose_x(0)
            pe.wait_ge(xt_lo_ready, KD)
            project(0, 0, 0, False)
            for part in range(2):
                project_values(part, 0, 0, part, 0)
            soft_scores(0)
            linear_scores(0)
            transpose_x(1)

            def step(s):
                if not s.at(HALVES - 1, H - 1):
                    next_half = s.half + 1 if s.at(s.half, H - 1) else s.half
                    project(s.n + 1, next_half, 1 - s.member, True)
                pe.wait_ge(weights_ready, s.n + 1)
                for b in range(HB):
                    last = pe.transpose(t_ps[:, b, :], weights[:, b, :, :].rearrange("p g t -> p (g t)"), c.ident[:, :])
                last.then_inc(t_done, 1)
                if s.follows(2):
                    if s.at(0, H - 2):
                        pe.wait_ge(xt_lo_ready, HALVES * KD)
                    if s.at(1, 0):
                        pe.wait_ge(x_added, HB)
                    project_values(s.n + 2, s.half + 1 if s.at(0, H - 2) or s.at(0, H - 1) else s.half,
                                   s.pair + 1, s.member, 1 - s.slot)
                if not s.at(HALVES - 1, H - 1):
                    soft_scores(s.n + 1)
                pe.wait_ge(wt_ready, s.n + 1)
                pe.wait_ge(wt_near_ready, s.n + 1)
                if not s.at(0, 0):
                    pe.wait_ge(memory_added, s.n)
                if s.at(HALVES - 1, H - 2) or s.at(0, 0):
                    pe.wait_ge(v_ready, s.n + 2)
                cols = slice(s.member * DK, (s.member + 1) * DK)
                for b in range(HB):
                    last = pe.matmul(att_ps[b // 2][:, b % 2, :, :], v_sb[:, s.slot, b, cols], weights_t[:, b, :, :],
                                     start=True, stop=True)
                last.then_inc(att_done, 1)
                if not s.at(HALVES - 1, H - 1):
                    linear_scores(s.n + 1)
                if s.at(s.half, H - 1):
                    output(s.half)

            head_steps(pe, step)
    phase.close()

NX, HD, L = 16, 16, 64
CROSS_SCALE = 1.0 / float(HD) ** 0.5
CH = NX // 2
ROWG = 32


def cross_phase(c, ctx_t, wq_t, wkv_t, wout_t):
    nc = c.nc
    phase = ExitStack()

    def sb(name, shape, dt):
        return c.sb(name, shape, dt, phase)

    wq = sb("x_wq", [P, KD, D], F32)
    wkv = sb("x_wkv", [L, 2 * D], F32)
    wout = sb("x_wout", [P, KD, D], F32)
    ctx_in = sb("x_ctx", [L, B, S], F32)
    xn = sb("x_xn", [P, B, D], F32)
    stats = sb("x_stats", [P, B, 6], F32)
    meanvar = sb("x_meanvar", [P, B, 2], F32)
    std = sb("x_std", [P, B], F32)
    rstd = sb("x_rstd", [P, B], F32)
    xn_t = sb("x_xn_t", [P, KD, B * S], F32)
    q_t = sb("x_q_t", [P, KD, B * S], F32)
    k_t = sb("x_k_t", [P, KD, B * S], F32)
    v_aug = sb("x_v_aug", [P, B, NX, HD + 1], F32)
    parity = sb("x_parity", [P, 2], F32)
    q_sel = sb("x_q_sel", [P, 2, KD, S], F32)
    k_sel = sb("x_k_sel", [P, KD, S], F32)
    mask = sb("x_mask", [P, 4, S], BF16)
    row_max = sb("x_row_max", [P, 2, CH], F32)
    shifted = sb("x_shifted", [P, CH, S], F32)
    probs = sb("x_probs", [P, 2, CH, S], F32)
    probs_t = sb("x_probs_t", [P, 2, CH, S], F32)
    inv = sb("x_inv", [P, NX], F32)
    heads = sb("x_heads", [P, NX, HD], F32)
    heads_t = sb("x_heads_t", [P, KD, S], F32)

    s_ps = [c.psum[:, 2 * i * BANK:2 * (i + 1) * BANK].rearrange("p (h t) -> p h t", h=CH) for i in range(2)]
    t_ps = c.psum[:, 4 * BANK:6 * BANK].rearrange("p (h t) -> p h t", h=CH)
    o_ps = c.bank[6][:, 0:NX * (HD + 1)].rearrange("p (h d) -> p h d", h=NX)
    ht_ps = c.bank[7][:, 0:KD * S]
    y_ps = c.bank[7][:, KD * S:KD * S + D]

    sem = c.sem
    w_loaded, consts = sem("xw_loaded"), sem("x_consts")
    ln_chain, var_ready, std_ready, xn_ready = sem("x_ln_chain"), sem("x_var_ready"), sem("x_std_ready"), sem("x_xn_ready")
    kv_done, kv_ready = sem("x_kv_done"), sem("x_kv_ready")
    xt_done, xt_ready = sem("x_xt_done"), sem("x_xt_ready")
    q_done, q_ready, sel_ready = sem("x_q_done"), sem("x_q_ready"), sem("x_sel_ready")
    s_done, max_ready, shifted_ready = sem("x_s_done"), sem("x_max_ready"), sem("x_shifted_ready")
    probs_ready, t_done, t_ready = sem("x_probs_ready"), sem("x_t_done"), sem("x_t_ready")
    pv_done, inv_ready, heads_ready = sem("x_pv_done"), sem("x_inv_ready"), sem("x_heads_ready")
    ht_done, ht_ready, y_done, y_added = sem("x_ht_done"), sem("x_ht_ready"), sem("x_y_done"), sem("x_y_added")

    def chunk_heads(ch):
        return [(r * 4 + k * 2 + odd, 2 * ch + r, k, odd) for r in range(2) for k in range(KD) for odd in range(2)]

    def batches(eng, step):
        step(0, 0)
        step(1, 1)
        with eng.Fori(2, B - 1) as b:
            step(b, None)
        step(B - 1, B - 1)

    with nc.Block() as block:
        @block.sync
        def _(sp):
            sp.dma_start(ctx_in[:, :, :], ctx_t.rearrange("b l s -> l b s")).then_inc(w_loaded, 16)
            sp.dma_start(wkv[:, :], wkv_t).then_inc(w_loaded, 16)
            sp.dma_start(wq[:, :, :], wq_t.rearrange("(k p) n -> p k n", p=P)).then_inc(w_loaded, 16)
            sp.dma_start(wout[:, :, :], wout_t.rearrange("(k p) n -> p k n", p=P)).then_inc(w_loaded, 16)
            c.load_experts(sp)

        @block.gpsimd
        def _(pool):
            pool.memset(mask[:, :, :], 0.0).then_inc(consts, 1)
            pool.memset(v_aug[:, :, :, HD:HD + 1], 1.0).then_inc(consts, 1)
            pool.memset(parity[:, :], 0.0).then_inc(consts, 1)
            pool.wait_ge(consts, 3)
            pool.affine_select(out=mask[:, :, :], in_=mask[:, :, :], compare_op=ALU.is_ge, fill=MASKED, base=0,
                               pattern=[[0, 4], [-1, S]], channel_multiplier=1).then_inc(consts, 1)
            n = 4
            for odd in range(2):
                col = parity[:, odd:odd + 1]
                for start in range(HD * odd, P, 2 * HD):
                    for base, fill in ((start, 1.0), (start + HD, 0.0)):
                        if base < P:
                            pool.wait_ge(consts, n)
                            pool.affine_select(out=col, in_=col, compare_op=ALU.is_gt, fill=fill, base=base,
                                               pattern=[[0, 1]], channel_multiplier=-1).then_inc(consts, 1)
                            n += 1
            c.n_x_consts = n
            pool.wait_ge(consts, n)

        @block.scalar
        def _(act):
            for i in range(4):
                act.wait_ge(kv_done, i + 1)
                act.activation(k_t[:, i // 2, (i % 2) * BANK:(i % 2 + 1) * BANK], c.bank[i][:, :], ACT.Copy).then_inc(kv_ready, 1)
            for i in range(4):
                act.wait_ge(kv_done, 5 + i)
                act.activation(v_aug[:, 2 * i:2 * i + 2, :, 0:HD], c.bank[4 + i][:, :].rearrange("p (b h d) -> p b h d", b=2, h=NX),
                               ACT.Copy).then_inc(kv_ready, 1)
            act.wait_ge(var_ready, 1)
            act.activation(std[:, :], meanvar[:, :, 1], ACT.Sqrt, bias=c.eps[:, :]).then_inc(std_ready, 1)
            for i in range(4):
                act.wait_ge(q_done, i + 1)
                act.activation(q_t[:, i // 2, (i % 2) * BANK:(i % 2 + 1) * BANK], c.bank[4 + i][:, :], ACT.Copy).then_inc(q_ready, 1)

            def step(b, static):
                for ch in range(2):
                    u = 2 * b + ch
                    act.wait_ge(shifted_ready, u + 1)
                    if not static == 0:
                        act.wait_ge(t_done, u - 1)
                    act.activation(probs[:, ch, :, :], shifted[:, :, :], ACT.Exp, scale=CROSS_SCALE).then_inc(probs_ready, 1)
                    act.wait_ge(t_done, u + 1)
                    if not static == 0:
                        act.wait_ge(pv_done, u - 1)
                    act.activation(probs_t[:, ch, :, :], t_ps, ACT.Copy).then_inc(t_ready, 1)
                    if ch == 0 and static != 0:
                        head_columns(b - 1)

            def head_columns(b):
                act.wait_ge(ht_done, b + 1)
                act.activation(heads_t[:, :, :], ht_ps.rearrange("p (k s) -> p k s", k=KD), ACT.Copy).then_inc(ht_ready, 1)

            batches(act, step)
            head_columns(B - 1)

        @block.vector
        def _(dve):
            for b in range(B):
                dve.bn_stats(stats[:, b, :], c.x_sb[:, b, :]).then_inc(ln_chain, 1)
            for b in range(B):
                dve.wait_ge(ln_chain, b + 1)
                last = dve.bn_aggr(meanvar[:, b, :], stats[:, b, :])
            last.then_inc(var_ready, 1)
            dve.wait_ge(std_ready, 1)
            dve.reciprocal(rstd[:, :], std[:, :]).then_inc(ln_chain, 1)
            dve.wait_ge(ln_chain, B + 1)
            for b in range(B):
                dve.tensor_scalar(xn[:, b, :], c.x_sb[:, b, :], meanvar[:, b, 0:1], rstd[:, b:b + 1],
                                  ALU.subtract, ALU.mult).then_inc(xn_ready, 1)
            for i in range(4):
                dve.wait_ge(xt_done, i + 1)
                dve.tensor_copy(xn_t[:, i % 2, (i // 2) * BANK:(i // 2 + 1) * BANK], c.bank[i][:, :]).then_inc(xt_ready, 1)

            def select(b, ch):
                rows = slice(2 * ch * ROWG, 2 * (ch + 1) * ROWG)
                at = bass.ds(b * S, S)
                for odd in range(2):
                    dve.tensor_scalar(q_sel[rows, odd, :, :], q_t[rows, :, at], parity[rows, odd:odd + 1], None, ALU.mult)
                dve.tensor_copy(k_sel[rows, :, :], k_t[rows, :, at]).then_inc(sel_ready, 1)

            dve.wait_ge(q_ready, 4)
            dve.wait_ge(kv_ready, 4)
            dve.wait_ge(consts, c.n_x_consts)
            select(0, 0)
            select(0, 1)

            def step(b, static):
                for ch in range(2):
                    u = 2 * b + ch
                    dve.wait_ge(s_done, u + 1)
                    dve.tensor_reduce(row_max[:, ch, :], s_ps[ch], AX.X, ALU.max).then_inc(max_ready, 1)
                    dve.wait_ge(max_ready, u + 1)
                    if not (static == 0 and ch == 0):
                        dve.wait_ge(probs_ready, u)
                    dve.tensor_tensor(shifted[:, :, :], s_ps[ch], row_max[:, ch, :].unsqueeze(2).to_broadcast([P, CH, S]),
                                      ALU.subtract).then_inc(shifted_ready, 1)
                    if static != B - 1:
                        select(b + 1, ch)
                    if ch == 0 and static != 0:
                        normalise(b - 1)
                    if ch == 1 and static != 0:
                        add_output(b - 1)

            def normalise(b):
                dve.wait_ge(pv_done, 2 * b + 2)
                dve.reciprocal(inv[:, :], o_ps[:, :, HD]).then_inc(inv_ready, 1)
                dve.wait_ge(inv_ready, b + 1)
                dve.tensor_tensor(heads[:, :, :], o_ps[:, :, 0:HD], inv[:, :].unsqueeze(2).to_broadcast([P, NX, HD]),
                                  ALU.mult).then_inc(heads_ready, 1)

            def add_output(b):
                dve.wait_ge(y_done, b + 1)
                rows = c.x_sb[:, bass.ds(b, 1), :].rearrange("p b d -> p (b d)")
                dve.tensor_tensor(rows, rows, y_ps, ALU.add).then_inc(y_added, 1)

            batches(dve, step)
            normalise(B - 1)
            add_output(B - 1)

        @block.tensor
        def _(pe):
            pe.wait_ge(w_loaded, 64)
            for i in range(4):
                pe.matmul(c.bank[i][:, :], wkv[:, (i // 2) * P:(i // 2 + 1) * P],
                          ctx_in[:, (i % 2) * HB:(i % 2 + 1) * HB, :], start=True, stop=True).then_inc(kv_done, 1)
            for i in range(4):
                for b in range(2):
                    last = pe.matmul(c.bank[4 + i][:, b * D:(b + 1) * D], ctx_in[:, 2 * i + b, :], wkv[:, D:2 * D],
                                     start=True, stop=True)
                last.then_inc(kv_done, 1)
            pe.wait_ge(kv_ready, 4)
            for i in range(4):
                half, k = i // 2, i % 2
                pe.wait_ge(xn_ready, (half + 1) * HB)
                for b in range(HB):
                    last = pe.transpose(c.bank[i][:, b * S:(b + 1) * S], xn[:, half * HB + b, k * P:(k + 1) * P], c.ident[:, :])
                last.then_inc(xt_done, 1)
            pe.wait_ge(kv_ready, 8)
            pe.wait_ge(xt_ready, 4)
            for i in range(4):
                for k in range(KD):
                    last = pe.matmul(c.bank[4 + i][:, :], wq[:, k, (i // 2) * P:(i // 2 + 1) * P],
                                     xn_t[:, k, (i % 2) * BANK:(i % 2 + 1) * BANK], start=k == 0, stop=k == KD - 1)
                last.then_inc(q_done, 1)
            pe.wait_ge(q_ready, 4)
            pe.wait_ge(consts, c.n_x_consts)

            def scores(b, ch, first):
                if not first:
                    pe.wait_ge(shifted_ready, 2 * b + ch - 1)
                pe.wait_ge(sel_ready, 2 * b + ch + 1)
                for r in range(2):
                    pe.matmul(c.bank[2 * ch + r][:, :], c.ident_b[:, :], mask[:, :, :], start=True, stop=False,
                              skip_group_check=True)
                for place, group, k, odd in chunk_heads(ch):
                    rows = slice(group * ROWG, (group + 1) * ROWG)
                    last = pe.matmul(s_ps[ch][:, place, :], q_sel[rows, odd, k, :], k_sel[rows, k, :],
                                     start=False, stop=True, skip_group_check=True)
                last.then_inc(s_done, 1)

            def weigh(b, ch):
                pe.wait_ge(t_ready, 2 * b + ch + 1)
                if ch == 0:
                    wait_past(pe, heads_ready, b)
                for place, group, k, odd in chunk_heads(ch):
                    head = k * CH + group * 2 + odd
                    last = pe.matmul(o_ps[:, head, :], probs_t[:, ch, place, :],
                                     v_aug[:, bass.ds(b, 1), head, :].rearrange("p b d -> p (b d)"), start=True, stop=True)
                last.then_inc(pv_done, 1)

            def transpose_weights(b, ch, first):
                pe.wait_ge(probs_ready, 2 * b + ch + 1)
                if not first:
                    pe.wait_ge(t_ready, 2 * b + ch)
                for place in range(CH):
                    last = pe.transpose(t_ps[:, place, :], probs[:, ch, place, :], c.ident[:, :])
                last.then_inc(t_done, 1)

            def transpose_heads(b):
                pe.wait_ge(heads_ready, b + 1)
                wait_past(pe, y_added, b)
                for k in range(KD):
                    last = pe.transpose(ht_ps[:, k * S:(k + 1) * S], heads[:, k * CH:(k + 1) * CH, :].rearrange("p h d -> p (h d)"),
                                        c.ident[:, :])
                last.then_inc(ht_done, 1)

            def project(b):
                pe.wait_ge(ht_ready, b + 1)
                for k in range(KD):
                    last = pe.matmul(y_ps, heads_t[:, k, :], wout[:, k, :], start=k == 0, stop=k == KD - 1)
                last.then_inc(y_done, 1)

            scores(0, 0, True)

            def step(b, static):
                scores(b, 1, static == 0)
                if static != 0:
                    weigh(b - 1, 1)
                transpose_weights(b, 0, static == 0)
                if static != 0:
                    transpose_heads(b - 1)
                if static != B - 1:
                    scores(b + 1, 0, False)
                if static != 0:
                    project(b - 1)
                weigh(b, 0)
                transpose_weights(b, 1, False)

            batches(pe, step)
            weigh(B - 1, 1)
            transpose_heads(B - 1)
            project(B - 1)
    phase.close()

NE, M = 8, 512
KM = M // P
TOPK = 2
PICKS = TOPK * B
TILES = (TOPK * B * S + NE * (P - 1)) // P
EW = 2 * KD * M + KM * D


def expert_phase(c, gate_w, xn_dram, picks_dram, out):
    nc = c.nc
    phase = ExitStack()

    def sb(name, shape, dt):
        return c.sb(name, shape, dt, phase)

    xn = sb("e_xn", [P, B, D], F32)
    stats = sb("e_stats", [P, B, 6], F32)
    meanvar = sb("e_meanvar", [P, B, 2], F32)
    std = sb("e_std", [P, B], F32)
    rstd = sb("e_rstd", [P, B], F32)
    xn_t = sb("e_xn_t", [P, KD, B * S], F32)
    gate = sb("e_gate", [P, KD, NE], F32)
    iota_i = sb("e_iota_i", [P, P + 1], I32)
    iota = sb("e_iota", [P, P + 1], F32)
    tile_start = sb("e_tile_start", [P, TILES + 1], F32)
    spare_row = sb("e_spare_row", [P, TILES], F32)
    ones = sb("e_ones", [P, P], BF16)
    before = sb("e_before", [P, P], BF16)
    ones_f = sb("e_ones_f", [P, NE], F32)
    logits = sb("e_logits", [P, B, NE], F32)
    top = sb("e_top", [P, B, NE], F32)
    top_idx = sb("e_top_idx", [P, B, NE], U32)
    chosen_id = sb("e_chosen_id", [P, B, TOPK], F32)
    chosen = sb("e_chosen", [P, TOPK, B, NE], F32)
    either = sb("e_either", [P, B + 1, NE], BF16)
    diff = sb("e_diff", [P, B], F32)
    ratio = sb("e_ratio", [P, B], F32)
    share = sb("e_share", [P, TOPK, B], F32)
    n_over = sb("e_n_over", [P, NE, NE], F32)
    n_tiles = sb("e_n_tiles", [P, NE], F32)
    end_tile = sb("e_end_tile", [P, NE], F32)
    base = sb("e_base", [P, NE], F32)
    place = sb("e_place", [P, B, NE], F32)
    place_k = sb("e_place_k", [P, TOPK, B, NE], F32)
    row_f = sb("e_row_f", [P, TOPK, B], F32)
    reached = sb("e_reached", [P, PICKS, TILES + 1], F32)
    in_tile = sb("e_in_tile", [P, PICKS, 3, TILES], BF16)
    tile_of = sb("e_tile_of", [P, PICKS], F32)
    at_row = sb("e_at_row", [P, PICKS], F32)
    row_hot = sb("e_row_hot", [P, PICKS, P], BF16)
    pick = sb("e_pick", [P, TILES], F32)
    wrap = sb("e_wrap", [P, TILES], F32)
    spare = sb("e_spare", [P, TILES], F32)
    token_f = sb("e_token_f", [P, TILES], F32)
    token_row = sb("e_token_row", [P, TILES], U32)
    pick_row = sb("e_pick_row", [P, TILES], U32)
    ended = sb("e_ended", [1, TILES, NE], F32)
    owner_f = sb("e_owner_f", [1, TILES], F32)
    owner = sb("e_owner", [1, TILES], I32)
    x_rows = sb("e_x_rows", [P, 2, D], F32)
    x_cols = sb("e_x_cols", [P, 2, KD, P], F32)
    silu = sb("e_silu", [P, 2, M], F32)
    inner = sb("e_inner", [P, 2, M], F32)
    inner_t = sb("e_inner_t", [P, 2, KM, P], F32)
    y_rows = sb("e_y_rows", [P, 2, D], F32)
    picked = sb("e_picked", [P, TOPK, B, D], F32)

    x_ps = c.bank[0][:, 0:KD * P].rearrange("p (k t) -> p k t", k=KD)
    t_ps = c.bank[1].rearrange("p (m t) -> p m t", m=KM)
    y_ps = [c.bank[2][:, 0:D], c.bank[3][:, 0:D]]
    h_ps = [(c.bank[4], c.bank[5]), (c.bank[6], c.bank[7])]
    logit_ps = c.bank[0][:, 0:B * NE].rearrange("p (b e) -> p b e", b=B)
    rank_ps = c.bank[1][:, 0:(B + 1) * NE].rearrange("p (b e) -> p b e", b=B + 1)
    invert_ps = c.bank[2][:, 0:3 * TILES].rearrange("p (q t) -> p q t", q=3)

    sem = c.sem
    gate_loaded, consts, iota_made = sem("e_gate_loaded"), sem("e_consts"), sem("e_iota_made")
    ln_chain, var_ready, std_ready, xn_ready = sem("e_ln_chain"), sem("e_var_ready"), sem("e_std_ready"), sem("e_xn_ready")
    xt_done, xt_ready = sem("e_xt_done"), sem("e_xt_ready")
    logits_done, route, diff_ready, ratio_ready = sem("e_logits_done"), sem("e_route"), sem("e_diff_ready"), sem("e_ratio_ready")
    either_ready, counts_done = sem("e_either_ready"), sem("e_counts_done")
    xn_stored, hot_ready, inverted = sem("e_xn_stored"), sem("e_hot_ready"), sem("e_inverted")
    tokens_known, picks_known, owner_known = sem("e_tokens_known"), sem("e_picks_known"), sem("e_owner_known")
    x_loaded = [sem(f"e_x_loaded{i}") for i in range(2)]
    y_stored = [sem(f"e_y_stored{i}") for i in range(2)]
    x_done, x_ready = sem("e_x_done"), sem("e_x_ready")
    h_done, silu_ready, inner_ready = sem("e_h_done"), sem("e_silu_ready"), sem("e_inner_ready")
    t_done, t_ready, y_done, y_ready = sem("e_t_done"), sem("e_t_ready"), sem("e_y_done"), sem("e_y_ready")
    gathered = [sem(f"e_gathered{i}") for i in range(B)]
    mixed, out_stored = sem("e_mixed"), sem("e_out_stored")

    def tiles(eng, step):
        for slot in range(2):
            step(slot, slot, 0, TILES - 1 - slot)
        with eng.Fori(1, (TILES - 3) // 2) as pair:
            for slot in range(2):
                step(pair * 2 + slot, slot, pair, None)
        for tile in range(TILES - 3, TILES):
            step(tile, tile % 2, tile // 2, TILES - 1 - tile)

    def more(left, n):
        return left is None or left >= n

    with nc.Block() as block:
        @block.sync
        def _(sp):
            sp.dma_start(gate[:, :, :], gate_w.rearrange("(k p) e -> p k e", p=P)).then_inc(gate_loaded, 16)
            sp.wait_ge(xn_ready, B)
            sp.dma_start(xn_dram.rearrange("(b p) d -> p b d", p=P), xn[:, :, :]).then_inc(xn_stored, 16)
            for slot in range(2):
                sp.wait_ge(y_stored[slot], 16 * ((TILES + 1 - slot) // 2))
            picks = picks_dram[0:PICKS * P, :].rearrange("(k b p) d -> p k b d", k=TOPK, b=B)
            for b in range(B):
                sp.dma_start(picked[:, :, b, :], picks[:, :, b, :]).then_inc(gathered[b], 16)
            for b in range(B):
                sp.wait_ge(mixed, TOPK * (b + 1))
                sp.dma_start(out[b], c.x_sb[:, b, :]).then_inc(out_stored, 16)
            sp.wait_ge(out_stored, 16 * B)

        @block.gpsimd
        def _(pool):
            pool.memset(ones[:, :], 1.0).then_inc(consts, 1)
            pool.memset(before[:, :], 1.0).then_inc(consts, 1)
            pool.wait_ge(consts, 2)
            pool.affine_select(out=before[:, :], in_=before[:, :], compare_op=ALU.is_gt, fill=0.0, base=0,
                               pattern=[[1, P]], channel_multiplier=-1).then_inc(consts, 1)
            pool.wait_ge(consts, 3)
            pool.iota(iota_i[:, 0:P], pattern=[[1, P]], base=0, channel_multiplier=0).then_inc(iota_made, 1)
            pool.wait_ge(iota_made, 1)
            pool.iota(iota_i[:, P:P + 1], pattern=[[0, 1]], base=0, channel_multiplier=1).then_inc(iota_made, 1)
            pool.wait_ge(xn_stored, 16)
            pool.wait_ge(tokens_known, 1)

            def load(tile):
                slot = tile % 2
                pool.indirect_dma_start(out=x_rows[:, slot, :], out_offset=None, in_=xn_dram,
                                        in_offset=bass.IndirectOffsetOnAxis(ap=token_row[:, tile:tile + 1], axis=0)
                                        ).then_inc(x_loaded[slot], 16)

            def store(tile):
                slot = tile % 2
                pool.wait_ge(y_ready, tile + 1)
                pool.indirect_dma_start(out=picks_dram, out_offset=bass.IndirectOffsetOnAxis(ap=pick_row[:, tile:tile + 1], axis=0),
                                        in_=y_rows[:, slot, :], in_offset=None).then_inc(y_stored[slot], 16)

            load(0)
            load(1)
            pool.wait_ge(picks_known, 1)
            for tile in range(TILES):
                if tile + 2 < TILES:
                    pool.wait_ge(x_done, tile + 1)
                    load(tile + 2)
                if tile > 0:
                    store(tile - 1)
            store(TILES - 1)

        @block.scalar
        def _(act):
            act.wait_ge(var_ready, 1)
            act.activation(std[:, :], meanvar[:, :, 1], ACT.Sqrt, bias=c.eps[:, :]).then_inc(std_ready, 1)
            act.wait_ge(diff_ready, 1)
            act.activation(ratio[:, :], diff[:, :], ACT.Exp).then_inc(ratio_ready, 1)

            def columns(tile, slot):
                act.wait_ge(x_done, tile + 1)
                act.activation(x_cols[:, slot, :, :], x_ps, ACT.Copy).then_inc(x_ready, 1)

            def silu_of(tile, slot):
                act.wait_ge(h_done, tile * 2 + 1)
                act.activation(silu[:, slot, :], h_ps[slot][0], ACT.Silu).then_inc(silu_ready, 1)

            columns(0, 0)
            columns(1, 1)
            silu_of(0, 0)

            def step(tile, slot, pair, left):
                act.wait_ge(t_done, tile + 1)
                act.activation(inner_t[:, slot, :, :], t_ps, ACT.Copy).then_inc(t_ready, 1)
                if more(left, 2):
                    columns(tile + 2, slot)
                if more(left, 1):
                    silu_of(tile + 1, 1 - slot)

            tiles(act, step)

        @block.vector
        def _(dve):
            for b in range(B):
                dve.bn_stats(stats[:, b, :], c.x_sb[:, b, :]).then_inc(ln_chain, 1)
            for b in range(B):
                dve.wait_ge(ln_chain, b + 1)
                last = dve.bn_aggr(meanvar[:, b, :], stats[:, b, :])
            last.then_inc(var_ready, 1)
            dve.wait_ge(std_ready, 1)
            dve.reciprocal(rstd[:, :], std[:, :]).then_inc(ln_chain, 1)
            dve.wait_ge(ln_chain, B + 1)
            for b in range(B):
                dve.tensor_scalar(xn[:, b, :], c.x_sb[:, b, :], meanvar[:, b, 0:1], rstd[:, b:b + 1],
                                  ALU.subtract, ALU.mult).then_inc(xn_ready, 1)
            for i in range(4):
                dve.wait_ge(xt_done, i + 1)
                dve.tensor_copy(xn_t[:, i % 2, (i // 2) * BANK:(i // 2 + 1) * BANK], c.bank[4 + i][:, :]).then_inc(xt_ready, 1)

            n_route = [0]

            def chained(instruction):
                n_route[0] += 1
                instruction.then_inc(route, 1)
                dve.wait_ge(route, n_route[0])

            dve.wait_ge(iota_made, 2)
            dve.memset(ones_f[:, :], 1.0)
            dve.memset(either[:, B, :], 0.0)
            chained(dve.tensor_copy(iota[:, :], iota_i[:, :]))
            chained(dve.tensor_scalar(tile_start[:, :], iota[:, 0:TILES + 1], float(P), None, ALU.mult))
            dve.tensor_scalar(spare_row[:, :], tile_start[:, 0:TILES], iota[:, P:P + 1], float(PICKS * P), ALU.add, ALU.add)
            dve.wait_ge(logits_done, 1)
            chained(dve.tensor_copy(logits[:, :, :], logit_ps))
            for b in range(B):
                last = dve.max(top[:, b, :], logits[:, b, :])
            chained(last)
            for b in range(B):
                last = dve.max_index(top_idx[:, b, :], top[:, b, :], logits[:, b, :])
            chained(last)
            dve.tensor_tensor(diff[:, :], top[:, :, 1], top[:, :, 0], ALU.subtract).then_inc(diff_ready, 1)
            chained(dve.tensor_copy(chosen_id[:, :, :], top_idx[:, :, 0:TOPK]))
            ids = iota[:, 0:NE].unsqueeze(1).to_broadcast([P, B, NE])
            for k in range(TOPK):
                last = dve.tensor_tensor(chosen[:, k, :, :], ids, chosen_id[:, :, k].unsqueeze(2).to_broadcast([P, B, NE]), ALU.is_equal)
            chained(last)
            dve.tensor_tensor(either[:, 0:B, :], chosen[:, 0, :, :], chosen[:, 1, :, :], ALU.add).then_inc(either_ready, 1)
            dve.wait_ge(ratio_ready, 1)
            chained(dve.tensor_scalar(share[:, 1, :], ratio[:, :], 1.0, None, ALU.add))
            chained(dve.reciprocal(share[:, 0, :], share[:, 1, :]))
            chained(dve.tensor_tensor(share[:, 1, :], share[:, 0, :], ratio[:, :], ALU.mult))
            dve.wait_ge(counts_done, 1)
            chained(dve.tensor_tensor(n_over[:, :, :], rank_ps[:, B, :].unsqueeze(2).to_broadcast([P, NE, NE]),
                                      tile_start[:, 0:NE].unsqueeze(1).to_broadcast([P, NE, NE]), ALU.is_gt))
            chained(dve.tensor_reduce(n_tiles[:, :], n_over[:, :, :], AX.X, ALU.add))
            chained(dve.tensor_tensor_scan(end_tile[:, :], ones_f[:, :], n_tiles[:, :], 0.0, ALU.mult, ALU.add))
            chained(dve.tensor_tensor(base[:, :], end_tile[:, :], n_tiles[:, :], ALU.subtract))
            chained(dve.tensor_scalar(base[:, :], base[:, :], float(P), None, ALU.mult))
            chained(dve.tensor_tensor(place[:, :, :], rank_ps[:, 0:B, :], base[:, :].unsqueeze(1).to_broadcast([P, B, NE]), ALU.add))
            for k in range(TOPK):
                last = dve.tensor_tensor(place_k[:, k, :, :], chosen[:, k, :, :], place[:, :, :], ALU.mult)
            chained(last)
            chained(dve.tensor_reduce(row_f[:, :, :], place_k[:, :, :, :], AX.X, ALU.add))
            rows = row_f[:, :, :].rearrange("p k b -> p (k b)")
            chained(dve.tensor_tensor(reached[:, :, :], rows.unsqueeze(2).to_broadcast([P, PICKS, TILES + 1]),
                                      tile_start[:, :].unsqueeze(1).to_broadcast([P, PICKS, TILES + 1]), ALU.is_ge))
            chained(dve.tensor_reduce(tile_of[:, :], reached[:, :, 1:TILES + 1], AX.X, ALU.add))
            chained(dve.scalar_tensor_tensor(out=at_row[:, :], in0=tile_of[:, :], scalar=-float(P), in1=rows,
                                             op0=ALU.mult, op1=ALU.add))
            chained(dve.tensor_tensor(in_tile[:, :, 2, :], reached[:, :, 0:TILES], reached[:, :, 1:TILES + 1], ALU.subtract))
            dve.tensor_scalar(in_tile[:, :, 0, :], in_tile[:, :, 2, :], iota[:, P:P + 1], None, ALU.mult)
            dve.tensor_tensor(in_tile[:, :, 1, :], in_tile[:, :, 2, :], iota[:, 0:PICKS].unsqueeze(2).to_broadcast([P, PICKS, TILES]),
                              ALU.mult)
            for k in range(TOPK):
                some = slice(k * B, (k + 1) * B)
                dve.tensor_tensor(row_hot[:, some, :], iota[:, 0:P].unsqueeze(1).to_broadcast([P, B, P]),
                                  at_row[:, some].unsqueeze(2).to_broadcast([P, B, P]), ALU.is_equal).then_inc(hot_ready, 1)
            chained(dve.tensor_tensor(ended[:, :, :], end_tile[0:1, :].unsqueeze(1).to_broadcast([1, TILES, NE]),
                                      iota[0:1, 0:TILES].unsqueeze(2).to_broadcast([1, TILES, NE]), ALU.is_le))
            chained(dve.tensor_reduce(owner_f[:, :], ended[:, :, :], AX.X, ALU.add))
            chained(dve.tensor_scalar(owner_f[:, :], owner_f[:, :], float(NE - 1), float(EW), ALU.min, ALU.mult))
            dve.tensor_copy(owner[:, :], owner_f[:, :]).then_inc(owner_known, 1)
            dve.wait_ge(inverted, 1)
            chained(dve.tensor_scalar(wrap[:, :], invert_ps[:, 1, :], float(B), -float(B * S), ALU.is_ge, ALU.mult))
            chained(dve.tensor_scalar(pick[:, :], invert_ps[:, 1, :], float(P), None, ALU.mult))
            chained(dve.tensor_tensor(pick[:, :], pick[:, :], invert_ps[:, 0, :], ALU.add))
            chained(dve.tensor_tensor(token_f[:, :], pick[:, :], wrap[:, :], ALU.add))
            dve.tensor_copy(token_row[:, :], token_f[:, :]).then_inc(tokens_known, 1)
            chained(dve.tensor_scalar(spare[:, :], invert_ps[:, 2, :], -1.0, 1.0, ALU.mult, ALU.add))
            chained(dve.tensor_tensor(spare[:, :], spare[:, :], spare_row[:, :], ALU.mult))
            chained(dve.tensor_tensor(spare[:, :], spare[:, :], pick[:, :], ALU.add))
            dve.tensor_copy(pick_row[:, :], spare[:, :]).then_inc(picks_known, 1)

            def gated(tile, slot):
                dve.wait_ge(h_done, tile * 2 + 2)
                dve.wait_ge(silu_ready, tile + 1)
                dve.tensor_tensor(inner[:, slot, :], h_ps[slot][1], silu[:, slot, :], ALU.mult).then_inc(inner_ready, 1)

            gated(0, 0)

            def step(tile, slot, pair, left):
                if more(left, 1):
                    gated(tile + 1, 1 - slot)
                dve.wait_ge(y_done, tile + 1)
                wait_past(dve, y_stored[slot], pair * 16)
                dve.tensor_copy(y_rows[:, slot, :], y_ps[slot]).then_inc(y_ready, 1)

            tiles(dve, step)
            for b in range(B):
                dve.wait_ge(gathered[b], 16)
                for k in range(TOPK):
                    if k:
                        dve.wait_ge(mixed, TOPK * b + k)
                    dve.scalar_tensor_tensor(out=c.x_sb[:, b, :], in0=picked[:, k, b, :], scalar=share[:, k, b:b + 1],
                                             in1=c.x_sb[:, b, :], op0=ALU.mult, op1=ALU.add).then_inc(mixed, 1)

        @block.tensor
        def _(pe):
            for i in range(4):
                half, k = i // 2, i % 2
                pe.wait_ge(xn_ready, (half + 1) * HB)
                for b in range(HB):
                    last = pe.transpose(c.bank[4 + i][:, b * S:(b + 1) * S], xn[:, half * HB + b, k * P:(k + 1) * P], c.ident[:, :])
                last.then_inc(xt_done, 1)
            pe.wait_ge(gate_loaded, 16)
            pe.wait_ge(xt_ready, 4)
            for b in range(B):
                for k in range(KD):
                    last = pe.matmul(logit_ps[:, b, :], xn_t[:, k, b * S:(b + 1) * S], gate[:, k, :], start=k == 0, stop=k == KD - 1)
            last.then_inc(logits_done, 1)
            pe.wait_ge(consts, 3)
            pe.wait_ge(either_ready, 1)
            pe.matmul(rank_ps, before[:, :], either[:, :, :], start=True, stop=False, skip_group_check=True)
            for b in range(B):
                last = pe.matmul(rank_ps[:, b + 1:B + 1, :], ones[:, :], either[:, b:b + 1, :].to_broadcast([P, B - b, NE]),
                                 start=False, stop=b == B - 1, skip_group_check=True)
            last.then_inc(counts_done, 1)
            for n in range(PICKS):
                if n % B == 0:
                    pe.wait_ge(hot_ready, n // B + 1)
                last = pe.matmul(invert_ps, row_hot[:, n, :], in_tile[:, n, :, :], start=n == 0, stop=n == PICKS - 1)
            last.then_inc(inverted, 1)

            def expert_of(tile):
                return pe.value_load(owner[0:1, bass.ds(tile, 1)], min_val=0, max_val=(NE - 1) * EW)

            def columns(tile, slot, pair, first):
                pe.wait_ge(x_loaded[slot], pair * 16 + 16)
                if not first:
                    pe.wait_ge(x_ready, tile)
                for k in range(KD):
                    last = pe.transpose(x_ps[:, k, :], x_rows[:, slot, k * P:(k + 1) * P], c.ident[:, :])
                last.then_inc(x_done, 1)

            def expand(tile, slot, i, at):
                if i == 0:
                    pe.wait_ge(x_ready, tile + 1)
                for k in range(KD):
                    last = pe.matmul(h_ps[slot][i], x_cols[:, slot, k, :], c.expert_w[:, bass.ds(at + (i * KD + k) * M, M)],
                                     start=k == 0, stop=k == KD - 1)
                last.then_inc(h_done, 1)

            def transpose_inner(tile, slot):
                pe.wait_ge(inner_ready, tile + 1)
                wait_past(pe, t_ready, tile)
                for m in range(KM):
                    last = pe.transpose(t_ps[:, m, :], inner[:, slot, m * P:(m + 1) * P], c.ident[:, :])
                last.then_inc(t_done, 1)

            def reduce(tile, slot, pair, at):
                pe.wait_ge(t_ready, tile + 1)
                wait_past(pe, y_ready, pair * 2)
                for m in range(KM):
                    last = pe.matmul(y_ps[slot], inner_t[:, slot, m, :], c.expert_w[:, bass.ds(at + 2 * KD * M + m * D, D)],
                                     start=m == 0, stop=m == KM - 1)
                last.then_inc(y_done, 1)

            pe.wait_ge(owner_known, 1)
            pe.wait_ge(picks_known, 1)
            pe.wait_ge(c.experts_loaded, 16 * NE)
            columns(0, 0, 0, True)
            at = expert_of(0)
            for i in range(2):
                expand(0, 0, i, at)
            columns(1, 1, 0, False)

            def step(tile, slot, pair, left):
                if more(left, 1):
                    at_next = expert_of(tile + 1)
                    expand(tile + 1, 1 - slot, 0, at_next)
                transpose_inner(tile, slot)
                if more(left, 2):
                    columns(tile + 2, slot, pair + 1, False)
                if more(left, 1):
                    expand(tile + 1, 1 - slot, 1, at_next)
                reduce(tile, slot, pair, expert_of(tile))

            tiles(pe, step)
    phase.close()


def decoder_layer(nc, x, betas_t, wqk, wv, wo, ctx_t, xwq_t, xwkv_t, xwout_t, gate_w, expert_w, out):
    xn_dram = nc.dram_tensor("xn_dram", (B * S, D), F32, kind="Internal").ap()
    picks_dram = nc.dram_tensor("picks_dram", ((PICKS + TILES) * P, D), F32, kind="Internal").ap()
    with ExitStack() as ctx:
        c = Core(nc, ctx)
        c.experts_loaded = c.sem("experts_loaded")
        attention_phase(c, x, betas_t, wqk, wv, wo)
        c.expert_w = c.sb("expert_w", [P, NE * EW], F32)

        def load_experts(sp):
            for e in range(NE):
                sp.dma_start(c.expert_w[:, e * EW:(e + 1) * EW], expert_w[e]).then_inc(c.experts_loaded, 16)

        c.load_experts = load_experts
        cross_phase(c, ctx_t, xwq_t, xwkv_t, xwout_t)
        expert_phase(c, gate_w, xn_dram, picks_dram, out)


def kernel(x, ctx_512, L0_attn_Wq, L0_attn_Wk, L0_attn_Wv, L0_attn_Wo, L0_attn_betas, L0_xattn_Wq, L0_xattn_Wkv_expand,
           L0_xattn_Wout, L0_ffn_gate_kernel, L0_ffn_w0_kernel, L0_ffn_w1_kernel, L0_ffn_wo_kernel):
    import numpy as np
    import concourse.bacc as bacc
    from concourse.bass_utils import run_bass_kernel_spmd

    def laid(a):
        return np.ascontiguousarray(a)

    def rows(w):
        w = np.asarray(w)
        lead = w.shape[:-2]
        w = w.reshape(*lead, w.shape[-2] // P, P, w.shape[-1])
        return np.moveaxis(w, -3, -2).reshape(*lead, P, -1)

    def by_head(w, n):
        w = np.asarray(w)
        return np.moveaxis(w.reshape(w.shape[0], H // n, n * DK), 1, 0)

    arrays = {
        "x": laid(x),
        "betas_t": laid(np.asarray(L0_attn_betas).reshape(H, DK).T),
        "wqk": laid(np.concatenate([rows(by_head(L0_attn_Wq, 1)), rows(by_head(L0_attn_Wk, 1))], axis=-1)),
        "wv": laid(rows(by_head(L0_attn_Wv, GH)[[*range(NG), 0]])),
        "wo": laid(np.asarray(L0_attn_Wo).reshape(H, DK, D)),
        "ctx_t": laid(np.asarray(ctx_512).transpose(0, 2, 1)),
        "xwq_t": laid(np.asarray(L0_xattn_Wq).T),
        "xwkv_t": laid(np.asarray(L0_xattn_Wkv_expand).T),
        "xwout_t": laid(np.asarray(L0_xattn_Wout).T),
        "gate_w": laid(L0_ffn_gate_kernel),
        "expert_w": laid(np.concatenate([rows(L0_ffn_w0_kernel), rows(L0_ffn_w1_kernel), rows(L0_ffn_wo_kernel)], axis=-1)),
    }
    nc = bacc.Bacc("TRN2", target_bir_lowering=False, num_devices=1)
    args = [nc.dram_tensor(f"in_{name}", a.shape, mybir.dt.from_np(a.dtype), kind="ExternalInput").ap() for name, a in arrays.items()]
    out = nc.dram_tensor("out_0", (B, S, D), F32, kind="ExternalOutput").ap()
    decoder_layer(nc, *args, out)
    r = run_bass_kernel_spmd(nc, [{f"in_{name}": a for name, a in arrays.items()}], core_ids=[0])
    return r.results[0]["out_0"]
```

```python
from contextlib import ExitStack

import concourse.bass as bass
from concourse import mybir

F32 = mybir.dt.float32
F32R = mybir.dt.float32r
BF16 = mybir.dt.bfloat16
I32 = mybir.dt.int32
U32 = mybir.dt.uint32
ALU = mybir.AluOpType
ACT = mybir.ActivationFunctionType
AX = mybir.AxisListType

P = 128
BANK = 512
B, S, D = 8, 128, 256
KD = D // P
H, DK, SEG = 16, 128, 64
L = 64
NE = 8
HB = 4
HALVES = B // HB
TOK = HB * S
TURN = 4
GH = 2
NG = H // GH
LN_EPS = 1e-5
KV_BANKS = (0, 1, 6)
MASKED = -3.0e38
ATT_SCALE = 1.0 / float(DK) ** 0.5


class Core:

    def __init__(self, nc, ctx):
        self.nc, self.ctx = nc, ctx
        self.psum = ctx.enter_context(nc.psum_tensor("psum", [P, 8 * BANK], F32))
        self.bank = [self.psum[:, i * BANK:(i + 1) * BANK] for i in range(8)]
        self.x_sb = self.sb("x_sb", [P, B, D], F32)
        self.ident = self.sb("ident", [P, P], F32)
        self.ident_b = self.sb("ident_b", [P, P], BF16)
        self.eps = self.sb("eps", [P, 1], F32)
        self.xn = self.sb("xn", [P, B, D], F32)
        self.stats = self.sb("ln_stats", [P, B, 6], F32)
        self.meanvar = self.sb("ln_meanvar", [P, B, 2], F32)
        self.std = self.sb("ln_std", [P, B], F32)
        self.rstd = self.sb("ln_rstd", [P, B], F32)
        self.wq = self.sb("x_wq", [P, KD, D], F32)
        self.wout = self.sb("x_wout", [P, KD, D], F32)
        self.k_t = self.sb("x_k_t", [P, KD, B * S], F32)
        self.v = self.sb("x_v", [P, B, D], F32)
        self.gate = self.sb("e_gate", [P, KD, NE], F32)
        self.logits = self.sb("e_logits", [P, B, NE], F32)

    def sb(self, name, shape, dt, ctx=None):
        return (ctx or self.ctx).enter_context(self.nc.sbuf_tensor(name, shape, dt))

    def sem(self, name):
        return self.ctx.enter_context(self.nc.semaphore(name))


def wait_past(eng, sem, value):
    if not isinstance(value, int) or value > 0:
        eng.wait_ge(sem, value)


class Head:

    def __init__(self, half, first, loop=None):
        turns = loop if loop is not None else 0
        self.half, self.j, self.looped = half, first % TURN, loop is not None
        self.member, self.slot = self.j % GH, self.j // GH
        self.h = turns * TURN + first
        self.n = turns * TURN + (first + half * H)
        self.pair = turns * (TURN // GH) + (first + half * H) // GH
        self.quad = turns + (first + half * H) // TURN

    def at(self, half, h):
        return not self.looped and self.half == half and self.h == h

    def follows(self, n):
        return self.looped or self.half < HALVES - 1 or self.h + n < H

    def next_pair(self, n):
        at = self.pair - self.half * NG + n
        return at if self.looped else at % NG


def head_steps(eng, step):
    for half in range(HALVES):
        step(Head(half, 0))
        with eng.Fori(0, H // TURN - 1) as turn:
            for first in range(1, 1 + TURN):
                step(Head(half, first, turn))
        for h in range(H - 3, H):
            step(Head(half, h))


def attention_phase(c, x, betas_t, wqk, wv, wo, ctx_t, xwq_t, xwkv_t, xwout_t, gate_w):
    nc = c.nc
    phase = ExitStack()

    def sb(name, shape, dt):
        return c.sb(name, shape, dt, phase)

    ctx_in = sb("a_ctx", [L, B, S], F32)
    wkv = sb("a_wkv", [L, 2 * D], F32)
    xt_hi = sb("a_xt_hi", [P, KD, B * S], F32R)
    xt_lo = sb("a_xt_lo", [P, KD, B * S], F32R)
    qk_raw = sb("a_qk_raw", [P, 2, 2 * KD * DK], F32)
    qk_hi = sb("a_qk_hi", [P, 2, 2 * KD * DK], F32R)
    qk_lo = sb("a_qk_lo", [P, 2, 2 * KD * DK], F32R)
    wo_hi = sb("a_wo_hi", [P, H, D], F32R)
    wo_lo = sb("a_wo_lo", [P, H, D], F32R)
    wo_raw = [t[:, :, :].rearrange("p a n -> p (a n)") for t in (c.k_t, c.v)]
    att_hi = sb("a_att_hi", [P, 2, 2 * H * SEG], F32R)
    att_lo = sb("a_att_lo", [P, 2, 2 * H * SEG], F32R)
    wv_raw = sb("a_wv_raw", [P, 2, KD, GH * DK], F32)
    wv_hi = sb("a_wv_hi", [P, 2, KD, GH * DK], F32R)
    wv_lo = sb("a_wv_lo", [P, 2, KD, GH * DK], F32R)
    gate_in = sb("a_gate_in", [DK, H], F32)
    gate_exp = sb("a_gate_exp", [DK, 2, H], F32)
    gate = sb("a_gate", [DK, 2, H], F32)
    v_sb = sb("a_v", [P, 2, HB, GH * DK], F32)
    qk = sb("a_qk", [P, 2 * TOK + SEG], F32)
    relu_neg = sb("a_relu_neg", [P, 2, HB, SEG], F32)
    exp_neg = sb("a_exp_neg", [P, 2, HB, SEG], F32)
    sigma = sb("a_sigma", [P, 2, HB, SEG + 1], F32)
    row_max = sb("a_row_max", [P, HB], F32)
    shifted = sb("a_shifted", [P, HB, SEG], F32)
    probs = sb("a_probs", [P, HB, SEG], F32)
    sums = sb("a_sums", [P, 2, HB], F32)
    inv = sb("a_inv", [P, 2, HB], F32)
    weights = sb("a_weights", [P, HB, 2, SEG], F32)
    weights_t = sb("a_weights_t", [P, HB, 3, SEG], F32)
    att = sb("a_att", [P, HB, 2, H, SEG], F32)
    mask = sb("a_mask", [P, HB, SEG], BF16)

    q_sb = qk[:, 0:TOK].rearrange("p (b t) -> p b t", b=HB)
    k_sb = qk[:, TOK + SEG:2 * TOK + SEG].rearrange("p (b t) -> p b t", b=HB)
    linear_in = qk[:, SEG:2 * TOK + SEG].rearrange("p (a b g t) -> p a b g t", a=2, b=HB, g=2)[:, :, :, 0, :]
    q_ps, k_ps = c.bank[0], c.bank[1]
    soft_ps = c.bank[2][:, 0:HB * SEG].rearrange("p (b t) -> p b t", b=HB)
    lin_ps = c.bank[3][:, 0:HB * (SEG + 1)].rearrange("p (b t) -> p b t", b=HB)
    t_ps = c.bank[4][:, :].rearrange("p (b s) -> p b s", b=HB)
    att_ps = [c.bank[i][:, 0:2 * 3 * SEG].rearrange("p (b g s) -> p b g s", b=2, g=3) for i in (5, 7)]
    v_ps = c.bank[6].rearrange("p (b n) -> p b n", b=2)
    o_ps = [c.bank[7][:, 0:D], c.bank[6][:, 0:D]]

    sem = c.sem
    x_loaded = [sem(f"x_loaded{i}") for i in range(HALVES)]
    gate_loaded, gate_exped, gate_made = (sem(f"gate_{s}") for s in ("loaded", "exped", "made"))
    ident_zeroed, consts_ready, fills_ready = sem("ident_zeroed"), sem("consts_ready"), sem("fills_ready")
    table_ready = sem("table_ready")
    wo_hi_ready, wo_lo_ready = sem("wo_hi_ready"), sem("wo_lo_ready")
    att_hi_ready, att_hi_rest, att_lo_ready = sem("att_hi_ready"), sem("att_hi_rest"), sem("att_lo_ready")
    ln_chain, var_ready, std_ready, xn_ready = sem("ln_chain"), sem("var_ready"), sem("std_ready"), sem("xn_ready")
    xt_done, xt_hi_ready, xt_lo_ready = sem("xt_done"), sem("xt_hi_ready"), sem("xt_lo_ready")
    qk_loaded = [sem(f"qk_loaded{i}") for i in range(2)]
    wo_loaded, kv_loaded, cross_loaded = sem("wo_loaded"), sem("xkv_loaded"), sem("xw_loaded")
    kv_done, kv_copied = sem("xkv_done"), sem("xkv_copied")
    var2_ready, std2_ready, ln2_chain = sem("var2_ready"), sem("std2_ready"), sem("ln2_chain")
    wv_loaded = [sem(f"wv_loaded{i}") for i in range(2)]
    qk_hi_ready, qk_lo_ready = sem("qk_hi_ready"), sem("qk_lo_ready")
    wv_hi_ready, wv_lo_ready = sem("wv_hi_ready"), sem("wv_lo_ready")
    proj_done, qk_ready = sem("proj_done"), sem("qk_ready")
    relu_ready, expneg_ready, sigma_ready = sem("relu_ready"), sem("expneg_ready"), sem("sigma_ready")
    soft_done, lin_done = sem("soft_done"), sem("lin_done")
    max_ready, shifted_ready, probs_ready = sem("max_ready"), sem("shifted_ready"), sem("probs_ready")
    sums_ready, inv_ready, weights_ready = sem("sums_ready"), sem("inv_ready"), sem("weights_ready")
    t_done, wt_ready, wt_near_ready = sem("t_done"), sem("wt_ready"), sem("wt_near_ready")
    att_done, att_ready, memory_added = sem("att_done"), sem("att_ready"), sem("memory_added")
    v_done, v_ready = sem("v_done"), sem("v_ready")
    out_done, x_added = sem("out_done"), sem("x_added")

    def wo_quarter(q):
        flat = slice(q * (H // 4) * D, (q + 1) * (H // 4) * D)
        hi, lo = (t[:, :, :].rearrange("p h n -> p (h n)")[:, flat] for t in (wo_hi, wo_lo))
        return wo_raw[q // 2][:, (q % 2) * (H // 4) * D:(q % 2 + 1) * (H // 4) * D], hi, lo

    def quarter_at(s):
        return None if s.looped or s.half > 0 else (0, H - 3, H - 2, H - 1).index(s.h)

    def batch_of_att(b):
        return att[:, b % HB, :, :, :].rearrange("p g h s -> p (g h s)")

    def att_of(h, i, seg):
        return att[:, 2 * i:2 * i + 2, seg, bass.ds(h, 1), :].rearrange("p b h s -> p (h b) s")

    with nc.Block() as block:
        @block.sync
        def _(sp):
            xv = x.rearrange("b s d -> s b d")

            def load_qk(h, slot):
                sp.dma_start(qk_raw[:, slot, :], wqk[bass.ds(h, 1)].rearrange("a p n -> (a p) n")).then_inc(qk_loaded[slot], 16)

            def load_wv(g, slot):
                sp.dma_start(wv_raw[:, slot, :, :], wv[bass.ds(g, 1)].rearrange("a p (k n) -> (a p) k n", k=KD)).then_inc(wv_loaded[slot], 16)

            sp.dma_start(c.x_sb[:, 0:HB, :], xv[:, 0:HB, :]).then_inc(x_loaded[0], 16)
            sp.dma_start(c.x_sb[:, HB:B, :], xv[:, HB:B, :]).then_inc(x_loaded[1], 16)
            load_qk(0, 0)
            load_wv(0, 0)
            load_qk(1, 1)
            load_wv(1, 1)
            for i in range(2):
                sp.dma_start(wo_raw[i].rearrange("p (h n) -> p h n", n=D),
                             wo[i * (H // 2):(i + 1) * (H // 2)].rearrange("h v n -> v h n")).then_inc(wo_loaded, 16)
            sp.dma_start(c.wq[:, :, :], xwq_t.rearrange("(k p) n -> p k n", p=P)).then_inc(cross_loaded, 16)
            sp.dma_start(c.wout[:, :, :], xwout_t.rearrange("(k p) n -> p k n", p=P)).then_inc(cross_loaded, 16)
            sp.dma_start(c.gate[:, :, :], gate_w.rearrange("(k p) e -> p k e", p=P)).then_inc(cross_loaded, 16)

            def step(s):
                if s.follows(2):
                    ahead = s.h + 2 if s.looped else (s.h + 2) % H
                    sp.wait_ge(qk_lo_ready, s.n + 1)
                    load_qk(ahead, s.j % 2)
                if s.member == 0 and s.follows(4):
                    sp.wait_ge(wv_lo_ready, s.pair + 1)
                    load_wv(s.next_pair(2), s.slot)

            head_steps(sp, step)
            sp.wait_ge(cross_loaded, 48)

        @block.gpsimd
        def _(pool):
            pool.dma_start(gate_in[:, :], betas_t).then_inc(gate_loaded, 16)
            pool.memset(c.ident[:, :], 0.0).then_inc(ident_zeroed, 1)
            pool.memset(c.ident_b[:, :], 0.0).then_inc(ident_zeroed, 1)
            pool.memset(mask[:, :, :], 0.0).then_inc(ident_zeroed, 1)
            pool.memset(c.eps[:, :], LN_EPS).then_inc(consts_ready, 1)
            pool.wait_ge(ident_zeroed, 3)
            for m in (c.ident, c.ident_b):
                pool.affine_select(out=m[:, :], in_=m[:, :], compare_op=ALU.not_equal, fill=1.0, base=0,
                                   pattern=[[-1, P]], channel_multiplier=1).then_inc(consts_ready, 1)
            for seg in range(2):
                pool.wait_ge(consts_ready, 3 + seg)
                rows = mask[seg * SEG:(seg + 1) * SEG, :, :]
                pool.affine_select(out=rows, in_=rows, compare_op=ALU.is_ge, fill=MASKED, base=0,
                                   pattern=[[0, HB], [-1, SEG]], channel_multiplier=1).then_inc(consts_ready, 1)
            pool.wait_ge(consts_ready, 5)
            def split_qk(n, slot):
                pool.wait_ge(qk_hi_ready, n + 1)
                pool.tensor_tensor(qk_lo[:, slot, :], qk_raw[:, slot, :], qk_hi[:, slot, :], ALU.subtract).then_inc(qk_lo_ready, 1)

            def split_wv(group, slot):
                pool.wait_ge(wv_hi_ready, group + 1)
                pool.tensor_tensor(wv_lo[:, slot, :, :], wv_raw[:, slot, :, :], wv_hi[:, slot, :, :],
                                   ALU.subtract).then_inc(wv_lo_ready, 1)

            split_qk(0, 0)
            split_wv(0, 0)
            split_qk(1, 1)
            split_wv(1, 1)

            def step(s):
                if s.follows(2):
                    split_qk(s.n + 2, s.member)
                if s.member == 1 and s.follows(3):
                    split_wv(s.pair + 2, s.slot)
                if quarter_at(s) is not None:
                    q = quarter_at(s)
                    raw, hi, lo = wo_quarter(q)
                    pool.wait_ge(wo_hi_ready, q + 1)
                    pool.tensor_tensor(lo, raw, hi, ALU.subtract).then_inc(wo_lo_ready, 1)

            head_steps(pool, step)

        @block.scalar
        def _(act):
            act.dma_start(wkv[:, :], xwkv_t).then_inc(kv_loaded, 16)
            act.dma_start(ctx_in[:, :, :], ctx_t.rearrange("b l s -> l b s")).then_inc(kv_loaded, 16)
            def std_of(half):
                some = slice(half * HB, (half + 1) * HB)
                act.wait_ge(var_ready, half + 1)
                act.activation(c.std[:, some], c.meanvar[:, some, 1], ACT.Sqrt, bias=c.eps[:, :]).then_inc(std_ready, 1)

            act.wait_ge(consts_ready, 1)
            act.activation(c.std[:, 0:1], c.eps[:, :], ACT.Sqrt).then_inc(table_ready, 1)
            act.wait_ge(table_ready, 1)
            std_of(0)

            def split_qk(n, pair, slot):
                act.wait_ge(qk_loaded[slot], pair * 16 + 16)
                act.activation(qk_hi[:, slot, :], qk_raw[:, slot, :], ACT.Copy).then_inc(qk_hi_ready, 1)

            def split_wv(turn_pair, slot):
                act.wait_ge(wv_loaded[slot], turn_pair * 16 + 16)
                act.activation(wv_hi[:, slot, :, :], wv_raw[:, slot, :, :], ACT.Copy).then_inc(wv_hi_ready, 1)

            def near_weights(n):
                act.wait_ge(t_done, n + 1)
                act.activation(weights_t[0:SEG, :, 0:3:2, :], t_ps[0:SEG, :, :].rearrange("p b (g s) -> p b g s", g=2),
                               ACT.Copy).then_inc(wt_near_ready, 1)

            def cross_copy(part):
                for i in range(4):
                    n = part * 4 + i
                    out = (c.v[:, 2 * i:2 * i + 2, :].rearrange("p b n -> p (b n)") if part
                           else c.k_t[:, i // 2, (i % 2) * BANK:(i % 2 + 1) * BANK])
                    act.wait_ge(kv_done, n + 1)
                    act.activation(out, c.bank[KV_BANKS[n % 3]][:, :], ACT.Copy).then_inc(kv_copied, 1)

            def evacuate_qk(n):
                act.wait_ge(proj_done, n * 2 + 1)
                act.activation(qk[:, 0:TOK], q_ps[:, :], ACT.Copy).then_inc(qk_ready, 1)
                act.wait_ge(proj_done, n * 2 + 2)
                act.activation(qk[:, TOK + SEG:2 * TOK + SEG], k_ps[:, :], ACT.Copy).then_inc(qk_ready, 1)
                if not (isinstance(n, int) and n == 0):
                    near_weights(n - 1)
                act.wait_ge(qk_ready, n * 2 + 2)
                act.activation(relu_neg[:, :, :, :], linear_in, ACT.Relu, scale=-1.0).then_inc(relu_ready, 1)
                act.wait_ge(relu_ready, n + 1)
                act.activation(exp_neg[:, :, :, :], relu_neg[:, :, :, :], ACT.Exp, scale=-1.0).then_inc(expneg_ready, 1)

            def evacuate_values(fill, part, slot):
                act.wait_ge(v_done, fill + 1)
                act.activation(v_sb[:, slot, 2 * part:2 * part + 2, :], v_ps, ACT.Copy).then_inc(v_ready, 1)

            def transposed_x(half):
                for k in range(KD):
                    act.wait_ge(xt_done, half * KD + k + 1)
                    act.activation(xt_hi[:, k, half * TOK:(half + 1) * TOK], c.bank[4 + k][:, :], ACT.Copy).then_inc(xt_hi_ready, 1)

            split_qk(0, 0, 0)
            split_wv(0, 0)
            transposed_x(0)
            std_of(1)
            act.wait_ge(gate_loaded, 16)
            act.activation(gate_exp[:, 0, :], gate_in[:, :], ACT.Exp, scale=-1.0).then_inc(gate_exped, 1)
            act.activation(gate_exp[:, 1, :], gate_in[:, :], ACT.Exp).then_inc(gate_exped, 1)
            split_qk(1, 0, 1)
            split_wv(0, 1)
            evacuate_qk(0)
            for part in range(2):
                evacuate_values(part, part, 0)
            transposed_x(1)
            act.wait_ge(gate_made, 2)

            def split_wo(q):
                raw, hi, lo = wo_quarter(q)
                act.wait_ge(wo_loaded, 32)
                act.activation(hi, raw, ACT.Copy).then_inc(wo_hi_ready, 1)

            def split_att(b):
                if b % HB == 0:
                    act.wait_ge(att_ready, (b // HB + 1) * H * 2)
                    cols = slice(0, H * SEG)
                else:
                    act.wait_ge(memory_added, (b // HB + 1) * H)
                    cols = slice(0, 2 * H * SEG)
                if b >= 2:
                    act.wait_ge(out_done, b - 1)
                act.activation(att_hi[:, b % 2, cols], batch_of_att(b)[:, cols], ACT.Copy).then_inc(att_hi_ready, 1)

            def gate_products(h, n):
                act.wait_ge(att_done, n + 1)
                for i in range(2):
                    out = att[:, 2 * i:2 * i + 2, :, bass.ds(h, 1), :].rearrange("p b g h s -> p (h b) g s")
                    act.activation(out, att_ps[i][:, :, 0:2, :], ACT.Copy, scale=gate[:, 1, bass.ds(h, 1)]).then_inc(att_ready, 1)

            def step(s):
                if s.at(1, 0):
                    gate_products(H - 1, s.n - 1)
                    split_att(0)
                act.wait_ge(shifted_ready, s.n + 1)
                act.activation(probs[:, :, :], shifted[:, :, :], ACT.Exp, scale=ATT_SCALE).then_inc(probs_ready, 1)
                if s.looped or s.h > 0:
                    gate_products(s.h - 1, s.n - 1)
                if s.follows(2):
                    split_qk(s.n + 2, s.pair + 1, s.member)
                if s.member == 1 and s.follows(3):
                    act.wait_ge(v_done, s.n + 1)
                    split_wv(s.quad + 1, s.slot)
                if quarter_at(s) is not None:
                    split_wo(quarter_at(s))
                if s.at(1, 0):
                    for b in range(1, HB):
                        split_att(b)
                    act.wait_ge(out_done, HB)
                if not s.at(HALVES - 1, H - 1):
                    evacuate_qk(s.n + 1)
                else:
                    cross_copy(0)
                    near_weights(s.n)
                    cross_copy(1)
                if s.follows(2):
                    if not s.at(0, 0):
                        act.wait_ge(att_done, s.n)
                    evacuate_values(s.n + 2, s.member, 1 - s.slot)

            head_steps(act, step)
            gate_products(H - 1, HALVES * H - 1)
            split_att(HB)
            split_att(HB + 1)
            act.wait_ge(var2_ready, 1)
            act.activation(c.std[:, 0:HB], c.meanvar[:, 0:HB, 1], ACT.Sqrt, bias=c.eps[:, :]).then_inc(std2_ready, 1)
            for b in range(HB, B):
                if b + 2 < B:
                    split_att(b + 2)
                act.wait_ge(var2_ready, b - HB + 2)
                act.activation(c.std[:, b:b + 1], c.meanvar[:, b, 1:2], ACT.Sqrt, bias=c.eps[:, :]).then_inc(std2_ready, 1)

        @block.vector
        def _(dve):
            dve.memset(sigma[:, :, :, :], 1.0 / DK).then_inc(fills_ready, 1)
            dve.memset(sums[:, :, :], 1.0).then_inc(fills_ready, 1)
            dve.memset(weights_t[:, :, :, :], 0.0).then_inc(fills_ready, 1)
            dve.memset(weights[:, :, :, :], 0.0).then_inc(fills_ready, 1)
            def statistics(half):
                dve.wait_ge(x_loaded[half], 16)
                for b in range(half * HB, (half + 1) * HB):
                    last = dve.bn_stats(c.stats[:, b, :], c.x_sb[:, b, :])
                last.then_inc(ln_chain, 1)
                dve.wait_ge(ln_chain, 2 * half + 1)
                for b in range(half * HB, (half + 1) * HB):
                    last = dve.bn_aggr(c.meanvar[:, b, :], c.stats[:, b, :])
                last.then_inc(var_ready, 1)

            def normalise(half):
                some = slice(half * HB, (half + 1) * HB)
                dve.wait_ge(std_ready, half + 1)
                dve.reciprocal(c.rstd[:, some], c.std[:, some]).then_inc(ln_chain, 1)
                dve.wait_ge(ln_chain, 2 * half + 2)
                for b in range(half * HB, (half + 1) * HB):
                    dve.tensor_scalar(c.xn[:, b, :], c.x_sb[:, b, :], c.meanvar[:, b, 0:1], c.rstd[:, b:b + 1],
                                      ALU.subtract, ALU.mult).then_inc(xn_ready, 1)

            def transposed_x(half):
                for k in range(KD):
                    dve.wait_ge(xt_hi_ready, half * KD + k + 1)
                    hi = xt_hi[:, k, half * TOK:(half + 1) * TOK]
                    dve.tensor_tensor(xt_lo[:, k, half * TOK:(half + 1) * TOK], c.bank[4 + k][:, :], hi,
                                      ALU.subtract).then_inc(xt_lo_ready, 1)

            def sigma_of(n):
                dve.wait_ge(expneg_ready, n + 1)
                dve.scalar_tensor_tensor(out=sigma[:, :, :, 0:SEG], in0=linear_in, scalar=1.0, in1=exp_neg[:, :, :, :],
                                         op0=ALU.add, op1=ALU.max).then_inc(sigma_ready, 1)

            statistics(0)
            normalise(0)
            statistics(1)
            transposed_x(0)
            normalise(1)
            dve.wait_ge(gate_exped, 2)
            dve.tensor_scalar(gate_exp[:, :, :], gate_exp[:, :, :], 1.0, None, ALU.add).then_inc(gate_made, 1)
            dve.wait_ge(gate_made, 1)
            dve.reciprocal(gate[:, :, :], gate_exp[:, :, :]).then_inc(gate_made, 1)
            sigma_of(0)
            transposed_x(1)

            def step(s):
                if s.at(1, 0):
                    add_memory(H - 1, s.n - 1)
                    split_att(0)
                dve.wait_ge(soft_done, s.n + 1)
                dve.tensor_reduce(row_max[:, :], soft_ps, AX.X, ALU.max).then_inc(max_ready, 1)
                dve.wait_ge(max_ready, s.n + 1)
                dve.tensor_tensor(shifted[:, :, :], soft_ps, row_max[:, :].unsqueeze(2).to_broadcast([P, HB, SEG]),
                                  ALU.subtract).then_inc(shifted_ready, 1)
                dve.wait_ge(lin_done, s.n + 1)
                dve.tensor_reduce(sums[SEG:P, 1, :], lin_ps[SEG:P, :, :], AX.X, ALU.add)
                dve.wait_ge(probs_ready, s.n + 1)
                dve.tensor_reduce(sums[:, 0, :], probs[:, :, :], AX.X, ALU.add).then_inc(sums_ready, 1)
                dve.wait_ge(sums_ready, s.n + 1)
                dve.reciprocal(inv[:, :, :], sums[:, :, :]).then_inc(inv_ready, 1)
                dve.wait_ge(inv_ready, s.n + 1)
                if not s.at(0, 0):
                    dve.wait_ge(t_done, s.n)
                for seg in range(2):
                    rows = slice(seg * SEG, (seg + 1) * SEG)
                    dve.tensor_tensor(weights[rows, :, seg, :], probs[rows, :, :],
                                      inv[rows, 0, :].unsqueeze(2).to_broadcast([SEG, HB, SEG]), ALU.mult)
                dve.tensor_tensor(weights[SEG:P, :, 0, :], lin_ps[SEG:P, :, 0:SEG],
                                  inv[SEG:P, 1, :].unsqueeze(2).to_broadcast([SEG, HB, SEG]), ALU.mult).then_inc(weights_ready, 1)
                if s.looped or s.h > 0:
                    add_memory(s.h - 1, s.n - 1)
                if s.at(1, 0):
                    for b in range(HB):
                        if b + 1 < HB:
                            split_att(b + 1)
                        add_output(b)
                dve.wait_ge(t_done, s.n + 1)
                dve.tensor_copy(weights_t[SEG:P, :, 0:2, :].rearrange("p b g s -> p b (g s)"), t_ps[SEG:P, :, :]).then_inc(wt_ready, 1)
                if not s.at(HALVES - 1, H - 1):
                    sigma_of(s.n + 1)

            def add_memory(h, n):
                for i in range(2):
                    dve.wait_ge(att_ready, n * 2 + i + 1)
                    out = att_of(h, i, 1)
                    last = dve.scalar_tensor_tensor(out=out, in0=att_ps[i][:, :, 2, :], scalar=gate[:, 0, bass.ds(h, 1)],
                                                    in1=out, op0=ALU.mult, op1=ALU.add)
                last.then_inc(memory_added, 1)

            def split_att(b):
                if b % HB == 0:
                    cols = slice(H * SEG, 2 * H * SEG)
                    dve.wait_ge(memory_added, (b // HB + 1) * H)
                    if b >= 2:
                        dve.wait_ge(out_done, b - 1)
                    dve.tensor_copy(att_hi[:, b % 2, cols], batch_of_att(b)[:, cols]).then_inc(att_hi_rest, 1)
                    dve.wait_ge(att_hi_rest, b // HB + 1)
                dve.wait_ge(att_hi_ready, b + 1)
                dve.tensor_tensor(att_lo[:, b % 2, :], batch_of_att(b), att_hi[:, b % 2, :], ALU.subtract).then_inc(att_lo_ready, 1)

            def add_output(b):
                dve.wait_ge(out_done, b + 1)
                rows = c.x_sb[:, b, :]
                dve.tensor_tensor(rows, rows, o_ps[b % 2], ALU.add).then_inc(x_added, 1)

            def normalise_for_cross(batches, n):
                for b in batches:
                    dve.wait_ge(x_added, b + 1)
                    last = dve.bn_stats(c.stats[:, b, :], c.x_sb[:, b, :])
                last.then_inc(ln2_chain, 1)
                dve.wait_ge(ln2_chain, 2 * n + 1)
                for b in batches:
                    last = dve.bn_aggr(c.meanvar[:, b, :], c.stats[:, b, :])
                last.then_inc(var2_ready, 1)
                dve.wait_ge(std2_ready, n + 1)
                some = slice(batches[0], batches[-1] + 1)
                dve.reciprocal(c.rstd[:, some], c.std[:, some]).then_inc(ln2_chain, 1)
                dve.wait_ge(ln2_chain, 2 * n + 2)
                for b in batches:
                    dve.tensor_scalar(c.xn[:, b, :], c.x_sb[:, b, :], c.meanvar[:, b, 0:1], c.rstd[:, b:b + 1],
                                      ALU.subtract, ALU.mult)

            head_steps(dve, step)
            add_memory(H - 1, HALVES * H - 1)
            split_att(HB)
            split_att(HB + 1)
            normalise_for_cross(range(HB), 0)
            for b in range(HB, B):
                add_output(b)
                if b + 2 < B:
                    split_att(b + 2)
                normalise_for_cross([b], b - HB + 1)

        @block.tensor
        def _(pe):
            def transpose_x(half):
                for k in range(KD):
                    pe.wait_ge(xn_ready, (half + 1) * HB)
                    for b in range(HB):
                        last = pe.transpose(c.bank[4 + k][:, b * S:(b + 1) * S],
                                            c.xn[:, half * HB + b, k * P:(k + 1) * P], c.ident[:, :])
                    last.then_inc(xt_done, 1)

            def split_product(out, left, right, pick_l, pick_r, start=True):
                n = 0
                for k in range(KD):
                    for a, b in ((0, 0), (0, 1), (1, 0)):
                        last = pe.matmul(out, pick_l(left[a], k), pick_r(right[b], k),
                                         start=start and n == 0, stop=n == 3 * KD - 1, skip_group_check=not start)
                        n += 1
                return last

            def project(n, half, slot, free):
                pe.wait_ge(qk_lo_ready, n + 1)
                toks = slice(half * TOK, (half + 1) * TOK)
                for i, out in enumerate((q_ps, k_ps)):
                    if free:
                        pe.wait_ge(qk_ready, n * 2 + i - 1)
                    split_product(out[:, :], (qk_hi, qk_lo), (xt_hi, xt_lo),
                                  lambda w, k: w[:, slot, (i * KD + k) * DK:(i * KD + k + 1) * DK],
                                  lambda t, k: t[:, k, toks]).then_inc(proj_done, 1)

            def project_values(fill, half, group, part, slot):
                pe.wait_ge(wv_lo_ready, group + 1)
                if not (isinstance(fill, int) and fill == 0):
                    pe.wait_ge(v_ready, fill)
                for i in range(2):
                    at = (half * HB + 2 * part + i) * S
                    last = split_product(v_ps[:, i, :], (xt_hi, xt_lo), (wv_hi, wv_lo),
                                         lambda t, k: t[:, k, at:at + S], lambda w, k: w[:, slot, k, :])
                last.then_inc(v_done, 1)

            def soft_scores(n):
                pe.wait_ge(qk_ready, n * 2 + 2)
                pe.matmul(c.bank[2][:, 0:HB * SEG], c.ident_b[:, :], mask[:, :, :], start=True, stop=False,
                          skip_group_check=True)
                for b in range(HB):
                    for seg in range(2):
                        at = slice(seg * SEG, (seg + 1) * SEG)
                        last = pe.matmul(soft_ps[at, b, :], q_sb[:, b, at], k_sb[:, b, at], start=False, stop=True,
                                         skip_group_check=True)
                last.then_inc(soft_done, 1)

            def linear_scores(n):
                pe.wait_ge(sigma_ready, n + 1)
                for b in range(HB):
                    last = pe.matmul(lin_ps[SEG:P, b, :], sigma[:, 0, b, 0:SEG], sigma[:, 1, b, :], start=True, stop=True)
                last.then_inc(lin_done, 1)

            def output(half):
                pe.wait_ge(wo_lo_ready, 4)
                for b in range(half * HB, (half + 1) * HB):
                    if b % HB == 1:
                        pe.wait_ge(v_ready, H + 2 if half < HALVES - 1 else HALVES * H)
                        if half == HALVES - 1:
                            pe.wait_ge(kv_copied, 8)
                    if b >= 2:
                        pe.wait_ge(x_added, b - 1)
                    hi, lo = (t[:, b % 2, :].rearrange("p (r c) -> p r c", c=H) for t in (att_hi, att_lo))
                    pe.wait_ge(att_hi_ready, b + 1)
                    if b % HB == 0:
                        pe.wait_ge(att_hi_rest, b // HB + 1)
                    for i in range(H):
                        pe.matmul(o_ps[b % 2], hi[:, :, i], wo_hi[:, i, :], start=i == 0, stop=False)
                        pe.matmul(o_ps[b % 2], hi[:, :, i], wo_lo[:, i, :], start=False, stop=False)
                    pe.wait_ge(att_lo_ready, b + 1)
                    for i in range(H):
                        last = pe.matmul(o_ps[b % 2], lo[:, :, i], wo_hi[:, i, :], start=False, stop=i == H - 1)
                    last.then_inc(out_done, 1)

            def cross_products(part):
                pe.wait_ge(kv_loaded, 32)
                pe.wait_ge(v_ready, HALVES * H)
                for i in range(4):
                    n = part * 4 + i
                    if n >= 3:
                        pe.wait_ge(kv_copied, n - 2)
                    if part == 0:
                        last = pe.matmul(c.bank[KV_BANKS[n % 3]][:, :], wkv[:, (i // 2) * P:(i // 2 + 1) * P],
                                         ctx_in[:, (i % 2) * HB:(i % 2 + 1) * HB, :], start=True, stop=True)
                    else:
                        for b in range(2):
                            last = pe.matmul(c.bank[KV_BANKS[n % 3]][:, b * D:(b + 1) * D], ctx_in[:, 2 * i + b, :],
                                             wkv[:, D:2 * D], start=True, stop=True)
                    last.then_inc(kv_done, 1)

            pe.wait_ge(consts_ready, 5)
            pe.wait_ge(fills_ready, 4)
            transpose_x(0)
            pe.wait_ge(xt_lo_ready, KD)
            project(0, 0, 0, False)
            for part in range(2):
                project_values(part, 0, 0, part, 0)
            soft_scores(0)
            linear_scores(0)
            transpose_x(1)

            def step(s):
                if not s.at(HALVES - 1, H - 1):
                    next_half = s.half + 1 if s.at(s.half, H - 1) else s.half
                    project(s.n + 1, next_half, 1 - s.member, True)
                else:
                    cross_products(0)
                pe.wait_ge(weights_ready, s.n + 1)
                for b in range(HB):
                    last = pe.transpose(t_ps[:, b, :], weights[:, b, :, :].rearrange("p g t -> p (g t)"), c.ident[:, :])
                last.then_inc(t_done, 1)
                if s.follows(2):
                    if s.at(0, H - 2):
                        pe.wait_ge(xt_lo_ready, HALVES * KD)
                    if s.at(1, 0):
                        pe.wait_ge(x_added, HB)
                    project_values(s.n + 2, s.half + 1 if s.at(0, H - 2) or s.at(0, H - 1) else s.half,
                                   s.pair + 1, s.member, 1 - s.slot)
                if not s.at(HALVES - 1, H - 1):
                    soft_scores(s.n + 1)
                else:
                    cross_products(1)
                pe.wait_ge(wt_ready, s.n + 1)
                pe.wait_ge(wt_near_ready, s.n + 1)
                if not s.at(0, 0):
                    pe.wait_ge(memory_added, s.n)
                if s.at(HALVES - 1, H - 2) or s.at(0, 0):
                    pe.wait_ge(v_ready, s.n + 2)
                cols = slice(s.member * DK, (s.member + 1) * DK)
                for b in range(HB):
                    last = pe.matmul(att_ps[b // 2][:, b % 2, :, :], v_sb[:, s.slot, b, cols], weights_t[:, b, :, :],
                                     start=True, stop=True)
                last.then_inc(att_done, 1)
                if not s.at(HALVES - 1, H - 1):
                    linear_scores(s.n + 1)
                if s.at(s.half, H - 1):
                    output(s.half)

            head_steps(pe, step)
    phase.close()

NX, HD = 16, 16
CROSS_SCALE = 1.0 / float(HD) ** 0.5
CH = NX // 2
ROWG = 32


def cross_phase(c):
    nc = c.nc
    phase = ExitStack()

    def sb(name, shape, dt):
        return c.sb(name, shape, dt, phase)

    wq, wout, k_t, v_sb = c.wq, c.wout, c.k_t, c.v
    xn_t = sb("x_xn_t", [P, KD, B * S], F32)
    q_t = sb("x_q_t", [P, KD, B * S], F32)
    v_pad = sb("x_v_pad", [P, NX, ROWG], F32)
    parity = sb("x_parity", [P, 2], F32)
    q_sel = sb("x_q_sel", [P, 2, KD, S], F32)
    k_sel = sb("x_k_sel", [P, KD, S], F32)
    mask = sb("x_mask", [P, 4, S], BF16)
    row_max = sb("x_row_max", [P, 2, CH], F32)
    neg_max = sb("x_neg_max", [P, 2, CH], F32)
    probs = sb("x_probs", [P, 2, CH, S], F32)
    probs_t = sb("x_probs_t", [P, 2, CH, S], F32)
    sums = sb("x_sums", [P, KD, 4, 2], F32)
    inv_sums = sb("x_inv_sums", [P, NX], F32)
    inv = sb("x_inv", [P, D], F32)
    inv_t = sb("x_inv_t", [P, KD, S], F32)
    heads_t = sb("x_heads_t", [P, KD, S], F32)

    s_ps = [c.psum[:, 2 * i * BANK:2 * (i + 1) * BANK].rearrange("p (h t) -> p h t", h=CH) for i in range(2)]
    t_ps = c.psum[:, 4 * BANK:6 * BANK].rearrange("p (h t) -> p h t", h=CH)
    ht_ps = c.bank[6][:, 0:KD * S].rearrange("p (k s) -> p k s", k=KD)
    xt_ps = [c.bank[i][:, :].rearrange("p (k t) -> p k t", k=KD) for i in range(B // 2)]
    logit_ps = c.bank[4][:, 0:B * NE].rearrange("p (b e) -> p b e", b=B)
    it_ps = c.bank[7][:, 0:KD * S].rearrange("p (k s) -> p k s", k=KD)
    y_ps = c.bank[7][:, KD * S:KD * S + D]

    sem = c.sem
    consts, v_zeroed, stats_made = sem("x_consts"), sem("x_v_zeroed"), sem("x_stats_made")
    xt_done, xt_ready = sem("x_xt_done"), sem("x_xt_ready")
    q_done, q_ready, sel_ready, padded = sem("x_q_done"), sem("x_q_ready"), sem("x_sel_ready"), sem("x_padded")
    s_done, max_ready, neg_ready = sem("x_s_done"), sem("x_max_ready"), sem("x_neg_ready")
    probs_ready, t_done, t_ready = sem("x_probs_ready"), sem("x_t_done"), sem("x_t_ready")
    var3_ready, std3_ready, ln3_chain, xn3_ready = sem("e_var_ready"), sem("e_std_ready"), sem("e_ln_chain"), sem("e_xn_ready")
    xt3_done, xt3_ready, logits_done = sem("e_xt_done"), sem("e_xt_ready"), sem("e_logits_done")
    wo_loaded = [sem(f"e_wo_loaded{i}") for i in range(2)]
    wo_hi_ready, wo_split = sem("e_wo_hi_ready"), sem("e_wo_split")
    inv_spread, t_first_ready = sem("x_inv_spread"), sem("x_t_first_ready")
    pv_done, inv_ready, heads_ready = sem("x_pv_done"), sem("x_inv_ready"), sem("x_heads_ready")
    it_done, it_ready, y_done, y_added = sem("x_it_done"), sem("x_it_ready"), sem("x_y_done"), sem("x_y_added")

    def chunk_heads(ch):
        return [(r * 4 + k * 2 + odd, 2 * ch + r, k, odd) for r in range(2) for k in range(KD) for odd in range(2)]

    def batches(eng, step):
        step(0, 0)
        step(1, 1)
        with eng.Fori(2, B - 1) as b:
            step(b, None)
        step(B - 1, B - 1)

    with nc.Block() as block:
        @block.sync
        def _(sp):
            c.load_experts(sp)
            sp.wait_ge(q_done, 4)
            for e in range(NE):
                if e >= 2:
                    sp.wait_ge(wo_split, e - 1)
                sp.dma_start(xn_t[:, e % 2, :], c.expert_wo[e]).then_inc(wo_loaded[e % 2], 16)

        @block.gpsimd
        def _(pool):
            pool.memset(mask[:, :, :], 0.0).then_inc(consts, 1)
            pool.memset(v_pad[:, :, :], 0.0).then_inc(v_zeroed, 1)
            pool.memset(parity[:, :], 0.0).then_inc(consts, 1)
            pool.wait_ge(v_zeroed, 1)
            pool.wait_ge(consts, 2)
            pool.affine_select(out=mask[:, :, :], in_=mask[:, :, :], compare_op=ALU.is_ge, fill=MASKED, base=0,
                               pattern=[[0, 4], [-1, S]], channel_multiplier=1).then_inc(consts, 1)
            n = 3
            for odd in range(2):
                col = parity[:, odd:odd + 1]
                for start in range(HD * odd, P, 2 * HD):
                    for base, fill in ((start, 1.0), (start + HD, 0.0)):
                        if base < P:
                            pool.wait_ge(consts, n)
                            pool.affine_select(out=col, in_=col, compare_op=ALU.is_gt, fill=fill, base=base,
                                               pattern=[[0, 1]], channel_multiplier=-1).then_inc(consts, 1)
                            n += 1
            c.n_x_consts = n
            pool.wait_ge(consts, n)
            for e in range(NE):
                cols = slice(e * OW, (e + 1) * OW)
                pool.wait_ge(wo_loaded[e % 2], 16 * (e // 2 + 1))
                pool.tensor_copy(c.expert_wo_hi[:, cols], xn_t[:, e % 2, :]).then_inc(wo_hi_ready, 1)
                pool.wait_ge(wo_hi_ready, e + 1)
                pool.tensor_tensor(c.expert_wo_lo[:, cols], xn_t[:, e % 2, :], c.expert_wo_hi[:, cols], ALU.subtract).then_inc(wo_split, 1)

        @block.scalar
        def _(act):
            for i in range(4):
                act.wait_ge(q_done, i + 1)
                act.activation(q_t[:, i % 2, (i // 2) * BANK:(i // 2 + 1) * BANK], c.bank[4 + i][:, :], ACT.Copy).then_inc(q_ready, 1)

            def step(b, static):
                for ch in range(2):
                    u = 2 * b + ch
                    act.wait_ge(neg_ready, u + 1)
                    if not static == 0:
                        act.wait_ge(t_done, u - 1)
                        act.wait_ge(inv_ready, b)
                    for place, group, k, odd in chunk_heads(ch):
                        if place == CH // 2 and not (static == 0 and ch == 0):
                            copy_weights(u - 1, 1 - ch, static == 0 or (static == 1 and ch == 0))
                        last = act.activation(probs[:, ch, place, :], s_ps[ch][:, place, :], ACT.Exp, scale=CROSS_SCALE,
                                              bias=neg_max[:, ch, place:place + 1], accum_out=sums[:, k, group, odd:odd + 1])
                    last.then_inc(probs_ready, 1)

            def copy_weights(u, ch, first):
                act.wait_ge(t_done, u + 1)
                if not first:
                    act.wait_ge(pv_done, u - 1)
                act.activation(probs_t[:, ch, CH // 2:CH, :], t_ps[:, CH // 2:CH, :], ACT.Copy).then_inc(t_ready, 1)

            batches(act, step)
            copy_weights(2 * B - 1, 1, False)

            def std_of(some, n):
                act.wait_ge(var3_ready, n)
                act.activation(c.std[:, some], c.meanvar[:, some, 1], ACT.Sqrt, bias=c.eps[:, :]).then_inc(std3_ready, 1)

            std_of(slice(0, B - 1), 1)
            act.wait_ge(wo_split, NE)
            for i in range(B // 2):
                if i == 1:
                    std_of(slice(B - 1, B), 2)
                act.wait_ge(xt3_done, i + 1)
                act.activation(xn_t[:, :, 2 * i * S:2 * (i + 1) * S], xt_ps[i], ACT.Copy).then_inc(xt3_ready, 1)

        @block.vector
        def _(dve):
            def pad_values(b):
                values = v_sb[:, bass.ds(b, 1), :].rearrange("p b (g o d) -> p (b g) o d", o=2, d=HD)
                out = v_pad[:, :, :].rearrange("p (g o) n -> p g (o n)", o=2)
                for odd in range(2):
                    first = odd * (ROWG + HD)
                    last = dve.tensor_copy(out[:, :, first:first + HD], values[:, :, odd, :])
                last.then_inc(padded, 1)

            dve.wait_ge(v_zeroed, 1)
            pad_values(0)
            for i in range(4):
                dve.wait_ge(xt_done, i + 1)
                dve.tensor_copy(xn_t[:, i % 2, (i // 2) * BANK:(i // 2 + 1) * BANK], c.bank[i][:, :]).then_inc(xt_ready, 1)

            def select(b, ch):
                rows = slice(2 * ch * ROWG, 2 * (ch + 1) * ROWG)
                at = bass.ds(b * S, S)
                for odd in range(2):
                    dve.tensor_scalar(q_sel[rows, odd, :, :], q_t[rows, :, at], parity[rows, odd:odd + 1], None, ALU.mult)
                dve.tensor_copy(k_sel[rows, :, :], k_t[rows, :, at]).then_inc(sel_ready, 1)

            dve.wait_ge(q_ready, 2)
            dve.wait_ge(consts, c.n_x_consts)
            select(0, 0)
            select(0, 1)
            dve.wait_ge(q_ready, 4)

            def step(b, static):
                for ch in range(2):
                    u = 2 * b + ch
                    dve.wait_ge(s_done, u + 1)
                    dve.tensor_reduce(row_max[:, ch, :], s_ps[ch], AX.X, ALU.max).then_inc(max_ready, 1)
                    dve.wait_ge(max_ready, u + 1)
                    if not (static == 0):
                        dve.wait_ge(probs_ready, u - 1)
                    dve.tensor_scalar(neg_max[:, ch, :], row_max[:, ch, :], -CROSS_SCALE, None, ALU.mult).then_inc(neg_ready, 1)
                    if ch == 0 and static != 0:
                        invert_sums(b - 1)
                    if not (static == 0 and ch == 0):
                        copy_weights(u - 1, 1 - ch, static == 0 or (static == 1 and ch == 0))
                    if ch == 0 and static not in (0, 1):
                        add_output(b - 2)
                    if static != B - 1:
                        select(b + 1, ch)
                    if ch == 0 and static != 0:
                        normalise(b - 1)
                        pad_values(b)

            def copy_weights(u, ch, first):
                dve.wait_ge(t_done, u + 1)
                if not first:
                    dve.wait_ge(pv_done, u - 1)
                dve.tensor_copy(probs_t[:, ch, 0:CH // 2, :], t_ps[:, 0:CH // 2, :]).then_inc(t_first_ready, 1)

            def invert_sums(b):
                dve.wait_ge(probs_ready, 2 * b + 2)
                dve.reciprocal(inv_sums[:, :], sums[:, :, :, :].rearrange("p k g o -> p (k g o)")).then_inc(inv_ready, 1)
                dve.wait_ge(inv_ready, b + 1)
                wait_past(dve, it_done, b)
                dve.tensor_copy(inv[:, :].rearrange("p (h d) -> p h d", h=NX),
                                inv_sums[:, :].unsqueeze(2).to_broadcast([P, NX, HD])).then_inc(inv_spread, 1)

            def normalise(b):
                dve.wait_ge(it_done, b + 1)
                dve.tensor_copy(inv_t[:, :, :], it_ps).then_inc(it_ready, 1)
                dve.wait_ge(it_ready, b + 1)
                dve.wait_ge(pv_done, 2 * b + 2)
                wait_past(dve, y_done, b)
                dve.tensor_tensor(heads_t[:, :, :], ht_ps, inv_t[:, :, :], ALU.mult).then_inc(heads_ready, 1)

            def add_output(b):
                dve.wait_ge(y_done, b + 1)
                rows = c.x_sb[:, bass.ds(b, 1), :].rearrange("p b d -> p (b d)")
                dve.tensor_tensor(rows, rows, y_ps, ALU.add).then_inc(y_added, 1)
                dve.wait_ge(y_added, b + 1)
                dve.bn_stats(c.stats[:, bass.ds(b, 1), :].rearrange("p b n -> p (b n)"), rows).then_inc(stats_made, 1)

            batches(dve, step)
            invert_sums(B - 1)
            copy_weights(2 * B - 1, 1, False)
            add_output(B - 2)
            dve.wait_ge(stats_made, B - 1)
            for b in range(B - 1):
                last = dve.bn_aggr(c.meanvar[:, b, :], c.stats[:, b, :])
            last.then_inc(var3_ready, 1)
            normalise(B - 1)

            def layernorm(b):
                dve.tensor_scalar(c.xn[:, b, :], c.x_sb[:, b, :], c.meanvar[:, b, 0:1], c.rstd[:, b:b + 1],
                                  ALU.subtract, ALU.mult).then_inc(xn3_ready, 1)

            dve.wait_ge(std3_ready, 1)
            dve.reciprocal(c.rstd[:, 0:B - 1], c.std[:, 0:B - 1]).then_inc(ln3_chain, 1)
            dve.wait_ge(ln3_chain, 1)
            for b in range(HB):
                layernorm(b)
            add_output(B - 1)
            dve.wait_ge(stats_made, B)
            dve.bn_aggr(c.meanvar[:, B - 1, :], c.stats[:, B - 1, :]).then_inc(var3_ready, 1)
            for b in range(HB, B - 1):
                layernorm(b)
            dve.wait_ge(std3_ready, 2)
            dve.reciprocal(c.rstd[:, B - 1:B], c.std[:, B - 1:B]).then_inc(ln3_chain, 1)
            dve.wait_ge(ln3_chain, 2)
            layernorm(B - 1)
            dve.wait_ge(logits_done, 1)
            dve.tensor_copy(c.logits[:, :, :], logit_ps)

        @block.tensor
        def _(pe):
            for i in range(4):
                half, k = i // 2, i % 2
                for b in range(HB):
                    last = pe.transpose(c.bank[i][:, b * S:(b + 1) * S], c.xn[:, half * HB + b, k * P:(k + 1) * P], c.ident[:, :])
                last.then_inc(xt_done, 1)
            for i in range(4):
                pe.wait_ge(xt_ready, 2 * (i // 2) + 2)
                for k in range(KD):
                    last = pe.matmul(c.bank[4 + i][:, :], wq[:, k, (i % 2) * P:(i % 2 + 1) * P],
                                     xn_t[:, k, (i // 2) * BANK:(i // 2 + 1) * BANK], start=k == 0, stop=k == KD - 1)
                last.then_inc(q_done, 1)
            pe.wait_ge(consts, c.n_x_consts)

            def scores(b, ch, first):
                if not first:
                    pe.wait_ge(probs_ready, 2 * b + ch - 1)
                pe.wait_ge(sel_ready, 2 * b + ch + 1)
                for r in range(2):
                    pe.matmul(c.bank[2 * ch + r][:, :], c.ident_b[:, :], mask[:, :, :], start=True, stop=False,
                              skip_group_check=True)
                for place, group, k, odd in chunk_heads(ch):
                    rows = slice(group * ROWG, (group + 1) * ROWG)
                    last = pe.matmul(s_ps[ch][:, place, :], q_sel[rows, odd, k, :], k_sel[rows, k, :],
                                     start=False, stop=True, skip_group_check=True)
                last.then_inc(s_done, 1)

            def weigh(b, ch):
                pe.wait_ge(t_ready, 2 * b + ch + 1)
                pe.wait_ge(t_first_ready, 2 * b + ch + 1)
                if ch == 0:
                    pe.wait_ge(padded, b + 1)
                    wait_past(pe, heads_ready, b)
                for place, group, k, odd in chunk_heads(ch):
                    head = k * CH + group * 2 + odd
                    last = pe.matmul(ht_ps[group * ROWG:(group + 1) * ROWG, k, :],
                                     v_pad[:, head, :], probs_t[:, ch, place, :],
                                     start=odd == 0, stop=odd == 1)
                last.then_inc(pv_done, 1)

            def transpose_weights(b, ch, first):
                pe.wait_ge(probs_ready, 2 * b + ch + 1)
                if not first:
                    pe.wait_ge(t_ready, 2 * b + ch)
                    pe.wait_ge(t_first_ready, 2 * b + ch)
                for place in range(CH):
                    last = pe.transpose(t_ps[:, place, :], probs[:, ch, place, :], c.ident[:, :])
                last.then_inc(t_done, 1)

            def transpose_inverse(b):
                pe.wait_ge(inv_spread, b + 1)
                wait_past(pe, y_added, b)
                for k in range(KD):
                    last = pe.transpose(it_ps[:, k, :], inv[:, k * P:(k + 1) * P], c.ident[:, :])
                last.then_inc(it_done, 1)

            def project(b):
                pe.wait_ge(heads_ready, b + 1)
                for k in range(KD):
                    last = pe.matmul(y_ps, heads_t[:, k, :], wout[:, k, :], start=k == 0, stop=k == KD - 1)
                last.then_inc(y_done, 1)

            scores(0, 0, True)
            pe.wait_ge(q_ready, 4)

            def step(b, static):
                scores(b, 1, static == 0)
                if static != 0:
                    weigh(b - 1, 1)
                    transpose_inverse(b - 1)
                transpose_weights(b, 0, static == 0)
                if static != B - 1:
                    scores(b + 1, 0, False)
                if static != 0:
                    project(b - 1)
                weigh(b, 0)
                transpose_weights(b, 1, False)

            batches(pe, step)
            weigh(B - 1, 1)
            transpose_inverse(B - 1)
            project(B - 1)

            def transpose_xn(i):
                pe.wait_ge(xn3_ready, 2 * i + 2)
                for b in range(2):
                    for k in range(KD):
                        last = pe.transpose(xt_ps[i][:, k, b * S:(b + 1) * S], c.xn[:, 2 * i + b, k * P:(k + 1) * P], c.ident[:, :])
                last.then_inc(xt3_done, 1)

            def choose(i):
                pe.wait_ge(xt3_ready, i + 1)
                for b in range(2 * i, 2 * i + 2):
                    for k in range(KD):
                        last = pe.matmul(logit_ps[:, b, :], xn_t[:, k, b * S:(b + 1) * S], c.gate[:, k, :],
                                         start=k == 0, stop=k == KD - 1)
                return last

            for i in range(B // 2):
                transpose_xn(i)
                if i > 0:
                    choose(i - 1)
            choose(B // 2 - 1).then_inc(logits_done, 1)
    phase.close()

M = 512
KM = M // P
TOPK = 2
PICKS = TOPK * B
TILES = (TOPK * B * S + NE * (P - 1)) // P
EW, OW = 2 * KD * M, KM * D


def expert_phase(c, xn_dram, picks_dram, out):
    nc = c.nc
    phase = ExitStack()

    def sb(name, shape, dt):
        return c.sb(name, shape, dt, phase)

    xn, logits = c.xn, c.logits
    iota_i = sb("e_iota_i", [P, P + 1], I32)
    iota = sb("e_iota", [P, P + 1], F32)
    tile_start = sb("e_tile_start", [P, TILES + 1], F32)
    spare_row = sb("e_spare_row", [P, TILES], F32)
    ones = sb("e_ones", [P, P], BF16)
    before = sb("e_before", [P, P], BF16)
    ones_f = sb("e_ones_f", [P, NE], F32)
    top = sb("e_top", [P, B, NE], F32)
    top_idx = sb("e_top_idx", [P, B, NE], U32)
    chosen_id = sb("e_chosen_id", [P, B, TOPK], F32)
    chosen = sb("e_chosen", [P, TOPK, B, NE], F32)
    either = sb("e_either", [P, B + 1, NE], BF16)
    diff = sb("e_diff", [P, B], F32)
    ratio = sb("e_ratio", [P, B], F32)
    share = sb("e_share", [P, TOPK, B], F32)
    n_over = sb("e_n_over", [P, NE, NE], F32)
    n_tiles = sb("e_n_tiles", [P, NE], F32)
    end_tile = sb("e_end_tile", [P, NE], F32)
    base = sb("e_base", [P, NE], F32)
    place = sb("e_place", [P, B, NE], F32)
    place_k = sb("e_place_k", [P, TOPK, B, NE], F32)
    row_f = sb("e_row_f", [P, TOPK, B], F32)
    reached = sb("e_reached", [P, PICKS, TILES + 1], F32)
    in_tile = sb("e_in_tile", [P, PICKS, 3, TILES], BF16)
    tile_of = sb("e_tile_of", [P, PICKS], F32)
    at_row = sb("e_at_row", [P, PICKS], F32)
    row_hot = sb("e_row_hot", [P, PICKS, P], BF16)
    pick = sb("e_pick", [P, TILES], F32)
    wrap = sb("e_wrap", [P, TILES], F32)
    spare = sb("e_spare", [P, TILES], F32)
    token_f = sb("e_token_f", [P, TILES], F32)
    token_row = sb("e_token_row", [P, TILES], U32)
    pick_row = sb("e_pick_row", [P, TILES], U32)
    ended = sb("e_ended", [1, TILES, NE], F32)
    owner_f = sb("e_owner_f", [1, TILES], F32)
    owner = sb("e_owner", [1, 2, TILES], I32)
    x_rows = sb("e_x_rows", [P, 2, D], F32)
    x_cols = sb("e_x_cols", [P, 2, KD, P], F32)
    silu = sb("e_silu", [P, 2, M], F32)
    inner = sb("e_inner", [P, 2, M], F32)
    inner_hi = sb("e_inner_hi", [P, 2, KM, P], F32R)
    inner_lo = sb("e_inner_lo", [P, 2, KM, P], F32R)
    y_rows = sb("e_y_rows", [P, 2, D], F32)
    picked = [c.v, c.k_t[:, :, :].rearrange("p k n -> p (k n)").rearrange("p (b d) -> p b d", b=B)]

    x_ps = c.bank[0][:, 0:KD * P].rearrange("p (k t) -> p k t", k=KD)
    t_ps = c.bank[1].rearrange("p (m t) -> p m t", m=KM)
    y_ps = [c.bank[2][:, 0:D], c.bank[3][:, 0:D]]
    h_ps = [(c.bank[4], c.bank[5]), (c.bank[6], c.bank[7])]
    rank_ps = c.bank[1][:, 0:(B + 1) * NE].rearrange("p (b e) -> p b e", b=B + 1)
    invert_ps = c.bank[2][:, 0:3 * TILES].rearrange("p (q t) -> p q t", q=3)

    sem = c.sem
    consts, iota_made = sem("e_consts"), sem("e_iota_made")
    route, diff_ready, ratio_ready = sem("e_route"), sem("e_diff_ready"), sem("e_ratio_ready")
    either_ready, counts_done = sem("e_either_ready"), sem("e_counts_done")
    xn_stored, hot_ready, inverted = sem("e_xn_stored"), sem("e_hot_ready"), sem("e_inverted")
    tokens_known, picks_known, owner_known = sem("e_tokens_known"), sem("e_picks_known"), sem("e_owner_known")
    x_loaded = [sem(f"e_x_loaded{i}") for i in range(2)]
    y_stored = [sem(f"e_y_stored{i}") for i in range(2)]
    x_done, x_ready = sem("e_x_done"), sem("e_x_ready")
    h_done, silu_ready, inner_ready = sem("e_h_done"), sem("e_silu_ready"), sem("e_inner_ready")
    t_done, t_ready, t_lo_ready, y_done, y_ready = sem("e_t_done"), sem("e_t_ready"), sem("e_t_lo_ready"), sem("e_y_done"), sem("e_y_ready")
    gathered = [sem(f"e_gathered{i}") for i in range(B)]
    mixed, out_stored = sem("e_mixed"), sem("e_out_stored")

    def tiles(eng, step):
        for slot in range(2):
            step(slot, slot, 0, TILES - 1 - slot)
        with eng.Fori(1, (TILES - 3) // 2) as pair:
            for slot in range(2):
                step(pair * 2 + slot, slot, pair, None)
        for tile in range(TILES - 3, TILES):
            step(tile, tile % 2, tile // 2, TILES - 1 - tile)

    def more(left, n):
        return left is None or left >= n

    with nc.Block() as block:
        @block.sync
        def _(sp):
            sp.dma_start(xn_dram.rearrange("(b p) d -> p b d", p=P), xn[:, :, :]).then_inc(xn_stored, 16)
            for slot in range(2):
                sp.wait_ge(y_stored[slot], 16 * ((TILES + 1 - slot) // 2))
            picks = picks_dram[0:PICKS * P, :].rearrange("(k b p) d -> p k b d", k=TOPK, b=B)
            for b in range(B):
                for k in range(TOPK):
                    sp.dma_start(picked[k][:, b, :], picks[:, k, b, :]).then_inc(gathered[b], 16)
            for b in range(B):
                sp.wait_ge(mixed, TOPK * (b - b % 2) + 3 + b % 2)
                sp.dma_start(out[b], c.x_sb[:, b, :]).then_inc(out_stored, 16)
            sp.wait_ge(out_stored, 16 * B)

        @block.gpsimd
        def _(pool):
            pool.memset(ones[:, :], 1.0).then_inc(consts, 1)
            pool.memset(before[:, :], 1.0).then_inc(consts, 1)
            pool.wait_ge(consts, 2)
            pool.affine_select(out=before[:, :], in_=before[:, :], compare_op=ALU.is_gt, fill=0.0, base=0,
                               pattern=[[1, P]], channel_multiplier=-1).then_inc(consts, 1)
            pool.wait_ge(consts, 3)
            pool.iota(iota_i[:, 0:P], pattern=[[1, P]], base=0, channel_multiplier=0).then_inc(iota_made, 1)
            pool.wait_ge(iota_made, 1)
            pool.iota(iota_i[:, P:P + 1], pattern=[[0, 1]], base=0, channel_multiplier=1).then_inc(iota_made, 1)
            pool.wait_ge(xn_stored, 16)
            pool.wait_ge(tokens_known, 1)

            def load(tile):
                slot = tile % 2
                pool.indirect_dma_start(out=x_rows[:, slot, :], out_offset=None, in_=xn_dram,
                                        in_offset=bass.IndirectOffsetOnAxis(ap=token_row[:, tile:tile + 1], axis=0)
                                        ).then_inc(x_loaded[slot], 16)

            def store(tile):
                slot = tile % 2
                pool.wait_ge(y_ready, tile + 1)
                pool.indirect_dma_start(out=picks_dram, out_offset=bass.IndirectOffsetOnAxis(ap=pick_row[:, tile:tile + 1], axis=0),
                                        in_=y_rows[:, slot, :], in_offset=None).then_inc(y_stored[slot], 16)

            load(0)
            load(1)
            pool.wait_ge(picks_known, 1)
            for tile in range(TILES):
                if tile + 2 < TILES:
                    pool.wait_ge(x_done, tile + 1)
                    load(tile + 2)
                if tile > 0:
                    store(tile - 1)
            store(TILES - 1)

        @block.scalar
        def _(act):
            act.wait_ge(diff_ready, 1)
            act.activation(ratio[:, :], diff[:, :], ACT.Exp).then_inc(ratio_ready, 1)

            def columns(tile, slot):
                act.wait_ge(x_done, tile + 1)
                act.activation(x_cols[:, slot, :, :], x_ps, ACT.Copy).then_inc(x_ready, 1)

            def silu_of(tile, slot):
                act.wait_ge(h_done, tile * 2 + 1)
                act.activation(silu[:, slot, :], h_ps[slot][0], ACT.Silu).then_inc(silu_ready, 1)

            columns(0, 0)
            columns(1, 1)
            silu_of(0, 0)

            def step(tile, slot, pair, left):
                act.wait_ge(t_done, tile + 1)
                wait_past(act, y_done, tile - 1)
                act.activation(inner_hi[:, slot, :, :], t_ps, ACT.Copy).then_inc(t_ready, 1)
                if more(left, 2):
                    columns(tile + 2, slot)
                if more(left, 1):
                    silu_of(tile + 1, 1 - slot)

            tiles(act, step)

        @block.vector
        def _(dve):
            n_route = [0]

            def chained(instruction):
                n_route[0] += 1
                instruction.then_inc(route, 1)
                dve.wait_ge(route, n_route[0])

            dve.wait_ge(iota_made, 2)
            dve.memset(ones_f[:, :], 1.0)
            dve.memset(either[:, B, :], 0.0)
            chained(dve.tensor_copy(iota[:, :], iota_i[:, :]))
            chained(dve.tensor_scalar(tile_start[:, :], iota[:, 0:TILES + 1], float(P), None, ALU.mult))
            dve.tensor_scalar(spare_row[:, :], tile_start[:, 0:TILES], iota[:, P:P + 1], float(PICKS * P), ALU.add, ALU.add)
            for b in range(B):
                last = dve.max(top[:, b, :], logits[:, b, :])
            chained(last)
            for b in range(B):
                last = dve.max_index(top_idx[:, b, :], top[:, b, :], logits[:, b, :])
            chained(last)
            dve.tensor_tensor(diff[:, :], top[:, :, 1], top[:, :, 0], ALU.subtract).then_inc(diff_ready, 1)
            chained(dve.tensor_copy(chosen_id[:, :, :], top_idx[:, :, 0:TOPK]))
            ids = iota[:, 0:NE].unsqueeze(1).to_broadcast([P, B, NE])
            for k in range(TOPK):
                last = dve.tensor_tensor(chosen[:, k, :, :], ids, chosen_id[:, :, k].unsqueeze(2).to_broadcast([P, B, NE]), ALU.is_equal)
            chained(last)
            dve.tensor_tensor(either[:, 0:B, :], chosen[:, 0, :, :], chosen[:, 1, :, :], ALU.add).then_inc(either_ready, 1)
            dve.wait_ge(ratio_ready, 1)
            chained(dve.tensor_scalar(share[:, 1, :], ratio[:, :], 1.0, None, ALU.add))
            chained(dve.reciprocal(share[:, 0, :], share[:, 1, :]))
            chained(dve.tensor_tensor(share[:, 1, :], share[:, 0, :], ratio[:, :], ALU.mult))
            dve.wait_ge(counts_done, 1)
            chained(dve.tensor_tensor(n_over[:, :, :], rank_ps[:, B, :].unsqueeze(2).to_broadcast([P, NE, NE]),
                                      tile_start[:, 0:NE].unsqueeze(1).to_broadcast([P, NE, NE]), ALU.is_gt))
            chained(dve.tensor_reduce(n_tiles[:, :], n_over[:, :, :], AX.X, ALU.add))
            chained(dve.tensor_tensor_scan(end_tile[:, :], ones_f[:, :], n_tiles[:, :], 0.0, ALU.mult, ALU.add))
            chained(dve.tensor_tensor(base[:, :], end_tile[:, :], n_tiles[:, :], ALU.subtract))
            chained(dve.tensor_scalar(base[:, :], base[:, :], float(P), None, ALU.mult))
            chained(dve.tensor_tensor(place[:, :, :], rank_ps[:, 0:B, :], base[:, :].unsqueeze(1).to_broadcast([P, B, NE]), ALU.add))
            for k in range(TOPK):
                last = dve.tensor_tensor(place_k[:, k, :, :], chosen[:, k, :, :], place[:, :, :], ALU.mult)
            chained(last)
            chained(dve.tensor_reduce(row_f[:, :, :], place_k[:, :, :, :], AX.X, ALU.add))
            rows = row_f[:, :, :].rearrange("p k b -> p (k b)")
            chained(dve.tensor_tensor(reached[:, :, :], rows.unsqueeze(2).to_broadcast([P, PICKS, TILES + 1]),
                                      tile_start[:, :].unsqueeze(1).to_broadcast([P, PICKS, TILES + 1]), ALU.is_ge))
            chained(dve.tensor_reduce(tile_of[:, :], reached[:, :, 1:TILES + 1], AX.X, ALU.add))
            chained(dve.scalar_tensor_tensor(out=at_row[:, :], in0=tile_of[:, :], scalar=-float(P), in1=rows,
                                             op0=ALU.mult, op1=ALU.add))
            chained(dve.tensor_tensor(in_tile[:, :, 2, :], reached[:, :, 0:TILES], reached[:, :, 1:TILES + 1], ALU.subtract))
            dve.tensor_scalar(in_tile[:, :, 0, :], in_tile[:, :, 2, :], iota[:, P:P + 1], None, ALU.mult)
            dve.tensor_tensor(in_tile[:, :, 1, :], in_tile[:, :, 2, :], iota[:, 0:PICKS].unsqueeze(2).to_broadcast([P, PICKS, TILES]),
                              ALU.mult)
            for k in range(TOPK):
                some = slice(k * B, (k + 1) * B)
                dve.tensor_tensor(row_hot[:, some, :], iota[:, 0:P].unsqueeze(1).to_broadcast([P, B, P]),
                                  at_row[:, some].unsqueeze(2).to_broadcast([P, B, P]), ALU.is_equal).then_inc(hot_ready, 1)
            chained(dve.tensor_tensor(ended[:, :, :], end_tile[0:1, :].unsqueeze(1).to_broadcast([1, TILES, NE]),
                                      iota[0:1, 0:TILES].unsqueeze(2).to_broadcast([1, TILES, NE]), ALU.is_le))
            chained(dve.tensor_reduce(owner_f[:, :], ended[:, :, :], AX.X, ALU.add))
            chained(dve.tensor_scalar(owner_f[:, :], owner_f[:, :], float(NE - 1), float(OW), ALU.min, ALU.mult))
            dve.tensor_copy(owner[:, 1, :], owner_f[:, :])
            chained(dve.tensor_scalar(owner_f[:, :], owner_f[:, :], float(EW // OW), None, ALU.mult))
            dve.tensor_copy(owner[:, 0, :], owner_f[:, :]).then_inc(owner_known, 1)
            dve.wait_ge(inverted, 1)
            chained(dve.tensor_scalar(wrap[:, :], invert_ps[:, 1, :], float(B), -float(B * S), ALU.is_ge, ALU.mult))
            chained(dve.tensor_scalar(pick[:, :], invert_ps[:, 1, :], float(P), None, ALU.mult))
            chained(dve.tensor_tensor(pick[:, :], pick[:, :], invert_ps[:, 0, :], ALU.add))
            chained(dve.tensor_tensor(token_f[:, :], pick[:, :], wrap[:, :], ALU.add))
            dve.tensor_copy(token_row[:, :], token_f[:, :]).then_inc(tokens_known, 1)
            chained(dve.tensor_scalar(spare[:, :], invert_ps[:, 2, :], -1.0, 1.0, ALU.mult, ALU.add))
            chained(dve.tensor_tensor(spare[:, :], spare[:, :], spare_row[:, :], ALU.mult))
            chained(dve.tensor_tensor(spare[:, :], spare[:, :], pick[:, :], ALU.add))
            dve.tensor_copy(pick_row[:, :], spare[:, :]).then_inc(picks_known, 1)

            def gated(tile, slot):
                dve.wait_ge(h_done, tile * 2 + 2)
                dve.wait_ge(silu_ready, tile + 1)
                dve.tensor_tensor(inner[:, slot, :], h_ps[slot][1], silu[:, slot, :], ALU.mult).then_inc(inner_ready, 1)

            gated(0, 0)

            def step(tile, slot, pair, left):
                dve.wait_ge(t_ready, tile + 1)
                dve.tensor_tensor(inner_lo[:, slot, :, :], t_ps, inner_hi[:, slot, :, :], ALU.subtract).then_inc(t_lo_ready, 1)
                if more(left, 1):
                    gated(tile + 1, 1 - slot)
                dve.wait_ge(y_done, tile + 1)
                wait_past(dve, y_stored[slot], pair * 16)
                dve.tensor_copy(y_rows[:, slot, :], y_ps[slot]).then_inc(y_ready, 1)

            tiles(dve, step)
            for b in range(0, B, 2):
                for k in range(TOPK):
                    for i in range(2):
                        if k == 0:
                            dve.wait_ge(gathered[b + i], 16 * TOPK)
                        else:
                            dve.wait_ge(mixed, TOPK * b + i + 1)
                        dve.scalar_tensor_tensor(out=c.x_sb[:, b + i, :], in0=picked[k][:, b + i, :], scalar=share[:, k, b + i:b + i + 1],
                                                 in1=c.x_sb[:, b + i, :], op0=ALU.mult, op1=ALU.add).then_inc(mixed, 1)

        @block.tensor
        def _(pe):
            pe.wait_ge(consts, 3)
            pe.wait_ge(either_ready, 1)
            pe.matmul(rank_ps, before[:, :], either[:, :, :], start=True, stop=False, skip_group_check=True)
            for b in range(B):
                last = pe.matmul(rank_ps[:, b + 1:B + 1, :], ones[:, :], either[:, b:b + 1, :].to_broadcast([P, B - b, NE]),
                                 start=False, stop=b == B - 1, skip_group_check=True)
            last.then_inc(counts_done, 1)
            for n in range(PICKS):
                if n % B == 0:
                    pe.wait_ge(hot_ready, n // B + 1)
                last = pe.matmul(invert_ps, row_hot[:, n, :], in_tile[:, n, :, :], start=n == 0, stop=n == PICKS - 1)
            last.then_inc(inverted, 1)

            def expert_of(tile, part, width):
                return pe.value_load(owner[0:1, part, bass.ds(tile, 1)], min_val=0, max_val=(NE - 1) * width)

            def columns(tile, slot, pair, first):
                pe.wait_ge(x_loaded[slot], pair * 16 + 16)
                if not first:
                    pe.wait_ge(x_ready, tile)
                for k in range(KD):
                    last = pe.transpose(x_ps[:, k, :], x_rows[:, slot, k * P:(k + 1) * P], c.ident[:, :])
                last.then_inc(x_done, 1)

            def expand(tile, slot, i, at):
                if i == 0:
                    pe.wait_ge(x_ready, tile + 1)
                for k in range(KD):
                    last = pe.matmul(h_ps[slot][i], x_cols[:, slot, k, :], c.expert_w[:, bass.ds(at + (i * KD + k) * M, M)],
                                     start=k == 0, stop=k == KD - 1)
                last.then_inc(h_done, 1)

            def transpose_inner(tile, slot):
                pe.wait_ge(inner_ready, tile + 1)
                wait_past(pe, t_lo_ready, tile)
                for m in range(KM):
                    last = pe.transpose(t_ps[:, m, :], inner[:, slot, m * P:(m + 1) * P], c.ident[:, :])
                last.then_inc(t_done, 1)

            def reduce(tile, slot, pair, at):
                pe.wait_ge(t_ready, tile + 1)
                wait_past(pe, y_ready, pair * 2)
                for m in range(KM):
                    for wo in (c.expert_wo_hi, c.expert_wo_lo):
                        pe.matmul(y_ps[slot], inner_hi[:, slot, m, :], wo[:, bass.ds(at + m * D, D)],
                                  start=m == 0 and wo is c.expert_wo_hi, stop=False)
                pe.wait_ge(t_lo_ready, tile + 1)
                for m in range(KM):
                    last = pe.matmul(y_ps[slot], inner_lo[:, slot, m, :], c.expert_wo_hi[:, bass.ds(at + m * D, D)],
                                     start=False, stop=m == KM - 1)
                last.then_inc(y_done, 1)

            pe.wait_ge(owner_known, 1)
            pe.wait_ge(picks_known, 1)
            pe.wait_ge(c.experts_loaded, 16 * NE)
            columns(0, 0, 0, True)
            at = expert_of(0, 0, EW)
            for i in range(2):
                expand(0, 0, i, at)
            columns(1, 1, 0, False)

            def step(tile, slot, pair, left):
                if more(left, 1):
                    at_next = expert_of(tile + 1, 0, EW)
                    expand(tile + 1, 1 - slot, 0, at_next)
                transpose_inner(tile, slot)
                if more(left, 2):
                    columns(tile + 2, slot, pair + 1, False)
                if more(left, 1):
                    expand(tile + 1, 1 - slot, 1, at_next)
                reduce(tile, slot, pair, expert_of(tile, 1, OW))

            tiles(pe, step)
    phase.close()


def decoder_layer(nc, x, betas_t, wqk, wv, wo, ctx_t, xwq_t, xwkv_t, xwout_t, gate_w, expert_w, expert_wo, out):
    xn_dram = nc.dram_tensor("xn_dram", (B * S, D), F32, kind="Internal").ap()
    picks_dram = nc.dram_tensor("picks_dram", ((PICKS + TILES) * P, D), F32, kind="Internal").ap()
    with ExitStack() as ctx:
        c = Core(nc, ctx)
        c.experts_loaded = c.sem("experts_loaded")
        attention_phase(c, x, betas_t, wqk, wv, wo, ctx_t, xwq_t, xwkv_t, xwout_t, gate_w)
        c.expert_w = c.sb("expert_w", [P, NE * EW], F32)
        c.expert_wo_hi = c.sb("expert_wo_hi", [P, NE * OW], F32R)
        c.expert_wo_lo = c.sb("expert_wo_lo", [P, NE * OW], F32R)
        c.expert_wo = expert_wo

        def load_experts(sp):
            for e in range(NE):
                sp.dma_start(c.expert_w[:, e * EW:(e + 1) * EW], expert_w[e]).then_inc(c.experts_loaded, 16)

        c.load_experts = load_experts
        cross_phase(c)
        expert_phase(c, xn_dram, picks_dram, out)


def kernel(x, ctx_512, L0_attn_Wq, L0_attn_Wk, L0_attn_Wv, L0_attn_Wo, L0_attn_betas, L0_xattn_Wq, L0_xattn_Wkv_expand,
           L0_xattn_Wout, L0_ffn_gate_kernel, L0_ffn_w0_kernel, L0_ffn_w1_kernel, L0_ffn_wo_kernel):
    import numpy as np
    import concourse.bacc as bacc
    from concourse.bass_utils import run_bass_kernel_spmd

    def laid(a):
        return np.ascontiguousarray(a)

    def rows(w):
        w = np.asarray(w)
        lead = w.shape[:-2]
        w = w.reshape(*lead, w.shape[-2] // P, P, w.shape[-1])
        return np.moveaxis(w, -3, -2).reshape(*lead, P, -1)

    def by_head(w, n):
        w = np.asarray(w)
        return np.moveaxis(w.reshape(w.shape[0], H // n, n * DK), 1, 0)

    arrays = {
        "x": laid(x),
        "betas_t": laid(np.asarray(L0_attn_betas).reshape(H, DK).T),
        "wqk": laid(np.concatenate([rows(by_head(L0_attn_Wq, 1)), rows(by_head(L0_attn_Wk, 1))], axis=-1)),
        "wv": laid(rows(by_head(L0_attn_Wv, GH)[[*range(NG), 0]])),
        "wo": laid(np.asarray(L0_attn_Wo).reshape(H, DK, D)),
        "ctx_t": laid(np.asarray(ctx_512).transpose(0, 2, 1)),
        "xwq_t": laid(np.asarray(L0_xattn_Wq).T),
        "xwkv_t": laid(np.asarray(L0_xattn_Wkv_expand).T),
        "xwout_t": laid(np.asarray(L0_xattn_Wout).T),
        "gate_w": laid(L0_ffn_gate_kernel),
        "expert_w": laid(np.concatenate([rows(L0_ffn_w0_kernel), rows(L0_ffn_w1_kernel)], axis=-1)),
        "expert_wo": laid(rows(L0_ffn_wo_kernel)),
    }
    nc = bacc.Bacc("TRN2", target_bir_lowering=False, num_devices=1)
    args = [nc.dram_tensor(f"in_{name}", a.shape, mybir.dt.from_np(a.dtype), kind="ExternalInput").ap() for name, a in arrays.items()]
    out = nc.dram_tensor("out_0", (B, S, D), F32, kind="ExternalOutput").ap()
    decoder_layer(nc, *args, out)
    r = run_bass_kernel_spmd(nc, [{f"in_{name}": a for name, a in arrays.items()}], core_ids=[0])
    return r.results[0]["out_0"]
```
